# Optimizing a Trainium2 kernel written in Bass

```python
import numpy as np
import jax
import jax.numpy as jnp

def _softmax(x, axis=-1):
    return jax.nn.softmax(x, axis=axis)

def _gelu(x):
    return jax.nn.gelu(x, approximate=True)

def _silu(x):
    return jax.nn.silu(x)

def _sigmoid(x):
    return jax.nn.sigmoid(x)

def _layernorm(x, axis=-1, eps=1e-05):
    m = jnp.mean(x, axis=axis, keepdims=True)
    v = jnp.var(x, axis=axis, keepdims=True)
    return (x - m) / jnp.sqrt(v + eps)

def _scatter_add(tgt, idx, src, axis=0):
    return tgt.at[idx].add(src)

def _segment_sum(src, seg, n):
    return jax.ops.segment_sum(src, seg, n)
kernel_name = 'mk_xattn_seq_d4_seqx_r4_0dc8f4'

def setup_inputs(seed: int=0):
    np.random.seed(seed)
    _w = jnp.asarray

    def _rec_inputs():
        import jax
        import jax.numpy as jnp
        _rk = jax.random.key(seed)
        x = -0.000917 + 0.9994 * jax.random.normal(jax.random.fold_in(_rk, 1), (2, 1024, 256), jnp.float32)
        _lenS = 1024 - jax.random.randint(jax.random.fold_in(_rk, 7), (2,), 0, max(1, 1024 // 4) + 1, jnp.int32)
        _lenS2 = 64 - jax.random.randint(jax.random.fold_in(_rk, 8), (2,), 0, max(1, 64 // 4) + 1, jnp.int32)
        _ctx_768P = jax.random.normal(jax.random.fold_in(_rk, 11), (2, 16, 192), jnp.float32)
        _ctx_768c = jax.random.dirichlet(jax.random.fold_in(_rk, 511), 0.3 * jnp.ones((16,), jnp.float32), (2, 64))
        _ctx_768t = jnp.einsum('bsk,bkd->bsd', _ctx_768c, _ctx_768P)
        _ctx_768t = _ctx_768t * jax.lax.rsqrt(jnp.mean(jnp.square(_ctx_768t)) + 1e-12) * 0.953939
        ctx_768 = 0.000947723 + 1.00027 * (_ctx_768t + 0.3 * jax.random.normal(jax.random.fold_in(_rk, 611), (2, 64, 192), jnp.float32))
        _validS = jnp.arange(1024)[None, :] < _lenS[:, None]
        _validS2 = jnp.arange(64)[None, :] < _lenS2[:, None]
        _causal = jnp.tril(jnp.ones((1024, 1024), dtype=bool))
        mask_BxS_bf0 = jnp.logical_not(jnp.ones((2, 1024), dtype=bool))
        mask_BxS2_bf0 = jnp.logical_not(jnp.ones((2, 64), dtype=bool))
        mask_BxS2_if1 = jnp.where(jnp.ones((2, 64), dtype=bool), 1, 0).astype(jnp.int32)
        return (x, ctx_768, mask_BxS_bf0, mask_BxS2_bf0, mask_BxS2_if1)
    x, ctx_768, mask_BxS_bf0, mask_BxS2_bf0, mask_BxS2_if1 = _rec_inputs()

    def _L0_xattn_setup():
        import jax, jax.numpy as jnp
        import numpy as np
        D_DEC, D_ENC, H, D_MLP = (256, 192, 16, 1024)
        HD = D_DEC // H

        def _layernorm(x, w, b, eps=1e-05):
            m = x.mean(-1, keepdims=True)
            v = ((x - m) ** 2).mean(-1, keepdims=True)
            return (x - m) / jnp.sqrt(v + eps) * w + b

        def _decoder_block(x, enc, tgt_mask, enc_mask, ln1_w, ln1_b, qkv_w, qkv_b, proj_w, proj_b, ln2_w, ln2_b, q_w, q_b, k_w, k_b, v_w, v_b, out_w, out_b, ln3_w, ln3_b, mlp1_w, mlp1_b, mlp2_w, mlp2_b):
            B, T, C = x.shape
            S = enc.shape[1]
            scale = HD ** (-0.5)
            neg = jnp.asarray(-jnp.inf, x.dtype)
            h = _layernorm(x, ln1_w, ln1_b)
            qkv = (h @ qkv_w + qkv_b).reshape(B, T, 3, H, HD)
            q, k, v = [qkv[:, :, i].transpose(0, 2, 1, 3) for i in range(3)]
            attn = jnp.einsum('bhtd,bhsd->bhts', q, k) * scale
            causal = jnp.triu(jnp.ones((T, T), bool), 1)
            attn = jnp.where(causal[None, None], neg, attn)
            attn = jnp.where(tgt_mask[:, None, None, :], neg, attn)
            attn = jax.nn.softmax(attn, axis=-1)
            sa = jnp.einsum('bhts,bhsd->bhtd', attn, v).transpose(0, 2, 1, 3).reshape(B, T, C)
            x = x + sa @ proj_w + proj_b
            h = _layernorm(x, ln2_w, ln2_b)
            q = (h @ q_w + q_b).reshape(B, T, H, HD).transpose(0, 2, 1, 3)
            k = (enc @ k_w + k_b).reshape(B, S, H, HD).transpose(0, 2, 1, 3)
            v = (enc @ v_w + v_b).reshape(B, S, H, HD).transpose(0, 2, 1, 3)
            attn = jnp.einsum('bhtd,bhsd->bhts', q, k) * scale
            attn = jnp.where(enc_mask[:, None, None, :], neg, attn)
            attn = jax.nn.softmax(attn, axis=-1)
            ca = jnp.einsum('bhts,bhsd->bhtd', attn, v).transpose(0, 2, 1, 3).reshape(B, T, C)
            x = x + ca @ out_w + out_b
            h = _layernorm(x, ln3_w, ln3_b)
            h = jax.nn.gelu(h @ mlp1_w + mlp1_b, approximate=False)
            x = x + h @ mlp2_w + mlp2_b
            return x
        key = jax.random.key(seed)
        ks = jax.random.split(key, 16)
        B, T, S = (4, 256, 144)

        def lin(k, din, dout):
            kw, kb = jax.random.split(k)
            bound = 1.0 / np.sqrt(din)
            W = jax.random.uniform(kw, (din, dout), jnp.float32, -bound, bound)
            b = jax.random.uniform(kb, (dout,), jnp.float32, -bound, bound)
            return (W, b)
        qkv_w, qkv_b = lin(ks[0], D_DEC, 3 * D_DEC)
        proj_w, proj_b = lin(ks[1], D_DEC, D_DEC)
        q_w, q_b = lin(ks[2], D_DEC, D_DEC)
        k_w, k_b = lin(ks[3], D_ENC, D_DEC)
        v_w, v_b = lin(ks[4], D_ENC, D_DEC)
        out_w, out_b = lin(ks[5], D_DEC, D_DEC)
        mlp1_w, mlp1_b = lin(ks[6], D_DEC, D_MLP)
        mlp2_w, mlp2_b = lin(ks[7], D_MLP, D_DEC)
        return {'x': jax.random.normal(ks[8], (B, T, D_DEC), jnp.float32), 'enc': jax.random.normal(ks[9], (B, S, D_ENC), jnp.float32), 'tgt_key_padding_mask': jnp.zeros((B, T), bool), 'enc_padding_mask': jnp.zeros((B, S), bool), 'ln1_w': jnp.ones((D_DEC,)), 'ln1_b': jnp.zeros((D_DEC,)), 'qkv_w': qkv_w, 'qkv_b': qkv_b, 'proj_w': proj_w, 'proj_b': proj_b, 'ln2_w': jnp.ones((D_DEC,)), 'ln2_b': jnp.zeros((D_DEC,)), 'q_w': q_w, 'q_b': q_b, 'k_w': k_w, 'k_b': k_b, 'v_w': v_w, 'v_b': v_b, 'out_w': out_w, 'out_b': out_b, 'ln3_w': jnp.ones((D_DEC,)), 'ln3_b': jnp.zeros((D_DEC,)), 'mlp1_w': mlp1_w, 'mlp1_b': mlp1_b, 'mlp2_w': mlp2_w, 'mlp2_b': mlp2_b}
    _L0_xattn_all = _L0_xattn_setup()
    _L0_xattn_in = {k: v for k, v in _L0_xattn_all.items() if k in ('ln1_w', 'ln1_b', 'qkv_w', 'qkv_b', 'proj_w', 'proj_b', 'ln2_w', 'ln2_b', 'q_w', 'q_b', 'k_w', 'k_b', 'v_w', 'v_b', 'out_w', 'out_b', 'ln3_w', 'ln3_b', 'mlp1_w', 'mlp1_b', 'mlp2_w', 'mlp2_b')}
    del _L0_xattn_all

    def _L1_xattn_setup():
        import jax, jax.numpy as jnp
        import numpy as np
        LN_EPS = 1e-05

        def _ln(x, g, b):
            m = jnp.mean(x, axis=-1, keepdims=True)
            v = jnp.mean((x - m) ** 2, axis=-1, keepdims=True)
            return (x - m) / jnp.sqrt(v + LN_EPS) * g + b
        key = jax.random.key(seed)
        ks = jax.random.split(key, 8)
        B, N, S, D, T = (16, 64, 512, 256, 192)

        def xavier(k, shape):
            fan_in, fan_out = shape
            lim = (6.0 / (fan_in + fan_out)) ** 0.5
            return jax.random.uniform(k, shape, minval=-lim, maxval=lim, dtype=jnp.float32)
        return {'prev_states': jax.random.normal(ks[0], (B, N, D), dtype=jnp.float32), 'input_tokens': jax.random.normal(ks[1], (B, S, T), dtype=jnp.float32), 'W_proj': xavier(ks[2], (T, D)), 'b_proj': jnp.zeros((D,), jnp.float32), 'g_state': jnp.ones((D,), jnp.float32), 'beta_state': jnp.zeros((D,), jnp.float32), 'g_input': jnp.ones((D,), jnp.float32), 'beta_input': jnp.zeros((D,), jnp.float32), 'g_out': jnp.ones((D,), jnp.float32), 'beta_out': jnp.zeros((D,), jnp.float32), 'W_u': xavier(ks[3], (2 * D, D)), 'b_u': jnp.full((D,), -1.0, jnp.float32), 'W_r': xavier(ks[4], (2 * D, D)), 'b_r': jnp.zeros((D,), jnp.float32), 'W_n': xavier(ks[5], (2 * D, D)), 'b_n': jnp.zeros((D,), jnp.float32)}
    _L1_xattn_all = _L1_xattn_setup()
    _L1_xattn_in = {k: v for k, v in _L1_xattn_all.items() if k in ('W_proj', 'b_proj', 'g_state', 'beta_state', 'g_input', 'beta_input', 'g_out', 'beta_out', 'W_u', 'b_u', 'W_r', 'b_r', 'W_n', 'b_n')}
    del _L1_xattn_all

    def _L2_xattn_setup():
        import jax, jax.numpy as jnp
        import numpy as np
        D_MODEL = 256
        D_COND = 192
        N_HEADS = 16
        D_HEAD = 64
        D_ATTN = N_HEADS * D_HEAD
        D_FF = 4 * D_MODEL

        def _layernorm(x, g, b, eps=1e-05):
            mu = jnp.mean(x, axis=-1, keepdims=True)
            var = jnp.var(x, axis=-1, keepdims=True)
            return (x - mu) * jax.lax.rsqrt(var + eps) * g + b

        def _attention(xq, xkv, wq, wk, wv, wo, bo):
            B, S, _ = xq.shape
            T = xkv.shape[1]
            q = (xq @ wq).reshape(B, S, N_HEADS, D_HEAD)
            k = (xkv @ wk).reshape(B, T, N_HEADS, D_HEAD)
            v = (xkv @ wv).reshape(B, T, N_HEADS, D_HEAD)
            scale = D_HEAD ** (-0.5)
            attn = jnp.einsum('bihd,bjhd->bhij', q, k) * scale
            attn = jax.nn.softmax(attn, axis=-1)
            out = jnp.einsum('bhij,bjhd->bihd', attn, v).reshape(B, S, D_ATTN)
            return out @ wo + bo
        key = jax.random.key(seed)
        ks = jax.random.split(key, 16)
        B, S, T = (8, 256, 64)
        n = jax.random.normal
        inp = {'x': n(ks[0], (B, S, D_MODEL), jnp.float32), 'cond_emb': n(ks[1], (B, T, D_COND), jnp.float32), 'ln1_g': jnp.ones((D_MODEL,), jnp.float32), 'ln1_b': jnp.zeros((D_MODEL,), jnp.float32), 'ln2_g': jnp.ones((D_MODEL,), jnp.float32), 'ln2_b': jnp.zeros((D_MODEL,), jnp.float32), 'ln3_g': jnp.ones((D_MODEL,), jnp.float32), 'ln3_b': jnp.zeros((D_MODEL,), jnp.float32), 'sa_wq': n(ks[2], (D_MODEL, D_ATTN), jnp.float32) * D_MODEL ** (-0.5), 'sa_wk': n(ks[3], (D_MODEL, D_ATTN), jnp.float32) * D_MODEL ** (-0.5), 'sa_wv': n(ks[4], (D_MODEL, D_ATTN), jnp.float32) * D_MODEL ** (-0.5), 'sa_wo': n(ks[5], (D_ATTN, D_MODEL), jnp.float32) * D_ATTN ** (-0.5), 'sa_bo': jnp.zeros((D_MODEL,), jnp.float32), 'ca_wq': n(ks[6], (D_MODEL, D_ATTN), jnp.float32) * D_MODEL ** (-0.5), 'ca_wk': n(ks[7], (D_COND, D_ATTN), jnp.float32) * D_COND ** (-0.5), 'ca_wv': n(ks[8], (D_COND, D_ATTN), jnp.float32) * D_COND ** (-0.5), 'ca_wo': n(ks[9], (D_ATTN, D_MODEL), jnp.float32) * D_ATTN ** (-0.5), 'ca_bo': jnp.zeros((D_MODEL,), jnp.float32), 'ff_w1': n(ks[10], (D_MODEL, 2 * D_FF), jnp.float32) * D_MODEL ** (-0.5), 'ff_b1': jnp.zeros((2 * D_FF,), jnp.float32), 'ff_w2': n(ks[11], (D_FF, D_MODEL), jnp.float32) * D_FF ** (-0.5), 'ff_b2': jnp.zeros((D_MODEL,), jnp.float32)}
        return inp
    _L2_xattn_all = _L2_xattn_setup()
    _L2_xattn_in = {k: v for k, v in _L2_xattn_all.items() if k in ('ln1_g', 'ln1_b', 'ln2_g', 'ln2_b', 'ln3_g', 'ln3_b', 'sa_wq', 'sa_wk', 'sa_wv', 'sa_wo', 'sa_bo', 'ca_wq', 'ca_wk', 'ca_wv', 'ca_wo', 'ca_bo', 'ff_w1', 'ff_b1', 'ff_w2', 'ff_b2')}
    del _L2_xattn_all

    def _L3_xattn_setup():
        import jax, jax.numpy as jnp
        import numpy as np
        import math
        H = 8
        D = 256
        D_I = 256
        D_L = 192
        EPS = 1e-05
        key = jax.random.key(seed)
        ks = jax.random.split(key, 8)
        B, NQ, NK = (8, 196, 128)
        img_embed = jax.random.normal(ks[0], (B, NQ, D_I), dtype=jnp.float32)
        sent_embed = jax.random.normal(ks[1], (B, NK, D_L), dtype=jnp.float32)
        atten_mask = jnp.ones((B, NK), dtype=jnp.int32)
        Wq = jax.random.normal(ks[2], (D_I, H * D), dtype=jnp.float32) * (1.0 / math.sqrt(D_I))
        Wk = jax.random.normal(ks[3], (D_L, H * D), dtype=jnp.float32) * (1.0 / math.sqrt(D_L))
        Wv = jax.random.normal(ks[4], (D_L, H * D), dtype=jnp.float32) * (1.0 / math.sqrt(D_L))
        Wo = jax.random.normal(ks[5], (H * D, D_I), dtype=jnp.float32) * (1.0 / math.sqrt(H * D))
        gamma = jnp.ones((D_I,), dtype=jnp.float32)
        beta = jnp.zeros((D_I,), dtype=jnp.float32)
        return {'img_embed': img_embed, 'sent_embed': sent_embed, 'atten_mask': atten_mask, 'Wq': Wq, 'Wk': Wk, 'Wv': Wv, 'Wo': Wo, 'gamma': gamma, 'beta': beta}
    _L3_xattn_all = _L3_xattn_setup()
    _L3_xattn_in = {k: v for k, v in _L3_xattn_all.items() if k in ('Wq', 'Wk', 'Wv', 'Wo', 'gamma', 'beta')}
    del _L3_xattn_all
    return {'x': x, 'ctx_768': ctx_768, 'mask_BxS_bf0': mask_BxS_bf0, 'mask_BxS2_bf0': mask_BxS2_bf0, 'mask_BxS2_if1': mask_BxS2_if1, 'L0_xattn_ln1_w': _L0_xattn_in['ln1_w'], 'L0_xattn_ln1_b': _L0_xattn_in['ln1_b'], 'L0_xattn_qkv_w': _L0_xattn_in['qkv_w'], 'L0_xattn_qkv_b': _L0_xattn_in['qkv_b'], 'L0_xattn_proj_w': _L0_xattn_in['proj_w'], 'L0_xattn_proj_b': _L0_xattn_in['proj_b'], 'L0_xattn_ln2_w': _L0_xattn_in['ln2_w'], 'L0_xattn_ln2_b': _L0_xattn_in['ln2_b'], 'L0_xattn_q_w': _L0_xattn_in['q_w'], 'L0_xattn_q_b': _L0_xattn_in['q_b'], 'L0_xattn_k_w': _L0_xattn_in['k_w'], 'L0_xattn_k_b': _L0_xattn_in['k_b'], 'L0_xattn_v_w': _L0_xattn_in['v_w'], 'L0_xattn_v_b': _L0_xattn_in['v_b'], 'L0_xattn_out_w': _L0_xattn_in['out_w'], 'L0_xattn_out_b': _L0_xattn_in['out_b'], 'L0_xattn_ln3_w': _L0_xattn_in['ln3_w'], 'L0_xattn_ln3_b': _L0_xattn_in['ln3_b'], 'L0_xattn_mlp1_w': _L0_xattn_in['mlp1_w'], 'L0_xattn_mlp1_b': _L0_xattn_in['mlp1_b'], 'L0_xattn_mlp2_w': _L0_xattn_in['mlp2_w'], 'L0_xattn_mlp2_b': _L0_xattn_in['mlp2_b'], 'L1_xattn_W_proj': _L1_xattn_in['W_proj'], 'L1_xattn_b_proj': _L1_xattn_in['b_proj'], 'L1_xattn_g_state': _L1_xattn_in['g_state'], 'L1_xattn_beta_state': _L1_xattn_in['beta_state'], 'L1_xattn_g_input': _L1_xattn_in['g_input'], 'L1_xattn_beta_input': _L1_xattn_in['beta_input'], 'L1_xattn_g_out': _L1_xattn_in['g_out'], 'L1_xattn_beta_out': _L1_xattn_in['beta_out'], 'L1_xattn_W_u': _L1_xattn_in['W_u'], 'L1_xattn_b_u': _L1_xattn_in['b_u'], 'L1_xattn_W_r': _L1_xattn_in['W_r'], 'L1_xattn_b_r': _L1_xattn_in['b_r'], 'L1_xattn_W_n': _L1_xattn_in['W_n'], 'L1_xattn_b_n': _L1_xattn_in['b_n'], 'L2_xattn_ln1_g': _L2_xattn_in['ln1_g'], 'L2_xattn_ln1_b': _L2_xattn_in['ln1_b'], 'L2_xattn_ln2_g': _L2_xattn_in['ln2_g'], 'L2_xattn_ln2_b': _L2_xattn_in['ln2_b'], 'L2_xattn_ln3_g': _L2_xattn_in['ln3_g'], 'L2_xattn_ln3_b': _L2_xattn_in['ln3_b'], 'L2_xattn_sa_wq': _L2_xattn_in['sa_wq'], 'L2_xattn_sa_wk': _L2_xattn_in['sa_wk'], 'L2_xattn_sa_wv': _L2_xattn_in['sa_wv'], 'L2_xattn_sa_wo': _L2_xattn_in['sa_wo'], 'L2_xattn_sa_bo': _L2_xattn_in['sa_bo'], 'L2_xattn_ca_wq': _L2_xattn_in['ca_wq'], 'L2_xattn_ca_wk': _L2_xattn_in['ca_wk'], 'L2_xattn_ca_wv': _L2_xattn_in['ca_wv'], 'L2_xattn_ca_wo': _L2_xattn_in['ca_wo'], 'L2_xattn_ca_bo': _L2_xattn_in['ca_bo'], 'L2_xattn_ff_w1': _L2_xattn_in['ff_w1'], 'L2_xattn_ff_b1': _L2_xattn_in['ff_b1'], 'L2_xattn_ff_w2': _L2_xattn_in['ff_w2'], 'L2_xattn_ff_b2': _L2_xattn_in['ff_b2'], 'L3_xattn_Wq': _L3_xattn_in['Wq'], 'L3_xattn_Wk': _L3_xattn_in['Wk'], 'L3_xattn_Wv': _L3_xattn_in['Wv'], 'L3_xattn_Wo': _L3_xattn_in['Wo'], 'L3_xattn_gamma': _L3_xattn_in['gamma'], 'L3_xattn_beta': _L3_xattn_in['beta']}

def reference(x, ctx_768, mask_BxS_bf0, mask_BxS2_bf0, mask_BxS2_if1, L0_xattn_ln1_w, L0_xattn_ln1_b, L0_xattn_qkv_w, L0_xattn_qkv_b, L0_xattn_proj_w, L0_xattn_proj_b, L0_xattn_ln2_w, L0_xattn_ln2_b, L0_xattn_q_w, L0_xattn_q_b, L0_xattn_k_w, L0_xattn_k_b, L0_xattn_v_w, L0_xattn_v_b, L0_xattn_out_w, L0_xattn_out_b, L0_xattn_ln3_w, L0_xattn_ln3_b, L0_xattn_mlp1_w, L0_xattn_mlp1_b, L0_xattn_mlp2_w, L0_xattn_mlp2_b, L1_xattn_W_proj, L1_xattn_b_proj, L1_xattn_g_state, L1_xattn_beta_state, L1_xattn_g_input, L1_xattn_beta_input, L1_xattn_g_out, L1_xattn_beta_out, L1_xattn_W_u, L1_xattn_b_u, L1_xattn_W_r, L1_xattn_b_r, L1_xattn_W_n, L1_xattn_b_n, L2_xattn_ln1_g, L2_xattn_ln1_b, L2_xattn_ln2_g, L2_xattn_ln2_b, L2_xattn_ln3_g, L2_xattn_ln3_b, L2_xattn_sa_wq, L2_xattn_sa_wk, L2_xattn_sa_wv, L2_xattn_sa_wo, L2_xattn_sa_bo, L2_xattn_ca_wq, L2_xattn_ca_wk, L2_xattn_ca_wv, L2_xattn_ca_wo, L2_xattn_ca_bo, L2_xattn_ff_w1, L2_xattn_ff_b1, L2_xattn_ff_w2, L2_xattn_ff_b2, L3_xattn_Wq, L3_xattn_Wk, L3_xattn_Wv, L3_xattn_Wo, L3_xattn_gamma, L3_xattn_beta):
    import jax
    import jax.numpy as jnp

    def _L0_xattn_ref(x, enc, tgt_key_padding_mask, enc_padding_mask, ln1_w, ln1_b, qkv_w, qkv_b, proj_w, proj_b, ln2_w, ln2_b, q_w, q_b, k_w, k_b, v_w, v_b, out_w, out_b, ln3_w, ln3_b, mlp1_w, mlp1_b, mlp2_w, mlp2_b):
        import jax, jax.numpy as jnp
        import numpy as np
        D_DEC, D_ENC, H, D_MLP = (256, 192, 16, 1024)
        HD = D_DEC // H

        def _layernorm(x, w, b, eps=1e-05):
            m = x.mean(-1, keepdims=True)
            v = ((x - m) ** 2).mean(-1, keepdims=True)
            return (x - m) / jnp.sqrt(v + eps) * w + b

        def _decoder_block(x, enc, tgt_mask, enc_mask, ln1_w, ln1_b, qkv_w, qkv_b, proj_w, proj_b, ln2_w, ln2_b, q_w, q_b, k_w, k_b, v_w, v_b, out_w, out_b, ln3_w, ln3_b, mlp1_w, mlp1_b, mlp2_w, mlp2_b):
            B, T, C = x.shape
            S = enc.shape[1]
            scale = HD ** (-0.5)
            neg = jnp.asarray(-jnp.inf, x.dtype)
            h = _layernorm(x, ln1_w, ln1_b)
            qkv = (h @ qkv_w + qkv_b).reshape(B, T, 3, H, HD)
            q, k, v = [qkv[:, :, i].transpose(0, 2, 1, 3) for i in range(3)]
            attn = jnp.einsum('bhtd,bhsd->bhts', q, k) * scale
            causal = jnp.triu(jnp.ones((T, T), bool), 1)
            attn = jnp.where(causal[None, None], neg, attn)
            attn = jnp.where(tgt_mask[:, None, None, :], neg, attn)
            attn = jax.nn.softmax(attn, axis=-1)
            sa = jnp.einsum('bhts,bhsd->bhtd', attn, v).transpose(0, 2, 1, 3).reshape(B, T, C)
            x = x + sa @ proj_w + proj_b
            h = _layernorm(x, ln2_w, ln2_b)
            q = (h @ q_w + q_b).reshape(B, T, H, HD).transpose(0, 2, 1, 3)
            k = (enc @ k_w + k_b).reshape(B, S, H, HD).transpose(0, 2, 1, 3)
            v = (enc @ v_w + v_b).reshape(B, S, H, HD).transpose(0, 2, 1, 3)
            attn = jnp.einsum('bhtd,bhsd->bhts', q, k) * scale
            attn = jnp.where(enc_mask[:, None, None, :], neg, attn)
            attn = jax.nn.softmax(attn, axis=-1)
            ca = jnp.einsum('bhts,bhsd->bhtd', attn, v).transpose(0, 2, 1, 3).reshape(B, T, C)
            x = x + ca @ out_w + out_b
            h = _layernorm(x, ln3_w, ln3_b)
            h = jax.nn.gelu(h @ mlp1_w + mlp1_b, approximate=False)
            x = x + h @ mlp2_w + mlp2_b
            return x
        return _decoder_block(x, enc, tgt_key_padding_mask, enc_padding_mask, ln1_w, ln1_b, qkv_w, qkv_b, proj_w, proj_b, ln2_w, ln2_b, q_w, q_b, k_w, k_b, v_w, v_b, out_w, out_b, ln3_w, ln3_b, mlp1_w, mlp1_b, mlp2_w, mlp2_b)

    def _L1_xattn_ref(prev_states, input_tokens, W_proj, b_proj, g_state, beta_state, g_input, beta_input, g_out, beta_out, W_u, b_u, W_r, b_r, W_n, b_n):
        import jax, jax.numpy as jnp
        import numpy as np
        LN_EPS = 1e-05

        def _ln(x, g, b):
            m = jnp.mean(x, axis=-1, keepdims=True)
            v = jnp.mean((x - m) ** 2, axis=-1, keepdims=True)
            return (x - m) / jnp.sqrt(v + LN_EPS) * g + b
        D = prev_states.shape[-1]
        tok = input_tokens @ W_proj + b_proj
        scores = jnp.einsum('bnd,bsd->bns', prev_states, tok) / jnp.sqrt(jnp.float32(D))
        attn = jax.nn.softmax(scores, axis=-1)
        routed = jnp.einsum('bns,bsd->bnd', attn, tok)
        ps_n = _ln(prev_states, g_state, beta_state)
        in_n = _ln(routed, g_input, beta_input)
        concat = jnp.concatenate([ps_n, in_n], axis=-1)
        u = jax.nn.sigmoid(concat @ W_u + b_u)
        r = jax.nn.sigmoid(concat @ W_r + b_r)
        reset_in = jnp.concatenate([r * ps_n, in_n], axis=-1)
        cand = jnp.tanh(reset_in @ W_n + b_n)
        new_state = (1.0 - u) * prev_states + u * cand
        return _ln(new_state, g_out, beta_out)

    def _L2_xattn_ref(x, cond_emb, ln1_g, ln1_b, ln2_g, ln2_b, ln3_g, ln3_b, sa_wq, sa_wk, sa_wv, sa_wo, sa_bo, ca_wq, ca_wk, ca_wv, ca_wo, ca_bo, ff_w1, ff_b1, ff_w2, ff_b2):
        import jax, jax.numpy as jnp
        import numpy as np
        D_MODEL = 256
        D_COND = 192
        N_HEADS = 16
        D_HEAD = 64
        D_ATTN = N_HEADS * D_HEAD
        D_FF = 4 * D_MODEL

        def _layernorm(x, g, b, eps=1e-05):
            mu = jnp.mean(x, axis=-1, keepdims=True)
            var = jnp.var(x, axis=-1, keepdims=True)
            return (x - mu) * jax.lax.rsqrt(var + eps) * g + b

        def _attention(xq, xkv, wq, wk, wv, wo, bo):
            B, S, _ = xq.shape
            T = xkv.shape[1]
            q = (xq @ wq).reshape(B, S, N_HEADS, D_HEAD)
            k = (xkv @ wk).reshape(B, T, N_HEADS, D_HEAD)
            v = (xkv @ wv).reshape(B, T, N_HEADS, D_HEAD)
            scale = D_HEAD ** (-0.5)
            attn = jnp.einsum('bihd,bjhd->bhij', q, k) * scale
            attn = jax.nn.softmax(attn, axis=-1)
            out = jnp.einsum('bhij,bjhd->bihd', attn, v).reshape(B, S, D_ATTN)
            return out @ wo + bo
        h = _layernorm(x, ln1_g, ln1_b)
        x = _attention(h, h, sa_wq, sa_wk, sa_wv, sa_wo, sa_bo) + x
        h = _layernorm(x, ln2_g, ln2_b)
        x = _attention(h, cond_emb, ca_wq, ca_wk, ca_wv, ca_wo, ca_bo) + x
        h = _layernorm(x, ln3_g, ln3_b)
        p = h @ ff_w1 + ff_b1
        a, gate = (p[..., :D_FF], p[..., D_FF:])
        h = a * jax.nn.gelu(gate, approximate=False) @ ff_w2 + ff_b2
        return h + x

    def _L3_xattn_ref(img_embed, sent_embed, atten_mask, Wq, Wk, Wv, Wo, gamma, beta):
        import jax, jax.numpy as jnp
        import numpy as np
        import math
        H = 8
        D = 256
        D_I = 256
        D_L = 192
        EPS = 1e-05
        B = img_embed.shape[0]
        Q = (img_embed @ Wq).reshape(B, -1, H, D).transpose(0, 2, 1, 3)
        K = (sent_embed @ Wk).reshape(B, -1, H, D).transpose(0, 2, 1, 3)
        V = (sent_embed @ Wv).reshape(B, -1, H, D).transpose(0, 2, 1, 3)
        score = jnp.einsum('bhqd,bhkd->bhqk', Q, K) / math.sqrt(D)
        mask = (atten_mask != 0)[:, None, None, :]
        score = jnp.where(mask, score, -jnp.inf)
        attn = jax.nn.softmax(score, axis=-1)
        ctx = jnp.einsum('bhqk,bhkd->bqhd', attn, V).reshape(B, -1, H * D)
        out = ctx @ Wo + img_embed
        mu = jnp.mean(out, axis=-1, keepdims=True)
        var = jnp.var(out, axis=-1, keepdims=True)
        return (out - mu) * jax.lax.rsqrt(var + EPS) * gamma + beta
    x = _L0_xattn_ref(x, ctx_768, mask_BxS_bf0, mask_BxS2_bf0, L0_xattn_ln1_w, L0_xattn_ln1_b, L0_xattn_qkv_w, L0_xattn_qkv_b, L0_xattn_proj_w, L0_xattn_proj_b, L0_xattn_ln2_w, L0_xattn_ln2_b, L0_xattn_q_w, L0_xattn_q_b, L0_xattn_k_w, L0_xattn_k_b, L0_xattn_v_w, L0_xattn_v_b, L0_xattn_out_w, L0_xattn_out_b, L0_xattn_ln3_w, L0_xattn_ln3_b, L0_xattn_mlp1_w, L0_xattn_mlp1_b, L0_xattn_mlp2_w, L0_xattn_mlp2_b)
    x = _L1_xattn_ref(x, ctx_768, L1_xattn_W_proj, L1_xattn_b_proj, L1_xattn_g_state, L1_xattn_beta_state, L1_xattn_g_input, L1_xattn_beta_input, L1_xattn_g_out, L1_xattn_beta_out, L1_xattn_W_u, L1_xattn_b_u, L1_xattn_W_r, L1_xattn_b_r, L1_xattn_W_n, L1_xattn_b_n)
    x = _L2_xattn_ref(x, ctx_768, L2_xattn_ln1_g, L2_xattn_ln1_b, L2_xattn_ln2_g, L2_xattn_ln2_b, L2_xattn_ln3_g, L2_xattn_ln3_b, L2_xattn_sa_wq, L2_xattn_sa_wk, L2_xattn_sa_wv, L2_xattn_sa_wo, L2_xattn_sa_bo, L2_xattn_ca_wq, L2_xattn_ca_wk, L2_xattn_ca_wv, L2_xattn_ca_wo, L2_xattn_ca_bo, L2_xattn_ff_w1, L2_xattn_ff_b1, L2_xattn_ff_w2, L2_xattn_ff_b2)
    x = _L3_xattn_ref(x, ctx_768, mask_BxS2_if1, L3_xattn_Wq, L3_xattn_Wk, L3_xattn_Wv, L3_xattn_Wo, L3_xattn_gamma, L3_xattn_beta)
    return x

_drawn_inputs = setup_inputs


def setup_inputs(seed=0):
    import zlib

    import numpy as np

    out = dict(_drawn_inputs(seed))
    spreads = {'L0_xattn_ln1_w': (1.0, 0.6),
     'L0_xattn_ln1_b': (0.0, 0.1),
     'L0_xattn_ln2_w': (1.0, 0.6),
     'L0_xattn_ln2_b': (0.0, 0.8),
     'L0_xattn_ln3_w': (1.0, 0.2),
     'L0_xattn_ln3_b': (0.0, 0.326),
     'L1_xattn_b_proj': (0.0, 0.1),
     'L1_xattn_g_state': (1.0, 0.2),
     'L1_xattn_beta_state': (0.0, 0.272),
     'L1_xattn_g_input': (1.0, 0.2),
     'L1_xattn_beta_input': (0.0, 0.1),
     'L1_xattn_g_out': (1.0, 0.2),
     'L1_xattn_beta_out': (0.0, 0.1),
     'L1_xattn_b_u': (-1.0, 0.2),
     'L1_xattn_b_r': (0.0, 0.8),
     'L1_xattn_b_n': (0.0, 0.1),
     'L2_xattn_ln1_g': (1.0, 0.2),
     'L2_xattn_ln1_b': (0.0, 0.1),
     'L2_xattn_ln2_g': (1.0, 0.2),
     'L2_xattn_ln2_b': (0.0, 0.384),
     'L2_xattn_ln3_g': (1.0, 0.2),
     'L2_xattn_ln3_b': (0.0, 0.1),
     'L2_xattn_sa_bo': (0.0, 0.1),
     'L2_xattn_ca_bo': (0.0, 0.1),
     'L2_xattn_ff_b1': (0.0, 0.1),
     'L2_xattn_ff_b2': (0.0, 0.1),
     'L3_xattn_gamma': (1.0, 0.2),
     'L3_xattn_beta': (0.0, 0.1)}
    factors = {'L0_xattn_q_w': 2.713,
     'L0_xattn_q_b': 8.0,
     'L0_xattn_k_w': 2.675,
     'L0_xattn_k_b': 8.0,
     'L0_xattn_mlp1_b': 4.232}
    for name, (base, spread) in spreads.items():
        noise = np.random.default_rng([zlib.crc32(name.encode()), seed]).standard_normal(out[name].shape)
        drawn = base * np.exp(spread * noise) if base else spread * noise
        out[name] = jnp.asarray(drawn.astype(out[name].dtype))
    for name, factor in factors.items():
        out[name] = (out[name] * factor).astype(out[name].dtype)
    return out
```

```python
import numpy as np
import concourse.bass as bass
from concourse import mybir
from contextlib import ExitStack

ALU = mybir.AluOpType
ACT = mybir.ActivationFunctionType
AX = mybir.AxisListType
F32 = mybir.dt.float32
F32R = mybir.dt.float32r
BF16 = mybir.dt.bfloat16
ds = bass.ds

P = 128
B, T, C = 2, 1024, 256
S2, CC = 64, 192
KC = C // P
TILES = B * T // P
TB = T // P
EPS = 1e-5
MASKED = -1e30


class Steps:

    def __init__(self, sem, names):
        self.sem, self.names, self.next = sem, names, 0
        assert len(set(names)) == len(names)

    def value(self, name, turn=0):
        return turn * len(self.names) + (self.names.index(name) + 1)

    def one(self, name):
        assert self.names[self.next % len(self.names)] == name, (name, self.names[self.next % len(self.names)])
        self.next += 1
        return 1


def part_load(nc, loads):
    with nc.semaphore("loaded") as loaded, nc.Block() as block:
        @block.sync
        def _(sp):
            for dst, src in loads:
                sp.dma_start(dst, src).then_inc(loaded, 16)
            sp.wait_ge(loaded, 16 * len(loads))


class Env:
    pass


def column(ap, n):
    return ap.rearrange("(c p) -> p c", p=P)


def part_prologue(nc, e, A):
    with ExitStack() as ctx:
        sb = lambda n, s, d=F32: ctx.enter_context(nc.sbuf_tensor(n, s, d))
        sem = lambda n: ctx.enter_context(nc.semaphore(n))
        ln1_g, ln1_b = sb("ln1_g", [P, KC]), sb("ln1_b", [P, KC])
        mask_row = sb("mask_row", [B, T], mybir.dt.uint8)
        mask_f = sb("mask_f", [B, T])
        stats = sb("stats", [P, TILES, 6])
        moments = sb("moments", [P, TILES, 2])
        rstd = sb("rstd", [P, TILES])
        h = sb("h", [P, TILES, C])
        ps = [ctx.enter_context(nc.psum_tensor(f"pre{i}", [P, 512], F32)) for i in range(8)]
        x_in, w_in, p_in, m_out = (sem(n) for n in ("x_in", "w_in", "p_in", "m_out"))
        order = [f"hT{i}" for i in range(8)]
        pe = Steps(sem("pre_pe"), order)
        ev = Steps(sem("pre_evac"), order)
        dv = Steps(sem("pre_dve"), ["maskf", "consts", "stats", "moments"] + [f"h{i}" for i in range(8)])
        ln = Steps(sem("pre_ln"), ["logvar", "rstd"])
        gp = Steps(sem("pre_pool"), ["zeros", "ident", "fills", "selects"])
        N_LOADS = 7
        block = ctx.enter_context(nc.Block())

        @block.sync
        def _(sp):
            sp.dma_start(e.x[:], A["x"].rearrange("b (t p) c -> p (b t) c", p=P)).then_inc(x_in, 16)
            rows = lambda n: A[n].rearrange("(k p) c -> p k c", p=P)
            loads = [
                (ln1_g[:], column(A["L0_xattn_ln1_w"], KC)), (ln1_b[:], column(A["L0_xattn_ln1_b"], KC)),
                (mask_row[:], A["mask_BxS_bf0"]),
                (e.qkv_w[:], rows("L0_xattn_qkv_w")),
                (e.qkv_b[:], column(A["L0_xattn_qkv_b"][0:2 * C], 2 * KC)),
                (e.v0_brep[:], A["L0_xattn_qkv_b"][2 * C:3 * C].partition_broadcast(P)),
                (e.proj_brep[:], A["L0_xattn_proj_b"].partition_broadcast(P)),
            ]
            assert len(loads) == N_LOADS
            for dst, src in loads:
                sp.dma_start(dst, src).then_inc(w_in, 16)
            sp.wait_ge(gp.sem, gp.value("fills"))
            for j in range(4):
                sp.dma_start(e.proj_w[32 * j:32 * j + 16, :, :],
                             A["L0_xattn_proj_w"].rearrange("(g j d) c -> j d g c", j=4, d=16)[j]).then_inc(p_in, 16)
            sp.wait_ge(dv.sem, dv.value("maskf"))
            for g in range(4):
                for b in range(B):
                    sp.dma_start(e.mask_dram[4 * b + g:4 * b + g + 1, :], mask_f[b:b + 1, :]).then_inc(m_out, 16)
            sp.wait_ge(m_out, 16 * 8)
            sp.wait_ge(p_in, 16 * 4)

        @block.gpsimd
        def _(pool):
            nc.gpsimd.memset(e.ident[:], 0.0)
            nc.gpsimd.memset(e.tri[:], 0.0)
            nc.gpsimd.memset(e.sel[:], 0.0).then_inc(gp.sem, gp.one("zeros"))
            pool.wait_ge(gp.sem, gp.value("zeros"))
            nc.gpsimd.affine_select(out=e.ident[:], in_=e.ident[:], compare_op=ALU.not_equal, fill=1.0, base=0,
                                    pattern=[[-1, P]], channel_multiplier=1).then_inc(gp.sem, gp.one("ident"))
            nc.gpsimd.memset(e.eps[:], EPS)
            nc.gpsimd.memset(e.ones[:], 1.0)
            nc.gpsimd.memset(e.proj_w[:], 0.0).then_inc(gp.sem, gp.one("fills"))
            nc.gpsimd.affine_select(out=e.tri[:], in_=e.tri[:], compare_op=ALU.is_ge, fill=MASKED, base=0,
                                    pattern=[[-1, P]], channel_multiplier=1)
            nc.gpsimd.affine_select(out=e.sel[:].rearrange("p (j d) -> p j d", j=4),
                                    in_=e.sel[:].rearrange("p (j d) -> p j d", j=4), compare_op=ALU.not_equal,
                                    fill=1.0, base=-16, pattern=[[-32, 4], [0, 32]],
                                    channel_multiplier=1).then_inc(gp.sem, gp.one("selects"))

        @block.vector
        def _(dve):
            dve.wait_ge(w_in, 16 * N_LOADS)
            dve.tensor_scalar(mask_f[:], mask_row[:], MASKED, None, ALU.mult).then_inc(dv.sem, dv.one("maskf"))
            dve.wait_ge(gp.sem, gp.value("selects"))
            dve.tensor_scalar(e.qkv_bs[:], e.qkv_b[:], 0.25, None, ALU.mult)
            dve.tensor_copy(e.ident_bf[:], e.ident[:])
            dve.tensor_copy(e.tri_bf[:], e.tri[:]).then_inc(dv.sem, dv.one("consts"))
            dve.wait_ge(x_in, 16)
            for t in range(TILES):
                ins = dve.bn_stats(stats[:, t, :], e.x[:, t, :])
            ins.then_inc(dv.sem, dv.one("stats"))
            dve.wait_ge(dv.sem, dv.value("stats"))
            for t in range(TILES):
                ins = dve.bn_aggr(moments[:, t, :], stats[:, t, :])
            ins.then_inc(dv.sem, dv.one("moments"))
            dve.wait_ge(ln.sem, ln.value("rstd"))
            for t in range(TILES):
                ins = dve.tensor_scalar(h[:, t, :], e.x[:, t, :], moments[:, t, 0:1], rstd[:, t:t + 1],
                                        ALU.subtract, ALU.mult)
                if t % 2:
                    ins.then_inc(dv.sem, dv.one(f"h{t // 2}"))

        @block.scalar
        def _(act):
            act.wait_ge(gp.sem, gp.value("fills"))
            act.wait_ge(w_in, 16 * N_LOADS)
            act.wait_ge(dv.sem, dv.value("moments"))
            act.activation(rstd[:], moments[:, :, 1], ACT.Ln, bias=e.eps[:]).then_inc(ln.sem, ln.one("logvar"))
            act.wait_ge(ln.sem, ln.value("logvar"))
            act.activation(rstd[:], rstd[:], ACT.Exp, scale=-0.5).then_inc(ln.sem, ln.one("rstd"))
            for i in range(8):
                act.wait_ge(pe.sem, pe.value(f"hT{i}"))
                for c in range(KC):
                    ins = act.activation(e.hT[:, c, i * 256:(i + 1) * 256], ps[i][:, c * 256:(c + 1) * 256],
                                         ACT.Identity, bias=ln1_b[:, c:c + 1], scale=ln1_g[:, c:c + 1])
                ins.then_inc(ev.sem, ev.one(f"hT{i}"))

        @block.tensor
        def _(te):
            te.wait_ge(gp.sem, gp.value("ident"))
            for i in range(8):
                te.wait_ge(dv.sem, dv.value(f"h{i}"))
                for c in range(KC):
                    for t in range(2):
                        ins = te.transpose(ps[i][:, (2 * c + t) * P:(2 * c + t + 1) * P],
                                           h[:, 2 * i + t, c * P:(c + 1) * P], e.ident[:])
                ins.then_inc(pe.sem, pe.one(f"hT{i}"))


def part_qkv0(nc, e):
    with ExitStack() as ctx:
        sb = lambda n, s, d=F32: ctx.enter_context(nc.sbuf_tensor(n, s, d))
        sem = lambda n: ctx.enter_context(nc.semaphore(n))
        full = [sb(f"qk_full{i}", [P, 512]) for i in range(2)]
        high = [sb(f"qk_high{i}", [P, 512], F32R) for i in range(2)]
        low = [sb(f"qk_low{i}", [P, 512], F32R) for i in range(2)]
        ps = [ctx.enter_context(nc.psum_tensor(f"qkv{i}", [P, 512], F32)) for i in range(8)]
        made, evacuated, split, v_kept = sem("qkv_made"), sem("qk_evacuated"), sem("qk_split"), sem("v_kept")
        stored = [sem("qk_stored0"), sem("qk_stored1")]
        QK = [(w, fc, quarter) for w in range(2) for fc in range(KC) for quarter in range(4)]
        block = ctx.enter_context(nc.Block())

        @block.tensor
        def _(te):
            for u, (w, fc, quarter) in enumerate(QK):
                if u >= 8:
                    te.wait_ge(evacuated, u - 7)
                for k in range(KC):
                    ins = te.matmul(ps[u % 8][:], e.qkv_w[:, k, w * C + fc * P:w * C + (fc + 1) * P],
                                    e.hT[:, k, quarter * 512:(quarter + 1) * 512], start=k == 0, stop=k == KC - 1)
                ins.then_inc(made, 1)
            for u in range(8):
                te.wait_ge(evacuated, 9 + u)
                for t in range(2):
                    for k in range(KC):
                        ins = te.matmul(ps[u][:, t * C:(t + 1) * C],
                                        e.hT[:, k, (2 * u + t) * P:(2 * u + t + 1) * P],
                                        e.qkv_w[:, k, 2 * C:3 * C], start=k == 0, stop=k == KC - 1)
                ins.then_inc(made, 1)

        @block.scalar
        def _(act):
            for u, (w, fc, quarter) in enumerate(QK):
                act.wait_ge(made, u + 1)
                if u >= 2:
                    act.wait_ge(split, 2 * (u - 1))
                act.activation(full[u % 2][:], ps[u % 8][:], ACT.Identity, scale=0.25 if w == 0 else 1.0,
                               bias=(e.qkv_bs if w == 0 else e.qkv_b)[:, 2 * w + fc:2 * w + fc + 1]
                               ).then_inc(evacuated, 1)

        @block.vector
        def _(dve):
            for u in range(len(QK)):
                dve.wait_ge(evacuated, u + 1)
                if u >= 2:
                    dve.wait_ge(stored[u % 2], 64 * (u // 2))
                dve.tensor_copy(high[u % 2][:], full[u % 2][:]).then_inc(split, 1)
                dve.wait_ge(split, 2 * u + 1)
                dve.tensor_tensor(out=low[u % 2][:], in0=full[u % 2][:], in1=high[u % 2][:].bitcast(F32),
                                  op=ALU.subtract).then_inc(split, 1)
            for u in range(8):
                dve.wait_ge(made, 17 + u)
                b, kt = 2 * u // TB, 2 * u % TB
                for t in range(2):
                    dve.tensor_tensor(out=e.v_all[:, b, :, kt + t, :],
                                      in0=ps[u][:, t * C:(t + 1) * C].rearrange("p (g f) -> p g f", g=4),
                                      in1=e.v0_brep[:].rearrange("p (g f) -> p g f", g=4), op=ALU.add)

        @block.sync
        def _(sp):
            for u, (w, fc, quarter) in enumerate(QK):
                b, cols = quarter // 2, slice((quarter % 2) * 512, (quarter % 2 + 1) * 512)
                sp.wait_ge(split, 2 * u + 2)
                for part, tile in ((0, high), (1, low)):
                    for half in range(2):
                        sp.dma_start(e.qk_dram[w, 4 * b + 2 * fc + half, part, :, cols],
                                     tile[u % 2][64 * half:64 * half + 64, :].bitcast(F32)).then_inc(stored[u % 2], 16)
            for i in range(2):
                sp.wait_ge(stored[i], 64 * 8)


def part_attention0(nc, e):
    with ExitStack() as ctx:
        sb = lambda n, s, d=F32: ctx.enter_context(nc.sbuf_tensor(n, s, d))
        sem = lambda n: ctx.enter_context(nc.semaphore(n))
        qs = [sb(f"q_stack{i}", [66, 4, T], F32R) for i in range(2)]
        ks = [sb(f"k_stack{i}", [66, 4, T], F32R) for i in range(2)]
        v4 = [sb(f"v_group{i}", [P, TB, 4, 32]) for i in range(2)]
        probs = [[sb(f"probs{j}{i}", [P, T]) for i in range(2)] for j in range(4)]
        raw, rden = sb("raw", [P, T]), sb("rden", [P, T])
        part_max, row_max = sb("part_max", [P, 2, 4, 4]), sb("row_max", [P, 4, TB])
        max_row = sb("max_row", [32, P], F32R)
        s1 = [ctx.enter_context(nc.psum_tensor(f"s1_{i}", [P, 512], F32)) for i in range(2)]
        s2 = [ctx.enter_context(nc.psum_tensor(f"s2_{i}", [P, T], F32)) for i in range(2)]
        o = ctx.enter_context(nc.psum_tensor("o", [P, T], F32))
        stack_in = [sem("stack_in0"), sem("stack_in1")]
        v_ready, rows_set = sem("v_ready"), sem("rows_set")
        s1_made, s1_max, max_made, max_turned, max_kept = (
            sem(n) for n in ("s1_made", "s1_max", "max_made", "max_turned", "max_kept"))
        max_out, max_in = sem("max_out"), sem("max_in")
        s2_made, exp_made, pv_made, raw_made = sem("s2_made"), sem("exp_made"), sem("pv_made"), sem("raw_made")
        den_made, log_made, rden_made, a_made = sem("den_made"), sem("log_made"), sem("rden_made"), sem("a_made")

        CH = [(j, t, k0, min(k0 + 512, (t + 1) * P)) for j in range(4) for t in range(TB)
              for k0 in range(0, (t + 1) * P, 512)]
        UN = [(kt, j) for kt in range(TB) for j in range(4)]
        N1, N2, G = len(CH), len(UN), 8
        pieces = lambda kt: [(max(kt * P, c0), c0 + 512) for c0 in (0, 512) if c0 + 512 > kt * P]

        def groups(engine, emit):
            emit(None, 0, 1, 1)
            emit(0, 1, 0, 1)
            with engine.Fori(0, 3) as i:
                emit(2 * i + 1, 2 * i + 2, 1, i + 2)
                emit(2 * i + 2, 2 * i + 3, 0, i + 2)
            emit(7, None, 1, None)

        block = ctx.enter_context(nc.Block())

        @block.sync
        def _(sp):
            sp.wait_ge(rows_set, 1)

            def emit(cur, nxt, par, loads):
                if nxt is not None:
                    q, k, done = qs[1 - par], ks[1 - par], stack_in[1 - par]
                    loads = [(stack[16 * i:16 * i + 16].bitcast(F32),
                              src[ds(nxt, 1), part].rearrange("g (j d) t -> d (g j) t", j=4))
                             for stack, src, parts in ((q, e.qk_dram[0], (0, 1, 0, 1)), (k, e.qk_dram[1], (0, 0, 1, 1)))
                             for i, part in enumerate(parts)]
                    if cur is not None and not (isinstance(cur, int) and cur == 0):
                        sp.wait_ge(s2_made, N2 * cur)
                    for dst, rows in loads:
                        sp.dma_start(dst, rows).then_inc(done, 16)
                    mask = e.mask_dram[ds(nxt, 1), :]
                    for j in range(4):
                        sp.dma_start(k[64:65, j, :].bitcast(F32), mask).then_inc(done, 16)
                    sp.wait_ge(max_kept, nxt + 1)
                    sp.dma_start(e.max_dram[1 - par], max_row[:].bitcast(F32)).then_inc(max_out, 16)
                    sp.wait_ge(max_out, 16 * (nxt + 1))
                    sp.dma_start(qs[1 - par][65:66].bitcast(F32), e.max_dram[1 - par].rearrange("(o j t) q -> o j (t q)", o=1, j=4)
                                 ).then_inc(max_in, 16)

            groups(sp, emit)

        @block.gpsimd
        def _(pool):
            pool.wait_ge(rows_set, 1)

            def emit(cur, nxt, par, loads):
                if nxt is not None:
                    if cur is not None and not (isinstance(cur, int) and cur == 0):
                        pool.wait_ge(pv_made, TB * cur)
                    src = e.v_all[:].rearrange("p b g k f -> p (b g) k f")[:, ds(nxt, 1)]
                    pool.tensor_copy(v4[1 - par][:, :, :, 0:16],
                                     src.rearrange("p o k (j d) -> p (o k) j d", j=4)).then_inc(v_ready, 1)

            groups(pool, emit)

        @block.tensor
        def _(te):
            te.wait_ge(rows_set, 1)

            def emit(cur, nxt, par, loads):
                if nxt is not None:
                    q1, k1 = qs[1 - par], ks[1 - par]

                    def chunk(i):
                        j, t, c0, c1 = CH[i]
                        if i >= 2:
                            te.wait_ge(s1_max, N1 * nxt + i - 1)
                        elif cur is not None and not (isinstance(cur, int) and cur == 0):
                            te.wait_ge(log_made, cur)
                        elif cur is not None:
                            te.wait_ge(max_kept, 1)
                        diagonal = c1 == (t + 1) * P
                        ins = te.matmul(s1[i % 2][:, 0:c1 - c0], q1[0:65, j, t * P:(t + 1) * P], k1[0:65, j, c0:c1],
                                        start=True, stop=not diagonal)
                        if diagonal:
                            ins = te.matmul(s1[i % 2][:, t * P - c0:c1 - c0], e.ident_bf[:], e.tri_bf[:],
                                            start=False, stop=True)
                        ins.then_inc(s1_made, 1)
                if cur is not None:
                    q2, k2, v = qs[par], ks[par], v4[par]

                    def unit(u):
                        kt, j = UN[u]
                        if u >= 2:
                            te.wait_ge(exp_made, N2 * cur + u - 1)
                        elif not (isinstance(cur, int) and cur == 0):
                            te.wait_ge(exp_made, N2 * cur)
                        for c0, c1 in pieces(kt):
                            diagonal = c0 == kt * P
                            ins = te.matmul(s2[u % 2][:, c0:c1], k2[0:66, j, kt * P:(kt + 1) * P], q2[0:66, j, c0:c1],
                                            start=True, stop=not diagonal)
                            if diagonal:
                                ins = te.matmul(s2[u % 2][:, c0:c0 + P], e.tri_bf[:], e.ident_bf[:],
                                                start=False, stop=True)
                        ins.then_inc(s2_made, 1)

                    def values(kt):
                        te.wait_ge(exp_made, N2 * cur + 4 * kt + 4)
                        for c0, c1 in pieces(kt):
                            for j in range(4):
                                last = kt == (3 if c1 == 512 else 7)
                                ins = te.matmul(o[32 * j:32 * j + 32, c0:c1], v[:, kt, j, :],
                                                probs[j][kt % 2][:, c0:c1], start=kt == 0, stop=last)
                        ins.then_inc(pv_made, 1)

                    te.wait_ge(max_in, 16 * (cur + 1))
                    te.wait_ge(v_ready, cur + 1)
                if cur is not None:
                    done = 0
                    for u in range(N2):
                        unit(u)
                        if u % 4 == 1 and u >= 5:
                            values(u // 4 - 1)
                        if nxt is not None and u >= 8:
                            if u == 8:
                                te.wait_ge(stack_in[1 - par], 192 * loads)
                            while done < (u - 7) * N1 // (N2 - 8):
                                chunk(done)
                                done += 1
                    values(TB - 1)
                else:
                    te.wait_ge(stack_in[1 - par], 192 * loads)
                    for i in range(N1):
                        chunk(i)
                if nxt is not None:
                    te.wait_ge(max_made, nxt + 1)
                    te.transpose(s1[0][0:32, 0:P], row_max[:].rearrange("p j t -> p (j t)"),
                                 e.ident[:]).then_inc(max_turned, 1)
                if cur is not None:
                    te.wait_ge(raw_made, cur + 1)
                    if nxt is not None:
                        te.wait_ge(max_kept, nxt + 1)
                    else:
                        te.wait_ge(s1_max, N1 * G)
                    for half in range(2):
                        ins = te.matmul(s1[half][:], e.sel[:], raw[:, half * 512:(half + 1) * 512],
                                        start=True, stop=True)
                    ins.then_inc(den_made, 1)

            groups(te, emit)

        @block.vector
        def _(dve):
            for i in range(2):
                dve.memset(qs[i][64:66].bitcast(F32), 1.0)
                dve.memset(v4[i][:], 1.0)
                ins = dve.memset(ks[i][64:66].bitcast(F32), 1.0)
            ins.then_inc(rows_set, 1)

            def emit(cur, nxt, par, loads):
                if nxt is not None:
                    for i, (j, t, c0, c1) in enumerate(CH):
                        dve.wait_ge(s1_made, N1 * nxt + i + 1)
                        dst = row_max[:, j, t:t + 1] if t < 4 else part_max[:, c0 // 512, j, t - 4:t - 3]
                        if i == 0 and cur is not None:
                            dve.wait_ge(max_turned, nxt)
                        dve.tensor_reduce(dst, s1[i % 2][:, 0:c1 - c0], AX.X, ALU.max).then_inc(s1_max, 1)
                    dve.wait_ge(s1_max, N1 * nxt + N1)
                    dve.tensor_tensor(out=row_max[:, :, 4:8], in0=part_max[:, 0], in1=part_max[:, 1],
                                      op=ALU.max).then_inc(max_made, 1)
                if cur is not None:
                    dve.wait_ge(rden_made, cur + 1)
                    dve.tensor_tensor(out=e.aT0[:, ds(cur, 1), :].rearrange("p o t -> p (o t)"), in0=raw[:],
                                      in1=rden[:], op=ALU.mult).then_inc(a_made, 1)

            groups(dve, emit)

        @block.scalar
        def _(act):
            def emit(cur, nxt, par, loads):
                if cur is not None:
                    for u, (kt, j) in enumerate(UN):
                        act.wait_ge(s2_made, N2 * cur + u + 1)
                        if kt >= 2:
                            act.wait_ge(pv_made, TB * cur + kt - 1)
                        elif not (isinstance(cur, int) and cur == 0) and j == 0:
                            act.wait_ge(pv_made, TB * cur)
                        act.activation(probs[j][kt % 2][:, kt * P:T], s2[u % 2][:, kt * P:T],
                                       ACT.Exp).then_inc(exp_made, 1)
                    act.wait_ge(pv_made, TB * (cur + 1))
                    if not (isinstance(cur, int) and cur == 0):
                        act.wait_ge(a_made, cur)
                    act.activation(raw[:], o[:], ACT.Identity).then_inc(raw_made, 1)
                if nxt is not None:
                    act.wait_ge(max_turned, nxt + 1)
                    if cur is not None:
                        act.wait_ge(max_out, 16 * nxt)
                    act.activation(max_row[:], s1[0][0:32, 0:P], ACT.Identity, scale=-1.0).then_inc(max_kept, 1)
                if cur is not None:
                    act.wait_ge(den_made, cur + 1)
                    for half in range(2):
                        ins = act.activation(rden[:, half * 512:(half + 1) * 512], s1[half][:], ACT.Ln)
                    ins.then_inc(log_made, 1)
                    act.wait_ge(log_made, cur + 1)
                    act.activation(rden[:], rden[:], ACT.Exp, scale=-1.0).then_inc(rden_made, 1)

            groups(act, emit)



def part_project0(nc, e):
    with ExitStack() as ctx:
        ps = [ctx.enter_context(nc.psum_tensor(f"prj{i}", [P, 2, C], F32)) for i in range(4)]
        made, added = ctx.enter_context(nc.semaphore("prj_made")), ctx.enter_context(nc.semaphore("prj_added"))
        block = ctx.enter_context(nc.Block())

        @block.tensor
        def _(te):
            for u in range(TILES // 2):
                if u >= 4:
                    te.wait_ge(added, u - 2)
                b = 2 * u // TB
                for i in range(2):
                    t = (2 * u + i) % TB
                    for g in range(4):
                        ins = te.matmul(ps[u % 4][:, i, :], e.aT0[:, 4 * b + g, t * P:(t + 1) * P], e.proj_w[:, g, :],
                                        start=g == 0, stop=g == 3)
                ins.then_inc(made, 1)

        @block.vector
        def _(dve):
            bias = e.proj_brep[:].unsqueeze(1).to_broadcast([P, TILES, C])
            dve.tensor_tensor(out=e.x[:], in0=e.x[:], in1=bias, op=ALU.add).then_inc(added, 1)
            dve.wait_ge(added, 1)
            for u in range(TILES // 2):
                dve.wait_ge(made, u + 1)
                x = e.x[:, 2 * u:2 * u + 2, :]
                dve.tensor_tensor(out=x, in0=ps[u % 4][:], in1=x, op=ALU.add).then_inc(added, 1)


def part_context0(nc, e, A, later):
    with ExitStack() as ctx:
        sb = lambda n, s, d=F32: ctx.enter_context(nc.sbuf_tensor(n, s, d))
        sem = lambda n: ctx.enter_context(nc.semaphore(n))
        ctx_rows = sb("ctx_rows", [P, CC])
        q_w, q_b = sb("q_w", [P, KC, C]), sb("q_b", [P, KC])
        k_w, k_b = sb("k_w", [96, 2, C]), sb("k_b", [P, KC])
        v_w, v_b = sb("v_w", [96, 2, C]), sb("v_b", [P, KC])
        o_w = sb("o_w", [P, KC, C])
        t_w, t_b = sb("t_w", [96, 2, C]), sb("t_b", [P, KC])
        t_brep = sb("t_brep", [S2, C])
        mask8 = sb("mask8", [P, B, S2], mybir.dt.uint8)
        mrep = sb("mrep", [P, B, S2])
        head16 = sb("head16", [P, 8])
        ones_col = sb("ones_col", [P, P])
        q_brep = sb("q_brep", [P, KC, P])
        q_wT = sb("q_wT", [P, KC, C])
        kT, vT = sb("kT", [P, KC, P]), sb("vT", [P, KC, P])
        kbd = sb("kbd", [P, B, KC, 8, S2])
        vbd = sb("vbd", [P, B, KC, 8, S2])
        ps = [ctx.enter_context(nc.psum_tensor(f"cross{i}", [P, 512], F32)) for i in range(8)]
        c_in, w_in, later_in = sem("c_in"), sem("cw_in"), sem("chain_w_in")
        order = (["ctxT", "q_wT", "kT", "vT", "tok", "tokT"]
                 + [f"M{b}{g}{d}" for b in range(B) for g in range(KC) for d in range(KC)]
                 + [f"bias{b}{g}" for b in range(B) for g in range(KC)]
                 + [f"VW{b}{c}" for b in range(B) for c in range(4)])
        pe = Steps(sem("cross_pe"), order)
        ev = Steps(sem("cross_evac"), order)
        dv = Steps(sem("cross_dve"), ["mrep", "brep", "kbd", "vbd"])
        gp = Steps(sem("cross_pool"), ["ones", "first", "second"])
        bank = lambda name: order.index(name) % 8
        N_LOADS = 11
        ALL_W = 16 * N_LOADS
        block = ctx.enter_context(nc.Block())

        @block.sync
        def _(sp):
            sp.dma_start(ctx_rows[:], A["ctx_768"].rearrange("b s c -> (b s) c")).then_inc(c_in, 16)
            rows96 = lambda n: A[n].rearrange("(k p) c -> p k c", p=96)
            rows = lambda n: A[n].rearrange("(k p) c -> p k c", p=P)
            loads = [
                (q_w[:], rows("L0_xattn_q_w")), (q_b[:], column(A["L0_xattn_q_b"], KC)),
                (k_w[:], rows96("L0_xattn_k_w")), (k_b[:], column(A["L0_xattn_k_b"], KC)),
                (v_w[:], rows96("L0_xattn_v_w")), (v_b[:], column(A["L0_xattn_v_b"], KC)),
                (o_w[:], rows("L0_xattn_out_w")),
                (t_w[:], rows96("L1_xattn_W_proj")), (t_b[:], column(A["L1_xattn_b_proj"], KC)),
                (t_brep[:], A["L1_xattn_b_proj"].partition_broadcast(S2)),
                (mask8[:], A["mask_BxS2_bf0"].rearrange("b s -> (b s)").partition_broadcast(P)
                 .rearrange("p (b s) -> p b s", b=B)),
            ]
            for dst, src in loads:
                sp.dma_start(dst, src).then_inc(w_in, 16)
            assert len(loads) == N_LOADS
            for dst, src in later:
                sp.dma_start(dst, src).then_inc(later_in, 16)
            sp.wait_ge(later_in, 16 * len(later))


        @block.gpsimd
        def _(pool):
            pool.memset(head16[:], 1.0)
            pool.memset(ones_col[:], 1.0).then_inc(gp.sem, gp.one("ones"))
            pool.wait_ge(gp.sem, gp.value("ones"))
            pool.affine_select(out=head16[:], in_=head16[:], compare_op=ALU.is_ge, fill=0.0, base=0,
                               pattern=[[-16, 8]], channel_multiplier=1).then_inc(gp.sem, gp.one("first"))
            pool.wait_ge(gp.sem, gp.value("first"))
            pool.affine_select(out=head16[:], in_=head16[:], compare_op=ALU.is_ge, fill=0.0, base=15,
                               pattern=[[16, 8]], channel_multiplier=-1).then_inc(gp.sem, gp.one("second"))

        @block.vector
        def _(dve):
            dve.wait_ge(w_in, ALL_W)
            dve.tensor_scalar(mrep[:], mask8[:], MASKED, None, ALU.mult).then_inc(dv.sem, dv.one("mrep"))
            dve.wait_ge(gp.sem, gp.value("second"))
            for g in range(KC):
                ins = dve.tensor_scalar(q_brep[:, g, :], ones_col[:], q_b[:, g:g + 1], 0.25, ALU.mult,
                                        ALU.mult)
            ins.then_inc(dv.sem, dv.one("brep"))
            head_rep = head16[:].unsqueeze(2).to_broadcast([P, 8, S2])
            dve.wait_ge(ev.sem, ev.value("vT"))
            for name, dst, src in (("kbd", kbd, kT), ("vbd", vbd, vT)):
                for b in range(B):
                    for g in range(KC):
                        rep = src[:, g, b * S2:(b + 1) * S2].unsqueeze(1).to_broadcast([P, 8, S2])
                        ins = dve.tensor_tensor(out=dst[:, b, g], in0=rep, in1=head_rep, op=ALU.mult)
                ins.then_inc(dv.sem, dv.one(name))
            dve.wait_ge(ev.sem, ev.value(f"bias{B - 1}{KC - 1}"))
            for b in range(B):
                view = e.bias0[:, b, :].rearrange("p (h s) -> p h s", s=S2)
                dve.tensor_tensor(out=view, in0=view, in1=mrep[:, b, :].unsqueeze(1).to_broadcast([P, 16, S2]),
                                  op=ALU.add)

        @block.scalar
        def _(act):
            def copy(name, dst, src, **kw):
                act.wait_ge(pe.sem, pe.value(name))
                act.activation(dst, src, ACT.Identity, **kw).then_inc(ev.sem, ev.one(name))

            act.wait_ge(w_in, ALL_W)
            p = lambda name: ps[bank(name)]
            copy("ctxT", e.ctxT[:], p("ctxT")[0:96, 0:256].rearrange("p (k s) -> p k s", k=2))
            copy("q_wT", q_wT[:], p("q_wT")[:].rearrange("p (k c) -> p k c", k=2))
            for name, dst, bias in (("kT", kT, k_b), ("vT", vT, v_b)):
                act.wait_ge(pe.sem, pe.value(name))
                for g in range(KC):
                    ins = act.activation(dst[:, g, :], p(name)[:, g * P:(g + 1) * P], ACT.Identity,
                                         bias=bias[:, g:g + 1])
                ins.then_inc(ev.sem, ev.one(name))
            act.wait_ge(pe.sem, pe.value("tok"))
            act.activation(e.tok[:], p("tok")[0:S2, :].rearrange("p (b c) -> p b c", b=B),
                           ACT.Identity).then_inc(ev.sem, ev.one("tok"))
            act.wait_ge(pe.sem, pe.value("tokT"))
            for g in range(KC):
                ins = act.activation(e.tokT[:, g, :], p("tokT")[:, g * P:(g + 1) * P], ACT.Identity,
                                     bias=t_b[:, g:g + 1])
            ins.then_inc(ev.sem, ev.one("tokT"))
            for b in range(B):
                for g in range(KC):
                    for d in range(KC):
                        copy(f"M{b}{g}{d}", e.m0[:, b, d, g * 512:(g + 1) * 512], p(f"M{b}{g}{d}")[:], scale=0.25)
            for b in range(B):
                for g in range(KC):
                    copy(f"bias{b}{g}", e.bias0[:, b, g * 512:(g + 1) * 512], p(f"bias{b}{g}")[:])
            for b in range(B):
                for c in range(4):
                    copy(f"VW{b}{c}", e.vw0[:, b, 2 * c:2 * c + 2, :],
                         p(f"VW{b}{c}")[:].rearrange("p (c n) -> p c n", c=2))

        @block.tensor
        def _(te):
            free = lambda name: te.wait_ge(ev.sem, order.index(name) - 7) if order.index(name) >= 8 else None
            p = lambda name: ps[bank(name)]
            te.wait_ge(c_in, 16)
            te.wait_ge(w_in, ALL_W)
            for k in range(2):
                ins = te.transpose(p("ctxT")[0:96, k * P:(k + 1) * P], ctx_rows[:, 96 * k:96 * k + 96], e.ident[:])
            ins.then_inc(pe.sem, pe.one("ctxT"))
            for g in range(KC):
                for d in range(KC):
                    ins = te.transpose(p("q_wT")[:, (2 * g + d) * P:(2 * g + d + 1) * P],
                                       q_w[:, d, g * P:(g + 1) * P], e.ident[:])
            ins.then_inc(pe.sem, pe.one("q_wT"))
            te.wait_ge(ev.sem, ev.value("ctxT"))
            for name, w in (("kT", k_w), ("vT", v_w)):
                for g in range(KC):
                    for k in range(2):
                        ins = te.matmul(p(name)[:, g * P:(g + 1) * P], w[:, k, g * P:(g + 1) * P], e.ctxT[:, k, :],
                                        start=k == 0, stop=k == 1)
                ins.then_inc(pe.sem, pe.one(name))
            for b in range(B):
                for k in range(2):
                    te.matmul(p("tok")[0:S2, b * C:(b + 1) * C], e.ctxT[:, k, b * S2:(b + 1) * S2], t_w[:, k, :],
                              start=k == 0, stop=False)
                ins = te.matmul(p("tok")[0:S2, b * C:(b + 1) * C], e.ident[0:S2, 0:S2], t_brep[:],
                                start=False, stop=True)
            ins.then_inc(pe.sem, pe.one("tok"))
            for g in range(KC):
                for k in range(2):
                    ins = te.matmul(p("tokT")[:, g * P:(g + 1) * P], t_w[:, k, g * P:(g + 1) * P], e.ctxT[:, k, :],
                                    start=k == 0, stop=k == 1)
            ins.then_inc(pe.sem, pe.one("tokT"))
            te.wait_ge(dv.sem, dv.value("vbd"))
            for b in range(B):
                for g in range(KC):
                    for d in range(KC):
                        free(f"M{b}{g}{d}")
                        te.matmul(p(f"M{b}{g}{d}")[:], q_wT[:, g, d * P:(d + 1) * P],
                                  kbd[:, b, g].rearrange("p h s -> p (h s)"), start=True,
                                  stop=True).then_inc(pe.sem, pe.one(f"M{b}{g}{d}"))
            for b in range(B):
                for g in range(KC):
                    free(f"bias{b}{g}")
                    te.matmul(p(f"bias{b}{g}")[:], q_brep[:, g, :], kbd[:, b, g].rearrange("p h s -> p (h s)"),
                              start=True, stop=True).then_inc(pe.sem, pe.one(f"bias{b}{g}"))
            for b in range(B):
                for c in range(4):
                    free(f"VW{b}{c}")
                    for i in range(2):
                        g, pair = (2 * c + i) // 4, (2 * c + i) % 4
                        ins = te.matmul(p(f"VW{b}{c}")[:, i * C:(i + 1) * C],
                                        vbd[:, b, g, 2 * pair:2 * pair + 2, :].rearrange("p h s -> p (h s)"),
                                        o_w[:, g, :], start=True, stop=True)
                    ins.then_inc(pe.sem, pe.one(f"VW{b}{c}"))


BLOCKS = TB // 2


def norm_steps(name):
    return [f"{name}.stats", f"{name}.moments", f"{name}.h"]


class Chain:

    def __init__(self, nc, ctx, label, te, dve, act, pool):
        self.nc = nc
        sem = lambda n: ctx.enter_context(nc.semaphore(n))
        self.te, self.dve, self.act, self.pool = (
            [Steps(sem(f"{label}_{name}{s}"), order) for s in range(B)]
            for name, order in (("tensor", te), ("vector", dve), ("scalar", act), ("gpsimd", pool)))
        sb = lambda n, shape, d=F32: [ctx.enter_context(nc.sbuf_tensor(f"{label}_{n}{s}", shape, d)) for s in range(B)]
        self.sb = sb
        self.h, self.hT = sb("h", [P, 2, C]), sb("hT", [P, KC, 256])
        self.stats, self.moments, self.rstd = sb("stats", [P, 2, 6]), sb("moments", [P, 2, 2]), sb("rstd", [P, 2])
        self.scores, self.pT = sb("scores", [P, 2, 1024]), sb("pT", [P, 8, 256])
        self.top, self.total = sb("top", [P, 32]), sb("total", [P, 32])
        self.spare = sb("spare", [1, 1])
        self.xc, self.xT = sb("xc", [P, 2, C]), sb("xT", [P, KC, 256])
        self.ps = [ctx.enter_context(nc.psum_tensor(f"{label}_ps{s}", [P, 2048], F32)) for s in range(B)]


def after(engine, steps, name, turn):
    engine.wait_ge(steps.sem, steps.value(name, turn))


def after_spare(dve, ch, s, name, turn):
    after(dve, ch.dve[s], name, turn)
    dve.memset(ch.spare[s][:], 0.0)


def tokens(e, s, i):
    return e.x[:, TB * s:TB * (s + 1), :].rearrange("p (i t) c -> p i (t c)", t=2)[:, ds(i, 1), :].rearrange(
        "p o (t c) -> p (o t) c", t=2)


def norm_vector(dve, ch, name, i, source, before=None, second=None):
    for s in range(B):
        if before:
            before(s)
        for t in range(2):
            ins = dve.bn_stats(ch.stats[s][:, t, :], source(s)[:, t, :])
        ins.then_inc(ch.dve[s].sem, ch.dve[s].one(f"{name}.stats"))
    for s in range(B):
        after_spare(dve, ch, s, f"{name}.stats", i)
        for t in range(2):
            ins = dve.bn_aggr(ch.moments[s][:, t, :], ch.stats[s][:, t, :])
        ins.then_inc(ch.dve[s].sem, ch.dve[s].one(f"{name}.moments"))
    for s in range(B):
        after(dve, ch.act[s], f"{name}.rstd", i)
        for t in range(2):
            ins = dve.tensor_scalar(ch.h[s][:, t, :], source(s)[:, t, :], ch.moments[s][:, t, 0:1],
                                    ch.rstd[s][:, t:t + 1], ALU.subtract, ALU.mult)
        ins.then_inc(ch.dve[s].sem, ch.dve[s].one(f"{name}.h"))


def norm_scalar(act, ch, e, name, i):
    for s in range(B):
        after(act, ch.dve[s], f"{name}.moments", i)
        act.activation(ch.rstd[s][:], ch.moments[s][:, :, 1], ACT.Ln, bias=e.eps[:]).then_inc(
            ch.act[s].sem, ch.act[s].one(f"{name}.log"))
    for s in range(B):
        after(act, ch.act[s], f"{name}.log", i)
        act.activation(ch.rstd[s][:], ch.rstd[s][:], ACT.Exp, scale=-0.5).then_inc(
            ch.act[s].sem, ch.act[s].one(f"{name}.rstd"))


def turn_tensor(te, ch, e, src, s, bank):
    for c in range(KC):
        for t in range(2):
            ins = te.transpose(ch.ps[s][:, 512 * bank + (2 * c + t) * P:512 * bank + (2 * c + t + 1) * P],
                               src[:, t, c * P:(c + 1) * P], e.ident[:])
    return ins


def turned_scalar(act, ch, s, bank, dst, gain=None, bias=None):
    for c in range(KC):
        kw = dict(scale=gain[:, c:c + 1], bias=bias[:, c:c + 1]) if gain is not None else {}
        ins = act.activation(dst[:, c, :], ch.ps[s][:, 512 * bank + 256 * c:512 * bank + 256 * (c + 1)],
                             ACT.Identity, **kw)
    return ins


def cross_tensor(te, ch, e, name, i, lhs, lhs_ready, m, vw, cols):
    for s in range(B):
        after(te, ch.act[s], lhs_ready, i)
        for t in range(2):
            for c0 in range(0, cols, 512):
                for k in range(KC):
                    ins = te.matmul(ch.ps[s][:, t * cols + c0:t * cols + c0 + 512], lhs[s][:, k, t * P:(t + 1) * P],
                                    m[:, s, k, c0:c0 + 512], start=k == 0, stop=k == KC - 1)
        ins.then_inc(ch.te[s].sem, ch.te[s].one(f"{name}.scores"))
    for s in range(B):
        after(te, ch.pool[s], f"{name}.probs", i)
        for c in range(cols // P):
            for t in range(2):
                ins = te.transpose(ch.ps[s][:, c * 256 + t * P:c * 256 + (t + 1) * P],
                                   scores_of(ch, s, cols)[:, t, c * P:(c + 1) * P], e.ident[:])
        ins.then_inc(ch.te[s].sem, ch.te[s].one(f"{name}.turned"))
    for s in range(B):
        after(te, ch.act[s], f"{name}.kept", i)
        after(te, ch.dve[s], f"{name}.kept", i)
        for t in range(2):
            for c in range(cols // P):
                ins = te.matmul(ch.ps[s][:, t * C:(t + 1) * C], ch.pT[s][:, c, t * P:(t + 1) * P], vw[:, s, c, :],
                                start=c == 0, stop=c == cols // P - 1)
        ins.then_inc(ch.te[s].sem, ch.te[s].one(f"{name}.out"))


def scores_of(ch, s, cols):
    return ch.scores[s][:].rearrange("p t n -> p (t n)")[:, 0:2 * cols].rearrange("p (t n) -> p t n", t=2)


def cross_vector_steps(name, biased):
    return ([f"{name}.biased"] if biased else []) + [f"{name}.top", f"{name}.less", f"{name}.total", f"{name}.inverse",
                                                     f"{name}.kept"]


def cross_vector(dve, ch, name, i, cols, bias):
    heads = 2 * cols // S2
    sc = lambda s: scores_of(ch, s, cols)
    by_head = lambda ap: ap.rearrange("p t (h k) -> p t h k", k=S2)
    rep = lambda ap: ap.rearrange("p (t h) -> p t h", t=2).unsqueeze(3).to_broadcast([P, 2, heads // 2, S2])
    src = lambda s: ch.ps[s][:, 0:2 * cols].rearrange("p (t n) -> p t n", t=2)
    for s in range(B):
        after(dve, ch.te[s], f"{name}.scores", i)
        if bias is not None:
            dst = sc(s) if cols == 1024 else sc(s).rearrange("p t n -> p (t n)").rearrange("p (h k) -> p h k", k=S2)
            dve.tensor_tensor(out=dst, in0=src(s) if cols == 1024 else ch.ps[s][:, 0:2 * cols].rearrange(
                "p (h k) -> p h k", k=S2), in1=bias(s), op=ALU.add).then_inc(
                ch.dve[s].sem, ch.dve[s].one(f"{name}.biased"))
    for s in range(B):
        if bias is not None:
            after(dve, ch.dve[s], f"{name}.biased", i)
        dve.tensor_reduce(ch.top[s][:, 0:heads], by_head(sc(s) if bias is not None else src(s)), AX.X,
                          ALU.max).then_inc(ch.dve[s].sem, ch.dve[s].one(f"{name}.top"))
    for s in range(B):
        after(dve, ch.dve[s], f"{name}.top", i)
        dve.tensor_tensor(out=by_head(sc(s)), in0=by_head(sc(s) if bias is not None else src(s)),
                          in1=rep(ch.top[s][:, 0:heads]), op=ALU.subtract).then_inc(
            ch.dve[s].sem, ch.dve[s].one(f"{name}.less"))
    for s in range(B):
        after(dve, ch.act[s], f"{name}.exp", i)
        dve.tensor_reduce(ch.total[s][:, 0:heads], by_head(sc(s)), AX.X, ALU.add).then_inc(
            ch.dve[s].sem, ch.dve[s].one(f"{name}.total"))
    for s in range(B):
        after(dve, ch.dve[s], f"{name}.total", i)
        dve.reciprocal(ch.total[s][:, 0:heads], ch.total[s][:, 0:heads]).then_inc(
            ch.dve[s].sem, ch.dve[s].one(f"{name}.inverse"))
    for s in range(B):
        after(dve, ch.te[s], f"{name}.turned", i)
        half = cols
        dve.tensor_copy(ch.pT[s][:, cols // 256:cols // P, :].rearrange("p c n -> p (c n)"),
                        ch.ps[s][:, half:2 * half]).then_inc(ch.dve[s].sem, ch.dve[s].one(f"{name}.kept"))


def cross_scalar(act, ch, name, i, cols):
    for s in range(B):
        after(act, ch.dve[s], f"{name}.less", i)
        sc = scores_of(ch, s, cols)
        act.activation(sc, sc, ACT.Exp).then_inc(ch.act[s].sem, ch.act[s].one(f"{name}.exp"))
    for s in range(B):
        after(act, ch.te[s], f"{name}.turned", i)
        act.activation(ch.pT[s][:, 0:cols // 256, :].rearrange("p c n -> p (c n)"), ch.ps[s][:, 0:cols],
                       ACT.Identity).then_inc(ch.act[s].sem, ch.act[s].one(f"{name}.kept"))


def cross_gpsimd(pool, ch, name, i, cols):
    heads = 2 * cols // S2
    for s in range(B):
        after(pool, ch.dve[s], f"{name}.inverse", i)
        sc = scores_of(ch, s, cols).rearrange("p t (h k) -> p t h k", k=S2)
        inv = ch.total[s][:, 0:heads].rearrange("p (t h) -> p t h", t=2).unsqueeze(3).to_broadcast(
            [P, 2, heads // 2, S2])
        pool.tensor_tensor(out=sc, in0=sc, in1=inv, op=ALU.mult).then_inc(
            ch.pool[s].sem, ch.pool[s].one(f"{name}.probs"))


def add_vector(dve, ch, e, name, i, producer, bias, dst=None):
    for s in range(B):
        after(dve, ch.te[s], producer, i)
        x = tokens(e, s, i)
        dve.tensor_tensor(out=x, in0=ch.ps[s][:, 0:512].rearrange("p (t c) -> p t c", t=2), in1=x,
                          op=ALU.add).then_inc(ch.dve[s].sem, ch.dve[s].one(f"{name}.sum"))
    for s in range(B):
        after(dve, ch.dve[s], f"{name}.sum", i)
        x = tokens(e, s, i)
        dve.tensor_tensor(out=x, in0=x, in1=bias[:].unsqueeze(1).to_broadcast([P, 2, C]), op=ALU.add).then_inc(
            ch.dve[s].sem, ch.dve[s].one(f"{name}.x"))


def chain_loads0(nc, e, A, fb):
    rows = lambda n: A[n].rearrange("(k p) c -> p k c", p=P)
    w = e.w0 = Env()
    w.vec = {}
    w.m1, w.m1b, w.m2 = fb("mlp1_w", [P, KC, 1024]), fb("mlp1_b", [P, 8]), fb("mlp2_w", [P, 8, C])
    w.wu, w.wr, w.wn = (fb(n, [P, 4, C]) for n in ("w_u", "w_r", "w_n"))
    cols = {"ln2_g": "L0_xattn_ln2_w", "ln2_b": "L0_xattn_ln2_b", "ln3_g": "L0_xattn_ln3_w", "ln3_b": "L0_xattn_ln3_b",
            "st_g": "L1_xattn_g_state", "st_b": "L1_xattn_beta_state", "in_g": "L1_xattn_g_input",
            "in_b": "L1_xattn_beta_input", "r_b": "L1_xattn_b_r", "l2_g": "L2_xattn_ln1_g", "l2_b": "L2_xattn_ln1_b"}
    reps = {"out_b": "L0_xattn_out_b", "mlp2_b": "L0_xattn_mlp2_b", "u_b": "L1_xattn_b_u", "n_b": "L1_xattn_b_n",
            "o_g": "L1_xattn_g_out", "o_b": "L1_xattn_beta_out"}
    loads = [(w.m1[:], rows("L0_xattn_mlp1_w")), (w.m1b[:], column(A["L0_xattn_mlp1_b"], 8)),
             (w.m2[:], rows("L0_xattn_mlp2_w")), (w.wu[:], rows("L1_xattn_W_u")), (w.wr[:], rows("L1_xattn_W_r")),
             (w.wn[:], rows("L1_xattn_W_n"))]
    for n, src in cols.items():
        w.vec[n] = fb(f"c0_{n}", [P, KC])
        loads.append((w.vec[n][:], column(A[src], KC)))
    for n, src in reps.items():
        w.vec[n] = fb(f"r0_{n}", [P, C])
        loads.append((w.vec[n][:], A[src].partition_broadcast(P)))
    return loads


def part_chain0(nc, e):
    with ExitStack() as ctx:
        w = e.w0
        te_steps = ["n2.T", "ca.scores", "ca.turned", "ca.out", "n3.T", "mlp.up", "mlp.down", "n4.T", "rt.scores",
                    "rt.turned", "rt.routed", "n5.T", "gates", "cand", "n7.T"]
        dve_steps = (norm_steps("n2") + cross_vector_steps("ca", True) + ["ca.sum", "ca.x"] + norm_steps("n3")
                     + ["mlp.sum", "mlp.x"] + norm_steps("n4") + ["x.copy", "rt.top", "rt.minus", "rt.inverse", "rt.probs"]
                     + norm_steps("n5") + ["u.biased", "reset", "cand.biased", "cand.less", "cand.gated", "mixed"]
                     + norm_steps("n6") + ["out.gain", "out.x"] + norm_steps("n7"))
        act_steps = ["n2.log", "n2.rstd", "n2.hT", "ca.exp", "ca.kept", "n3.log", "n3.rstd", "n3.hT", "mlp.gelu",
                     "n4.log", "n4.rstd", "x.T", "n4.hT", "rt.exp", "rt.kept", "n5.log", "n5.rstd", "n5.hT",
                     "r", "u", "tanh", "n6.log", "n6.rstd", "n7.log", "n7.rstd", "n7.hT"]
        ch = Chain(nc, ctx, "c0", te_steps, dve_steps, act_steps, ["ca.probs"])
        stT, inT, rT = ch.sb("stT", [P, KC, 256]), ch.sb("inT", [P, KC, 256]), ch.sb("rT", [P, KC, 256])
        u, cand = ch.sb("u", [P, 2, C]), ch.sb("cand", [P, 2, C])
        rp, rpT = ch.sb("rp", [P, 2, P]), ch.sb("rpT", [S2, 256])
        top, total = ch.sb("rtop", [P, 2]), ch.sb("rtotal", [P, 2])
        up = ch.pT
        tiles = lambda s, bank: ch.ps[s][:, 512 * bank:512 * (bank + 1)].rearrange("p (t c) -> p t c", t=2)
        rep = lambda ap: ap[:].unsqueeze(1).to_broadcast([P, 2, C])
        block = ctx.enter_context(nc.Block())

        @block.tensor
        def _(te):
            with te.Fori(0, BLOCKS) as i:
                for s in range(B):
                    after(te, ch.dve[s], "n2.h", i)
                    turn_tensor(te, ch, e, ch.h[s], s, 0).then_inc(ch.te[s].sem, ch.te[s].one("n2.T"))
                cross_tensor(te, ch, e, "ca", i, ch.hT, "n2.hT", e.m0, e.vw0, 1024)
                for s in range(B):
                    after(te, ch.dve[s], "n3.h", i)
                    turn_tensor(te, ch, e, ch.h[s], s, 0).then_inc(ch.te[s].sem, ch.te[s].one("n3.T"))
                for s in range(B):
                    after(te, ch.act[s], "n3.hT", i)
                    for f in range(8):
                        for k in range(KC):
                            ins = te.matmul(ch.ps[s][:, 256 * f:256 * (f + 1)], w.m1[:, k, f * P:(f + 1) * P],
                                            ch.hT[s][:, k, :], start=k == 0, stop=k == KC - 1)
                    ins.then_inc(ch.te[s].sem, ch.te[s].one("mlp.up"))
                for s in range(B):
                    after(te, ch.act[s], "mlp.gelu", i)
                    for t in range(2):
                        for f in range(8):
                            ins = te.matmul(ch.ps[s][:, t * C:(t + 1) * C], up[s][:, f, t * P:(t + 1) * P],
                                            w.m2[:, f, :], start=f == 0, stop=f == 7)
                    ins.then_inc(ch.te[s].sem, ch.te[s].one("mlp.down"))
                for s in range(B):
                    after(te, ch.dve[s], "x.copy", i)
                    turn_tensor(te, ch, e, ch.xc[s], s, 0)
                    turn_tensor(te, ch, e, ch.h[s], s, 1).then_inc(ch.te[s].sem, ch.te[s].one("n4.T"))
                for s in range(B):
                    after(te, ch.act[s], "x.T", i)
                    for t in range(2):
                        for k in range(KC):
                            ins = te.matmul(ch.ps[s][:, 1024 + t * S2:1024 + (t + 1) * S2],
                                            ch.xT[s][:, k, t * P:(t + 1) * P], e.tokT[:, k, s * S2:(s + 1) * S2],
                                            start=k == 0, stop=k == KC - 1)
                    ins.then_inc(ch.te[s].sem, ch.te[s].one("rt.scores"))
                for s in range(B):
                    after(te, ch.dve[s], "rt.probs", i)
                    for t in range(2):
                        ins = te.transpose(ch.ps[s][:, 1024 + t * P:1024 + (t + 1) * P], rp[s][:, t, :], e.ident[:])
                    ins.then_inc(ch.te[s].sem, ch.te[s].one("rt.turned"))
                for s in range(B):
                    after(te, ch.act[s], "rt.kept", i)
                    for t in range(2):
                        ins = te.matmul(ch.ps[s][:, 1536 + t * C:1536 + (t + 1) * C], rpT[s][:, t * P:(t + 1) * P],
                                        e.tok[:, s, :], start=True, stop=True)
                    ins.then_inc(ch.te[s].sem, ch.te[s].one("rt.routed"))
                for s in range(B):
                    after(te, ch.dve[s], "n5.h", i)
                    turn_tensor(te, ch, e, ch.h[s], s, 0).then_inc(ch.te[s].sem, ch.te[s].one("n5.T"))
                for s in range(B):
                    after(te, ch.act[s], "n5.hT", i)
                    both = [(stT[s], 0), (stT[s], 1), (inT[s], 0), (inT[s], 1)]
                    for t in range(2):
                        for k, (src, c) in enumerate(both):
                            te.matmul(ch.ps[s][:, 512 + t * C:512 + (t + 1) * C], src[:, c, t * P:(t + 1) * P],
                                      w.wu[:, k, :], start=k == 0, stop=k == 3)
                    for f in range(KC):
                        for k, (src, c) in enumerate(both):
                            ins = te.matmul(ch.ps[s][:, 1024 + f * 256:1024 + (f + 1) * 256],
                                            w.wr[:, k, f * P:(f + 1) * P], src[:, c, :], start=k == 0, stop=k == 3)
                    ins.then_inc(ch.te[s].sem, ch.te[s].one("gates"))
                for s in range(B):
                    after(te, ch.dve[s], "reset", i)
                    for t in range(2):
                        for k, (src, c) in enumerate([(rT[s], 0), (rT[s], 1), (inT[s], 0), (inT[s], 1)]):
                            ins = te.matmul(ch.ps[s][:, 1536 + t * C:1536 + (t + 1) * C],
                                            src[:, c, t * P:(t + 1) * P], w.wn[:, k, :], start=k == 0, stop=k == 3)
                    ins.then_inc(ch.te[s].sem, ch.te[s].one("cand"))
                for s in range(B):
                    after(te, ch.dve[s], "n7.h", i)
                    turn_tensor(te, ch, e, ch.h[s], s, 0).then_inc(ch.te[s].sem, ch.te[s].one("n7.T"))
                for s in range(B):
                    after(te, ch.act[s], "n7.hT", i)

        @block.vector
        def _(dve):
            for s in range(B):
                dve.memset(rp[s][:, :, S2:P], 0.0)
            with dve.Fori(0, BLOCKS) as i:
                one = lambda s, name: (ch.dve[s].sem, ch.dve[s].one(name))
                x = lambda s: tokens(e, s, i)
                norm_vector(dve, ch, "n2", i, x)
                cross_vector(dve, ch, "ca", i, 1024, lambda s: e.bias0[:, s, :].unsqueeze(1).to_broadcast([P, 2, 1024]))
                add_vector(dve, ch, e, "ca", i, "ca.out", w.vec["out_b"])
                norm_vector(dve, ch, "n3", i, x, lambda s: after_spare(dve, ch, s, "ca.x", i))
                add_vector(dve, ch, e, "mlp", i, "mlp.down", w.vec["mlp2_b"])
                norm_vector(dve, ch, "n4", i, x, lambda s: after_spare(dve, ch, s, "mlp.x", i))
                for s in range(B):
                    dve.tensor_copy(ch.xc[s][:], x(s)).then_inc(*one(s, "x.copy"))
                for s in range(B):
                    after(dve, ch.te[s], "rt.scores", i)
                    dve.tensor_reduce(top[s][:], ch.ps[s][:, 1024:1024 + 2 * S2].rearrange("p (t k) -> p t k", t=2),
                                      AX.X, ALU.max).then_inc(*one(s, "rt.top"))
                for s in range(B):
                    after(dve, ch.dve[s], "rt.top", i)
                    dve.tensor_scalar(top[s][:], top[s][:], -1.0 / 16, None, ALU.mult).then_inc(*one(s, "rt.minus"))
                for s in range(B):
                    after(dve, ch.act[s], "rt.exp", i)
                    dve.reciprocal(total[s][:], total[s][:]).then_inc(*one(s, "rt.inverse"))
                for s in range(B):
                    after(dve, ch.dve[s], "rt.inverse", i)
                    dve.tensor_tensor(out=rp[s][:, :, 0:S2], in0=rp[s][:, :, 0:S2],
                                      in1=total[s][:].unsqueeze(2).to_broadcast([P, 2, S2]),
                                      op=ALU.mult).then_inc(*one(s, "rt.probs"))
                norm_vector(dve, ch, "n5", i, lambda s: tiles(s, 3), lambda s: after(dve, ch.te[s], "rt.routed", i))
                for s in range(B):
                    after(dve, ch.te[s], "gates", i)
                    dve.tensor_tensor(out=u[s][:], in0=tiles(s, 1), in1=rep(w.vec["u_b"]), op=ALU.add).then_inc(
                        *one(s, "u.biased"))
                for s in range(B):
                    after(dve, ch.act[s], "r", i)
                    dve.tensor_tensor(out=rT[s][:], in0=rT[s][:], in1=stT[s][:], op=ALU.mult).then_inc(
                        *one(s, "reset"))
                for s in range(B):
                    after(dve, ch.te[s], "cand", i)
                    dve.tensor_tensor(out=cand[s][:], in0=tiles(s, 3), in1=rep(w.vec["n_b"]), op=ALU.add).then_inc(
                        *one(s, "cand.biased"))
                for s in range(B):
                    after(dve, ch.act[s], "tanh", i)
                    dve.tensor_tensor(out=cand[s][:], in0=cand[s][:], in1=ch.xc[s][:], op=ALU.subtract).then_inc(
                        *one(s, "cand.less"))
                for s in range(B):
                    after(dve, ch.dve[s], "cand.less", i)
                    dve.tensor_tensor(out=cand[s][:], in0=cand[s][:], in1=u[s][:], op=ALU.mult).then_inc(
                        *one(s, "cand.gated"))
                for s in range(B):
                    after(dve, ch.dve[s], "cand.gated", i)
                    dve.tensor_tensor(out=ch.xc[s][:], in0=ch.xc[s][:], in1=cand[s][:], op=ALU.add).then_inc(
                        *one(s, "mixed"))
                norm_vector(dve, ch, "n6", i, lambda s: ch.xc[s][:], lambda s: after_spare(dve, ch, s, "mixed", i))
                for s in range(B):
                    after(dve, ch.dve[s], "n6.h", i)
                    dve.tensor_tensor(out=ch.h[s][:], in0=ch.h[s][:], in1=rep(w.vec["o_g"]), op=ALU.mult).then_inc(
                        *one(s, "out.gain"))
                for s in range(B):
                    after(dve, ch.dve[s], "out.gain", i)
                    dve.tensor_tensor(out=x(s), in0=ch.h[s][:], in1=rep(w.vec["o_b"]), op=ALU.add).then_inc(
                        *one(s, "out.x"))
                norm_vector(dve, ch, "n7", i, x, lambda s: after_spare(dve, ch, s, "out.x", i))
                for s in range(B):
                    after(dve, ch.te[s], "n7.T", i)

        @block.scalar
        def _(act):
            with act.Fori(0, BLOCKS) as i:
                one = lambda s, name: (ch.act[s].sem, ch.act[s].one(name))
                norm_scalar(act, ch, e, "n2", i)
                for s in range(B):
                    after(act, ch.te[s], "n2.T", i)
                    turned_scalar(act, ch, s, 0, ch.hT[s], w.vec["ln2_g"], w.vec["ln2_b"]).then_inc(*one(s, "n2.hT"))
                cross_scalar(act, ch, "ca", i, 1024)
                norm_scalar(act, ch, e, "n3", i)
                for s in range(B):
                    after(act, ch.te[s], "n3.T", i)
                    turned_scalar(act, ch, s, 0, ch.hT[s], w.vec["ln3_g"], w.vec["ln3_b"]).then_inc(*one(s, "n3.hT"))
                for s in range(B):
                    after(act, ch.te[s], "mlp.up", i)
                    for f in range(8):
                        ins = act.activation(up[s][:, f, :], ch.ps[s][:, 256 * f:256 * (f + 1)], ACT.Gelu,
                                             bias=w.m1b[:, f:f + 1])
                    ins.then_inc(*one(s, "mlp.gelu"))
                norm_scalar(act, ch, e, "n4", i)
                for s in range(B):
                    after(act, ch.te[s], "n4.T", i)
                    turned_scalar(act, ch, s, 0, ch.xT[s]).then_inc(*one(s, "x.T"))
                    turned_scalar(act, ch, s, 1, stT[s], w.vec["st_g"], w.vec["st_b"]).then_inc(*one(s, "n4.hT"))
                for s in range(B):
                    after(act, ch.dve[s], "rt.minus", i)
                    for t in range(2):
                        ins = act.activation(rp[s][:, t, 0:S2], ch.ps[s][:, 1024 + t * S2:1024 + (t + 1) * S2], ACT.Exp,
                                             scale=1.0 / 16, bias=top[s][:, t:t + 1], accum_out=total[s][:, t:t + 1])
                    ins.then_inc(*one(s, "rt.exp"))
                for s in range(B):
                    after(act, ch.te[s], "rt.turned", i)
                    act.activation(rpT[s][:], ch.ps[s][0:S2, 1024:1024 + 256], ACT.Identity).then_inc(
                        *one(s, "rt.kept"))
                norm_scalar(act, ch, e, "n5", i)
                for s in range(B):
                    after(act, ch.te[s], "n5.T", i)
                    turned_scalar(act, ch, s, 0, inT[s], w.vec["in_g"], w.vec["in_b"]).then_inc(*one(s, "n5.hT"))
                for s in range(B):
                    after(act, ch.te[s], "gates", i)
                    for f in range(KC):
                        ins = act.activation(rT[s][:, f, :], ch.ps[s][:, 1024 + f * 256:1024 + (f + 1) * 256],
                                             ACT.Sigmoid, bias=w.vec["r_b"][:, f:f + 1])
                    ins.then_inc(*one(s, "r"))
                for s in range(B):
                    after(act, ch.dve[s], "u.biased", i)
                    act.activation(u[s][:], u[s][:], ACT.Sigmoid).then_inc(*one(s, "u"))
                for s in range(B):
                    after(act, ch.dve[s], "cand.biased", i)
                    act.activation(cand[s][:], cand[s][:], ACT.Tanh).then_inc(*one(s, "tanh"))
                norm_scalar(act, ch, e, "n6", i)
                norm_scalar(act, ch, e, "n7", i)
                for s in range(B):
                    after(act, ch.te[s], "n7.T", i)
                    for c in range(KC):
                        dst = e.hT[:, c, s * T:(s + 1) * T].rearrange("p (i n) -> p i n", n=256)[:, ds(i, 1), :]
                        ins = act.activation(dst.rearrange("p o n -> p (o n)"), ch.ps[s][:, 256 * c:256 * (c + 1)],
                                             ACT.Identity, scale=w.vec["l2_g"][:, c:c + 1], bias=w.vec["l2_b"][:, c:c + 1])
                    ins.then_inc(*one(s, "n7.hT"))

        @block.gpsimd
        def _(pool):
            with pool.Fori(0, BLOCKS) as i:
                cross_gpsimd(pool, ch, "ca", i, 1024)


def part_attention2(nc, e, A, b):
    with ExitStack() as ctx:
        sb = lambda n, s, d=F32: ctx.enter_context(nc.sbuf_tensor(f"{n}_b{b}", s, d))
        sem = lambda n: ctx.enter_context(nc.semaphore(f"{n}_b{b}"))
        two = range(2)
        PAIRS, U, KEPT = 8, 16, 3
        w_c = [[sb(f"w{n}{i}", [P, KC, P]) for n in "qkv"] for i in two]
        qf, kf = sb("q_full", [P, T]), sb("k_full", [P, T])
        q_hl = [[sb(f"q_hl{j}{i}", [P, T], F32R) for j in two] for i in two]
        k_hh = [[sb(f"k_hh{j}{i}", [P, T], F32R) for j in two] for i in two]
        q_m = [[sb(f"q_m{j}{i}", [65, T], F32R) for j in two] for i in two]
        k_l = [[sb(f"k_l{j}{i}", [65, T], F32R) for j in two] for i in two]
        v = [sb(f"v{i}", [P, TB, P]) for i in two]
        probs = [[sb(f"pr{j}{i}", [P, T]) for i in range(KEPT)] for j in two]
        total = [sb(f"sum{j}", [P, T]) for j in two]
        rden = sb("rden2", [P, T])
        part_max, row_max = sb("pmax", [P, 2, 2, TB]), sb("rmax", [P, 2, TB])
        max_row = sb("maxr", [16, P], F32R)
        ring = ctx.enter_context(nc.psum_tensor(f"ring_b{b}", [P, T], F32))
        s2 = [ctx.enter_context(nc.psum_tensor(f"sc{i}_b{b}", [P, T], F32)) for i in two]
        o = ctx.enter_context(nc.psum_tensor(f"o_b{b}", [P, T], F32))
        w_in = [sem("w_in0"), sem("w_in1")]
        dup_in, max_out, max_in = [sem("dup_in0"), sem("dup_in1")], sem("max_out2"), sem("max_in2")
        rows_set = sem("rows_set2")
        proj_made, proj_kept, split = sem("proj_made"), sem("proj_kept"), sem("split")
        s1_made, s1_max, max_made, max_turned, max_kept = (
            sem(n) for n in ("s1m", "s1x", "max_made2", "max_turned2", "max_kept2"))
        s2_made, exp_made, pv_made = sem("s2m"), sem("expm"), sem("pvm")
        sum_a, sum_b = sem("sum_a"), sem("sum_b")
        den_made, log_made, rden_made, a_made = sem("denm"), sem("logm"), sem("rdenm"), sem("am")
        CH = [(j, t, half) for j in two for t in range(TB) for half in two]
        N1 = len(CH)
        hT = e.hT[:, :, b * T:(b + 1) * T]
        halves = [slice(0, 512), slice(512, T)]
        hi, lo = (slice(0, 64), slice(64, P)), (slice(64, P), slice(0, 64))
        running = lambda cur: cur is not None and not (isinstance(cur, int) and cur == 0)

        def pairs(engine, emit):
            emit(None, 0, 1, 1)
            emit(0, 1, 0, 1)
            with engine.Fori(0, 2) as i:
                emit(2 * i + 1, 2 * i + 2, 1, i + 2)
                emit(2 * i + 2, 2 * i + 3, 0, i + 2)
            emit(5, 6, 1, 4)
            emit(6, 7, 0, 4)
            emit(7, None, 1, None)

        block = ctx.enter_context(nc.Block())

        @block.sync
        def _(sp):
            def load(pair, par):
                for tile, n in zip(w_c[par], ("sa_wq", "sa_wk", "sa_wv")):
                    src = A["L2_xattn_" + n].rearrange("(k p) (g f) -> p k g f", p=P, f=P)[:, :, ds(pair, 1), :]
                    sp.dma_start(tile[:], src.rearrange("p k o f -> p k (o f)")).then_inc(w_in[par], 16)

            load(0, 0)

            def emit(cur, nxt, par, loads):
                if nxt is None:
                    return
                new = 1 - par
                if not (isinstance(nxt, int) and nxt == PAIRS - 1):
                    if running(nxt):
                        sp.wait_ge(proj_made, 3 * nxt)
                    load(nxt + 1, par)
                for j in two:
                    if running(cur) and j == 0:
                        sp.wait_ge(s2_made, U * cur)
                    sp.wait_ge(split, 8 * nxt + 1 + j)
                    sp.dma_start(q_m[new][j][0:64].bitcast(F32), q_hl[new][j][hi[j]].bitcast(F32)).then_inc(
                        dup_in[new], 16)
                for j in two:
                    sp.wait_ge(split, 8 * nxt + 3 + j)
                    sp.dma_start(k_hh[new][j][lo[j]].bitcast(F32), k_hh[new][j][hi[j]].bitcast(F32)).then_inc(
                        dup_in[new], 16)
                sp.wait_ge(max_kept, nxt + 1)
                sp.dma_start(e.max_dram[new, 0:16], max_row[:].bitcast(F32)).then_inc(max_out, 16)
                sp.wait_ge(max_out, 16 * (nxt + 1))
                for j in two:
                    sp.dma_start(q_m[new][j][64:65].bitcast(F32),
                                 e.max_dram[new, 8 * j:8 * j + 8].rearrange("(o t) q -> o (t q)", o=1)
                                 ).then_inc(max_in, 16)

            pairs(sp, emit)

        @block.tensor
        def _(te):
            te.wait_ge(rows_set, 1)

            def emit(cur, nxt, par, loads):
                new = 1 - par
                if nxt is not None:
                    te.wait_ge(w_in[new], 48 * loads)
                    if running(cur):
                        te.wait_ge(log_made, cur)
                    elif cur is not None:
                        te.wait_ge(max_kept, 1)
                    for n in range(2):
                        if n == 1:
                            te.wait_ge(proj_kept, 3 * nxt + 1)
                        for half in halves:
                            for k in range(KC):
                                ins = te.matmul(ring[:, half], w_c[new][n][:, k, :], hT[:, k, half], start=k == 0,
                                                stop=k == KC - 1)
                        ins.then_inc(proj_made, 1)
                    te.wait_ge(proj_kept, 3 * nxt + 2)
                    for t in range(TB):
                        for k in range(KC):
                            ins = te.matmul(ring[:, t * P:(t + 1) * P], hT[:, k, t * P:(t + 1) * P],
                                            w_c[new][2][:, k, :], start=k == 0, stop=k == KC - 1)
                    ins.then_inc(proj_made, 1)

                    def chunk(i):
                        j, t, half = CH[i]
                        if i < 2:
                            te.wait_ge(proj_kept, 3 * nxt + 3)
                        else:
                            te.wait_ge(s1_max, N1 * nxt + i - 1)
                        te.matmul(ring[:, halves[i % 2]], q_hl[new][j][:, t * P:(t + 1) * P],
                                  k_hh[new][j][:, halves[half]], start=True, stop=True).then_inc(s1_made, 1)

                def ready():
                    te.wait_ge(split, 8 * nxt + 8)
                    te.wait_ge(dup_in[new], 64 * loads)

                if cur is None:
                    ready()
                    for i in range(N1):
                        chunk(i)
                else:
                    def unit(u):
                        kt, j = divmod(u, 2)
                        keys = slice(kt * P, (kt + 1) * P)
                        if u >= 2 or running(cur):
                            te.wait_ge(exp_made, U * cur + u - 1 if u >= 2 else U * cur)
                        for half in halves:
                            te.matmul(s2[u % 2][:, half], k_hh[par][j][:, keys], q_hl[par][j][:, half],
                                      start=True, stop=False)
                            ins = te.matmul(s2[u % 2][:, half], k_l[par][j][:, keys], q_m[par][j][:, half],
                                            start=False, stop=True)
                        ins.then_inc(s2_made, 1)

                    def values(kt):
                        te.wait_ge(exp_made, U * cur + 2 * kt + 2)
                        if kt == 0 and running(cur):
                            te.wait_ge(a_made, cur)
                        for half in halves:
                            for j in two:
                                ins = te.matmul(o[64 * j:64 * j + 64, half], v[par][:, kt, 64 * j:64 * j + 64],
                                                probs[j][kt % KEPT][:, half], start=kt == 0, stop=kt == TB - 1)
                        ins.then_inc(pv_made, 1)

                    te.wait_ge(max_in, 32 * (cur + 1))
                    for u in range(U):
                        unit(u)
                        if u % 2 and u >= 3:
                            values(u // 2 - 1)
                        if nxt is not None:
                            if u == 0:
                                ready()
                            chunk(2 * u)
                            chunk(2 * u + 1)
                    values(TB - 1)
                if nxt is not None:
                    te.wait_ge(max_made, nxt + 1)
                    te.transpose(ring[0:16, 0:P], row_max[:].rearrange("p j t -> p (j t)"),
                                 e.ident[:]).then_inc(max_turned, 1)
                if cur is not None:
                    te.wait_ge(sum_a, 7 * (cur + 1))
                    te.wait_ge(sum_b, 7 * (cur + 1))
                    te.wait_ge(max_kept, nxt + 1 if nxt is not None else PAIRS)
                    for half in halves:
                        for j in two:
                            ins = te.matmul(ring[64 * j:64 * j + 64, half], e.ones[:], total[j][:, half],
                                            start=True, stop=True)
                    ins.then_inc(den_made, 1)

            pairs(te, emit)

        def sum_step(engine, j, done, cur, kt):
            engine.wait_ge(exp_made, U * cur + 2 * kt + 1 + j)
            if kt == 1:
                if running(cur):
                    engine.wait_ge(den_made, cur)
            else:
                engine.wait_ge(done, 7 * cur + kt - 1)
            other = probs[j][0] if kt == 1 else total[j]
            engine.tensor_tensor(out=total[j][:], in0=other[:], in1=probs[j][kt % KEPT][:],
                                 op=ALU.add).then_inc(done, 1)

        @block.gpsimd
        def _(pool):
            def emit(cur, nxt, par, loads):
                if cur is not None:
                    for kt in range(1, TB):
                        sum_step(pool, 0, sum_a, cur, kt)

            pairs(pool, emit)

        @block.vector
        def _(dve):
            for i in two:
                for j in two:
                    ins = dve.memset(k_l[i][j][64:65].bitcast(F32), 1.0)
            ins.then_inc(rows_set, 1)

            def emit(cur, nxt, par, loads):
                new = 1 - par
                if nxt is not None:
                    for n, (src, dst) in enumerate(((qf, q_hl), (kf, k_hh))):
                        dve.wait_ge(proj_kept, 3 * nxt + 1 + n)
                        for j in two:
                            dve.tensor_copy(dst[new][j][hi[j]], src[hi[j]]).then_inc(split, 1)
                    for n, (src, high, dst) in enumerate(((qf, q_hl, q_hl), (kf, k_hh, k_l))):
                        for j in two:
                            dve.wait_ge(split, 8 * nxt + 2 * n + j + 1)
                            rows = lo[j] if n == 0 else slice(0, 64)
                            dve.tensor_tensor(out=dst[new][j][rows], in0=src[hi[j]],
                                              in1=high[new][j][hi[j]].bitcast(F32), op=ALU.subtract
                                              ).then_inc(split, 1)

                def reduce(i):
                    j, t, half = CH[i]
                    dve.wait_ge(s1_made, N1 * nxt + i + 1)
                    dve.tensor_reduce(part_max[:, half, j, t:t + 1], ring[:, halves[i % 2]], AX.X,
                                      ALU.max).then_inc(s1_max, 1)

                for u in range(U):
                    if nxt is not None:
                        reduce(2 * u)
                        reduce(2 * u + 1)
                    if cur is not None and u % 2 and u >= 5:
                        sum_step(dve, 1, sum_b, cur, u // 2 - 1)
                if nxt is not None:
                    dve.wait_ge(s1_max, N1 * nxt + N1)
                    if cur is not None:
                        dve.wait_ge(max_turned, nxt)
                    dve.tensor_tensor(out=row_max[:], in0=part_max[:, 0], in1=part_max[:, 1],
                                      op=ALU.max).then_inc(max_made, 1)
                if cur is not None:
                    sum_step(dve, 1, sum_b, cur, TB - 1)
                    dve.wait_ge(rden_made, cur + 1)
                    dve.wait_ge(pv_made, TB * (cur + 1))
                    dve.tensor_tensor(out=e.aT2[:, ds(cur, 1), :].rearrange("p o t -> p (o t)"), in0=o[:],
                                      in1=rden[:], op=ALU.mult).then_inc(a_made, 1)

            pairs(dve, emit)

        @block.scalar
        def _(act):
            def emit(cur, nxt, par, loads):
                new = 1 - par
                if nxt is not None:
                    for n, (dst, scale) in enumerate(((qf, 0.125), (kf, 1.0))):
                        act.wait_ge(proj_made, 3 * nxt + 1 + n)
                        if cur is not None:
                            act.wait_ge(split, 8 * nxt - 2 + 2 * n)
                        act.activation(dst[:], ring[:], ACT.Identity, scale=scale).then_inc(proj_kept, 1)
                    act.wait_ge(proj_made, 3 * nxt + 3)
                    if running(cur):
                        act.wait_ge(pv_made, TB * cur)
                    act.activation(v[new][:].rearrange("p t f -> p (t f)"), ring[:],
                                   ACT.Identity).then_inc(proj_kept, 1)
                if cur is not None:
                    for u in range(U):
                        kt, j = divmod(u, 2)
                        act.wait_ge(s2_made, U * cur + u + 1)
                        if kt >= KEPT:
                            act.wait_ge(pv_made, TB * cur + kt - KEPT + 1)
                            act.wait_ge((sum_a, sum_b)[j], 7 * cur + max(kt - KEPT, 1))
                        elif running(cur):
                            act.wait_ge(pv_made, TB * cur)
                            act.wait_ge((sum_a, sum_b)[j], 7 * cur)
                        act.activation(probs[j][kt % KEPT][:], s2[u % 2][:], ACT.Exp).then_inc(exp_made, 1)
                if nxt is not None:
                    act.wait_ge(max_turned, nxt + 1)
                    if cur is not None:
                        act.wait_ge(max_out, 16 * nxt)
                    act.activation(max_row[:], ring[0:16, 0:P], ACT.Identity, scale=-1.0).then_inc(max_kept, 1)
                if cur is not None:
                    act.wait_ge(den_made, cur + 1)
                    if running(cur):
                        act.wait_ge(a_made, cur)
                    act.activation(rden[:], ring[:], ACT.Ln).then_inc(log_made, 1)
                    act.wait_ge(log_made, cur + 1)
                    act.activation(rden[:], rden[:], ACT.Exp, scale=-1.0).then_inc(rden_made, 1)

            pairs(act, emit)


def part_project2(nc, e, b):
    with ExitStack() as ctx:
        ps = [ctx.enter_context(nc.psum_tensor(f"wo{i}_b{b}", [P, 2, C], F32)) for i in range(4)]
        made, added = (ctx.enter_context(nc.semaphore(f"wo_{n}_b{b}")) for n in ("made", "added"))
        block = ctx.enter_context(nc.Block())

        @block.tensor
        def _(te):
            for u in range(TB // 2):
                for i in range(2):
                    t = 2 * u + i
                    for g in range(8):
                        ins = te.matmul(ps[u][:, i, :], e.aT2[:, g, t * P:(t + 1) * P], e.wo_w[:, g, :],
                                        start=g == 0, stop=g == 7)
                ins.then_inc(made, 1)

        @block.vector
        def _(dve):
            x = e.x[:, b * TB:(b + 1) * TB, :]
            dve.tensor_tensor(out=x, in0=x, in1=e.wo_brep[:].unsqueeze(1).to_broadcast([P, TB, C]),
                              op=ALU.add).then_inc(added, 1)
            dve.wait_ge(added, 1)
            for u in range(TB // 2):
                dve.wait_ge(made, u + 1)
                tile = x[:, 2 * u:2 * u + 2, :]
                dve.tensor_tensor(out=tile, in0=ps[u][:], in1=tile, op=ALU.add).then_inc(added, 1)


def part_context2(nc, e, A, later):
    with ExitStack() as ctx:
        sb = lambda n, s, d=F32: ctx.enter_context(nc.sbuf_tensor(n, s, d))
        sem = lambda n: ctx.enter_context(nc.semaphore(n))
        F3 = 16
        mask3 = sb("mask3", [P, B, S2], mybir.dt.int32)
        head64 = sb("head64", [P, 2])
        wq = [sb(f"wq{i}", [P, KC, 1024]) for i in range(2)]
        wk, wv = ([sb(f"w{n}_{i}", [96, 2, 1024]) for i in range(2)] for n in "kv")
        wo = [sb(f"wo{i}", [P, 8, C]) for i in range(2)]
        wqT = sb("wqT", [P, 8, C])
        kT, vT = sb("kT2", [P, 8, P]), sb("vT2", [P, 8, P])
        kbd, vbd = sb("kbd2", [P, B, 8, 2, S2]), sb("vbd2", [P, B, 8, 2, S2])
        ps = [ctx.enter_context(nc.psum_tensor(f"ctx{i}", [P, 512], F32)) for i in range(8)]
        w_in = [sem(f"w2_in{i}") for i in range(3)]
        later_in, mask_in = sem("chain2_w_in"), sem("mask3_in")
        names = []
        for g in range(3):
            names += [f"{g}.wqT{i}" for i in range(4)] + [f"{g}.kT{i}" for i in range(2)] + [f"{g}.vT{i}" for i in range(2)]
            if g == 0:
                names += [f"{g}.m{b}{d}{h}" for b in range(B) for d in range(KC) for h in range(2)]
                names += [f"{g}.vw{b}{i}" for b in range(B) for i in range(4)]
            else:
                names += [f"{g}.m{d}" for d in range(KC)] + [f"{g}.vw{b}" for b in range(B)]
        pe, ev = Steps(sem("ctx2_tensor"), names), Steps(sem("ctx2_scalar"), names)
        dv = Steps(sem("ctx2_vector"), ["mask", "kbd", "vbd"])
        gp = Steps(sem("ctx2_gpsimd"), ["ones", "first", "second"])
        bank = lambda n: ps[names.index(n) % 8]
        block = ctx.enter_context(nc.Block())

        @block.sync
        def _(sp):
            sp.dma_start(mask3[:], A["mask_BxS2_if1"].rearrange("b s -> (b s)").partition_broadcast(P)
                         .rearrange("p (b s) -> p b s", b=B)).then_inc(mask_in, 16)
            for g in range(3):
                if g == 2:
                    sp.wait_ge(ev.sem, ev.value("0.vw13"))
                names4 = (("L2_xattn_ca_wq", "L2_xattn_ca_wk", "L2_xattn_ca_wv", "L2_xattn_ca_wo") if g == 0 else
                          ("L3_xattn_Wq", "L3_xattn_Wk", "L3_xattn_Wv", "L3_xattn_Wo"))
                c0 = 1024 * max(g - 1, 0)
                for tile, n, p in ((wq, names4[0], P), (wk, names4[1], 96), (wv, names4[2], 96)):
                    sp.dma_start(tile[g % 2][:], A[n].rearrange("(k p) c -> p k c", p=p)[:, :, c0:c0 + 1024]
                                 ).then_inc(w_in[g], 16)
                sp.dma_start(wo[g % 2][:], A[names4[3]][c0:c0 + 1024, :].rearrange("(k p) c -> p k c", p=P)
                             ).then_inc(w_in[g], 16)
            for dst, src in later:
                sp.dma_start(dst, src).then_inc(later_in, 16)
            sp.wait_ge(later_in, 16 * len(later))

        @block.gpsimd
        def _(pool):
            pool.memset(head64[:], 1.0).then_inc(gp.sem, gp.one("ones"))
            pool.wait_ge(gp.sem, gp.value("ones"))
            pool.affine_select(out=head64[:], in_=head64[:], compare_op=ALU.is_ge, fill=0.0, base=0,
                               pattern=[[-64, 2]], channel_multiplier=1).then_inc(gp.sem, gp.one("first"))
            pool.wait_ge(gp.sem, gp.value("first"))
            pool.affine_select(out=head64[:], in_=head64[:], compare_op=ALU.is_ge, fill=0.0, base=63,
                               pattern=[[64, 2]], channel_multiplier=-1).then_inc(gp.sem, gp.one("second"))

        @block.vector
        def _(dve):
            dve.wait_ge(mask_in, 16)
            dve.tensor_scalar(e.bias3[:], mask3[:], 0.0, MASKED, ALU.is_equal, ALU.mult).then_inc(
                dv.sem, dv.one("mask"))
            dve.wait_ge(gp.sem, gp.value("second"))
            head_rep = head64[:].unsqueeze(2).to_broadcast([P, 2, S2])
            for name, dst, src in (("kbd", kbd, kT), ("vbd", vbd, vT)):
                dve.wait_ge(ev.sem, ev.value("0." + name[0] + "T1"))
                for b in range(B):
                    for c in range(8):
                        rep = src[:, c, b * S2:(b + 1) * S2].unsqueeze(1).to_broadcast([P, 2, S2])
                        ins = dve.tensor_tensor(out=dst[:, b, c], in0=rep, in1=head_rep, op=ALU.mult)
                ins.then_inc(dv.sem, dv.one(name))

        @block.scalar
        def _(act):
            def copy(name, dst, src, scale=1.0):
                act.wait_ge(pe.sem, pe.value(name))
                act.activation(dst, src, ACT.Identity, scale=scale).then_inc(ev.sem, ev.one(name))

            for g in range(3):
                if g == 1:
                    act.wait_ge(dv.sem, dv.value("vbd"))
                for i in range(4):
                    copy(f"{g}.wqT{i}", wqT[:, 2 * i:2 * i + 2, :], bank(f"{g}.wqT{i}")[:].rearrange(
                        "p (k c) -> p k c", k=2))
                for n, dst in (("k", kT), ("v", vT)):
                    for i in range(2):
                        copy(f"{g}.{n}T{i}", dst[:, 4 * i:4 * i + 4, :].rearrange("p k c -> p (k c)"),
                             bank(f"{g}.{n}T{i}")[:])
                if g == 0:
                    for b in range(B):
                        for d in range(KC):
                            for h in range(2):
                                copy(f"0.m{b}{d}{h}", e.m2[:, b, d, h * 512:(h + 1) * 512], bank(f"0.m{b}{d}{h}")[:],
                                     0.125)
                    for b in range(B):
                        for i in range(4):
                            copy(f"0.vw{b}{i}", e.vw2[:, b, 2 * i:2 * i + 2, :],
                                 bank(f"0.vw{b}{i}")[:].rearrange("p (k c) -> p k c", k=2))
                else:
                    heads = slice((g - 1) * 256, g * 256)
                    for d in range(KC):
                        n = f"{g}.m{d}"
                        act.wait_ge(pe.sem, pe.value(n))
                        for b in range(B):
                            src = bank(n)[:].rearrange("p (h b s) -> p b h s", b=B, s=S2)[:, b]
                            ins = act.activation(e.m3[:, b, d, heads].rearrange("p (h s) -> p h s", s=S2), src,
                                                 ACT.Identity, scale=0.0625)
                        ins.then_inc(ev.sem, ev.one(n))
                    for b in range(B):
                        copy(f"{g}.vw{b}", e.vw3[:, b, 2 * (g - 1):2 * g, :],
                             bank(f"{g}.vw{b}")[:].rearrange("p (k c) -> p k c", k=2))

        @block.tensor
        def _(te):
            def made(name, ins):
                ins.then_inc(pe.sem, pe.one(name))

            def free(name):
                if names.index(name) >= 8:
                    te.wait_ge(ev.sem, names.index(name) - 7)

            for g in range(3):
                te.wait_ge(w_in[g], 64)
                for i in range(4):
                    n = f"{g}.wqT{i}"
                    free(n)
                    for c in range(2):
                        for d in range(KC):
                            ins = te.transpose(bank(n)[:, (2 * c + d) * P:(2 * c + d + 1) * P],
                                               wq[g % 2][:, d, (2 * i + c) * P:(2 * i + c + 1) * P], e.ident[:])
                    ins.then_inc(pe.sem, pe.one(n))
                for letter, w in (("k", wk), ("v", wv)):
                    for i in range(2):
                        n = f"{g}.{letter}T{i}"
                        free(n)
                        for c in range(4):
                            for k in range(2):
                                ins = te.matmul(bank(n)[:, c * P:(c + 1) * P],
                                                w[g % 2][:, k, (4 * i + c) * P:(4 * i + c + 1) * P], e.ctxT[:, k, :],
                                                start=k == 0, stop=k == 1)
                        ins.then_inc(pe.sem, pe.one(n))
                if g == 0:
                    te.wait_ge(dv.sem, dv.value("vbd"))
                    for b in range(B):
                        for d in range(KC):
                            for h in range(2):
                                n = f"0.m{b}{d}{h}"
                                free(n)
                                for c in range(4):
                                    ins = te.matmul(bank(n)[:, c * P:(c + 1) * P], wqT[:, 4 * h + c, d * P:(d + 1) * P],
                                                    kbd[:, b, 4 * h + c].rearrange("p h s -> p (h s)"),
                                                    start=True, stop=True)
                                ins.then_inc(pe.sem, pe.one(n))
                    for b in range(B):
                        for i in range(4):
                            n = f"0.vw{b}{i}"
                            free(n)
                            for c in range(2):
                                ins = te.matmul(bank(n)[:, c * C:(c + 1) * C],
                                                vbd[:, b, 2 * i + c].rearrange("p h s -> p (h s)"),
                                                wo[0][:, 2 * i + c, :], start=True, stop=True)
                            ins.then_inc(pe.sem, pe.one(n))
                else:
                    te.wait_ge(ev.sem, ev.value(f"{g}.vT1"))
                    for d in range(KC):
                        n = f"{g}.m{d}"
                        free(n)
                        for h in range(4):
                            for c in range(2):
                                ins = te.matmul(bank(n)[:, h * P:(h + 1) * P], wqT[:, 2 * h + c, d * P:(d + 1) * P],
                                                kT[:, 2 * h + c, :], start=c == 0, stop=c == 1)
                        ins.then_inc(pe.sem, pe.one(n))
                    for b in range(B):
                        n = f"{g}.vw{b}"
                        free(n)
                        for h in range(4):
                            for c in range(2):
                                ins = te.matmul(bank(n)[64 * (h % 2):64 * (h % 2) + 64, (h // 2) * C:(h // 2 + 1) * C],
                                                vT[:, 2 * h + c, b * S2:(b + 1) * S2], wo[g % 2][:, 2 * h + c, :],
                                                start=c == 0, stop=c == 1)
                        ins.then_inc(pe.sem, pe.one(n))


def chain_loads2(nc, e, A, bb):
    rows = lambda n: A[n].rearrange("(k p) c -> p k c", p=P)
    w = e.w2 = Env()
    w.vec = {}
    w.f1, w.f1b, w.f2 = bb("ff1_w", [P, KC, 2048]), bb("ff1_b", [P, 16]), bb("ff2_w", [P, 8, C])
    loads = [(w.f1[:], rows("L2_xattn_ff_w1")), (w.f1b[:], column(A["L2_xattn_ff_b1"], 16)),
             (w.f2[:], rows("L2_xattn_ff_w2"))]
    for n, src in {"ln2_g": "L2_xattn_ln2_g", "ln2_b": "L2_xattn_ln2_b", "ln3_g": "L2_xattn_ln3_g",
                   "ln3_b": "L2_xattn_ln3_b"}.items():
        w.vec[n] = bb(f"c2_{n}", [P, KC])
        loads.append((w.vec[n][:], column(A[src], KC)))
    for n, src in {"ca_b": "L2_xattn_ca_bo", "ff2_b": "L2_xattn_ff_b2", "gamma": "L3_xattn_gamma",
                   "beta": "L3_xattn_beta"}.items():
        w.vec[n] = bb(f"r2_{n}", [P, C])
        loads.append((w.vec[n][:], A[src].partition_broadcast(P)))
    return loads


def part_chain2(nc, e, out):
    with ExitStack() as ctx:
        w = e.w2
        te_steps = ["n8.T", "cb.scores", "cb.turned", "cb.out", "n9.T", "ff.up0", "ff.up1", "ff.down", "x.T",
                    "cc.scores", "cc.turned", "cc.out"]
        dve_steps = (norm_steps("n8") + cross_vector_steps("cb", False) + ["cb.sum", "cb.x"] + norm_steps("n9")
                     + ["ff.gated0", "ff.gated1", "ff.sum", "ff.x", "x.copy"] + cross_vector_steps("cc", True)
                     + ["x.last"] + norm_steps("n10") + ["out.gain", "out"])
        act_steps = ["n8.log", "n8.rstd", "n8.hT", "cb.exp", "cb.kept", "n9.log", "n9.rstd", "n9.hT", "ff.gelu0",
                     "ff.gelu1", "x.T", "cc.exp", "cc.kept", "n10.log", "n10.rstd"]
        ch = Chain(nc, ctx, "c2", te_steps, dve_steps, act_steps, ["cb.probs", "cc.probs"])
        gate, inner = ch.sb("gate", [P, 4, 256]), ch.pT
        result = ch.sb("result", [P, 2, C])
        stored = [ctx.enter_context(nc.semaphore(f"out_stored{s}")) for s in range(B)]
        tiles = lambda s, bank: ch.ps[s][:, 512 * bank:512 * (bank + 1)].rearrange("p (t c) -> p t c", t=2)
        rep = lambda ap: ap[:].unsqueeze(1).to_broadcast([P, 2, C])
        block = ctx.enter_context(nc.Block())

        @block.sync
        def _(sp):
            with sp.Fori(0, BLOCKS) as i:
                for s in range(B):
                    after(sp, ch.dve[s], "out", i)
                    dst = out[s].rearrange("(i t p) c -> p i t c", p=P, t=2)[:, ds(i, 1)]
                    sp.dma_start(dst.rearrange("p o t c -> p (o t) c"), result[s][:]).then_inc(stored[s], 16)
            for s in range(B):
                sp.wait_ge(stored[s], 16 * BLOCKS)

        @block.tensor
        def _(te):
            with te.Fori(0, BLOCKS) as i:
                for s in range(B):
                    after(te, ch.dve[s], "n8.h", i)
                    turn_tensor(te, ch, e, ch.h[s], s, 0).then_inc(ch.te[s].sem, ch.te[s].one("n8.T"))
                cross_tensor(te, ch, e, "cb", i, ch.hT, "n8.hT", e.m2, e.vw2, 1024)
                for s in range(B):
                    after(te, ch.dve[s], "n9.h", i)
                    turn_tensor(te, ch, e, ch.h[s], s, 0).then_inc(ch.te[s].sem, ch.te[s].one("n9.T"))
                for half in range(2):
                    for s in range(B):
                        if half == 0:
                            after(te, ch.act[s], "n9.hT", i)
                        else:
                            after(te, ch.dve[s], "ff.gated0", i)
                        for part in range(2):
                            for f in range(4):
                                chunk = 8 * part + 4 * half + f
                                for k in range(KC):
                                    ins = te.matmul(ch.ps[s][:, 1024 * part + 256 * f:1024 * part + 256 * (f + 1)],
                                                    w.f1[:, k, chunk * P:(chunk + 1) * P], ch.hT[s][:, k, :],
                                                    start=k == 0, stop=k == KC - 1)
                        ins.then_inc(ch.te[s].sem, ch.te[s].one(f"ff.up{half}"))
                for s in range(B):
                    after(te, ch.dve[s], "ff.gated1", i)
                    for t in range(2):
                        for f in range(8):
                            ins = te.matmul(ch.ps[s][:, t * C:(t + 1) * C], inner[s][:, f, t * P:(t + 1) * P],
                                            w.f2[:, f, :], start=f == 0, stop=f == 7)
                    ins.then_inc(ch.te[s].sem, ch.te[s].one("ff.down"))
                for s in range(B):
                    after(te, ch.dve[s], "x.copy", i)
                    turn_tensor(te, ch, e, ch.xc[s], s, 0).then_inc(ch.te[s].sem, ch.te[s].one("x.T"))
                cross_tensor(te, ch, e, "cc", i, ch.xT, "x.T", e.m3, e.vw3, 512)
                for s in range(B):
                    after(te, ch.dve[s], "x.last", i)

        @block.vector
        def _(dve):
            with dve.Fori(0, BLOCKS) as i:
                one = lambda s, name: (ch.dve[s].sem, ch.dve[s].one(name))
                x = lambda s: tokens(e, s, i)
                norm_vector(dve, ch, "n8", i, x)
                cross_vector(dve, ch, "cb", i, 1024, None)
                add_vector(dve, ch, e, "cb", i, "cb.out", w.vec["ca_b"])
                norm_vector(dve, ch, "n9", i, x, lambda s: after_spare(dve, ch, s, "cb.x", i))
                for half in range(2):
                    for s in range(B):
                        after(dve, ch.act[s], f"ff.gelu{half}", i)
                        for f in range(4):
                            chunk = 4 * half + f
                            ins = dve.scalar_tensor_tensor(
                                out=inner[s][:, chunk, :], in0=ch.ps[s][:, 256 * f:256 * (f + 1)],
                                scalar=w.f1b[:, chunk:chunk + 1], in1=gate[s][:, f, :], op0=ALU.add, op1=ALU.mult)
                        ins.then_inc(*one(s, f"ff.gated{half}"))
                add_vector(dve, ch, e, "ff", i, "ff.down", w.vec["ff2_b"])
                for s in range(B):
                    after_spare(dve, ch, s, "ff.x", i)
                    dve.tensor_copy(ch.xc[s][:], x(s)).then_inc(*one(s, "x.copy"))
                cross_vector(dve, ch, "cc", i, 512,
                             lambda s: e.bias3[:, s, :].unsqueeze(1).to_broadcast([P, 16, S2]))
                for s in range(B):
                    after(dve, ch.te[s], "cc.out", i)
                    dve.tensor_tensor(out=ch.xc[s][:], in0=tiles(s, 0), in1=ch.xc[s][:], op=ALU.add).then_inc(
                        *one(s, "x.last"))
                norm_vector(dve, ch, "n10", i, lambda s: ch.xc[s][:], lambda s: after_spare(dve, ch, s, "x.last", i))
                for s in range(B):
                    after(dve, ch.dve[s], "n10.h", i)
                    dve.tensor_tensor(out=ch.h[s][:], in0=ch.h[s][:], in1=rep(w.vec["gamma"]), op=ALU.mult).then_inc(
                        *one(s, "out.gain"))
                for s in range(B):
                    after(dve, ch.dve[s], "out.gain", i)
                    dve.tensor_tensor(out=result[s][:], in0=ch.h[s][:], in1=rep(w.vec["beta"]), op=ALU.add).then_inc(
                        *one(s, "out"))
                for s in range(B):
                    dve.wait_ge(stored[s], 16 * i + 16)

        @block.scalar
        def _(act):
            with act.Fori(0, BLOCKS) as i:
                one = lambda s, name: (ch.act[s].sem, ch.act[s].one(name))
                norm_scalar(act, ch, e, "n8", i)
                for s in range(B):
                    after(act, ch.te[s], "n8.T", i)
                    turned_scalar(act, ch, s, 0, ch.hT[s], w.vec["ln2_g"], w.vec["ln2_b"]).then_inc(*one(s, "n8.hT"))
                cross_scalar(act, ch, "cb", i, 1024)
                norm_scalar(act, ch, e, "n9", i)
                for s in range(B):
                    after(act, ch.te[s], "n9.T", i)
                    turned_scalar(act, ch, s, 0, ch.hT[s], w.vec["ln3_g"], w.vec["ln3_b"]).then_inc(*one(s, "n9.hT"))
                for half in range(2):
                    for s in range(B):
                        after(act, ch.te[s], f"ff.up{half}", i)
                        for f in range(4):
                            ins = act.activation(gate[s][:, f, :], ch.ps[s][:, 1024 + 256 * f:1024 + 256 * (f + 1)],
                                                 ACT.Gelu, bias=w.f1b[:, 8 + 4 * half + f:9 + 4 * half + f])
                        ins.then_inc(*one(s, f"ff.gelu{half}"))
                for s in range(B):
                    after(act, ch.te[s], "x.T", i)
                    turned_scalar(act, ch, s, 0, ch.xT[s]).then_inc(*one(s, "x.T"))
                cross_scalar(act, ch, "cc", i, 512)
                norm_scalar(act, ch, e, "n10", i)

        @block.gpsimd
        def _(pool):
            with pool.Fori(0, BLOCKS) as i:
                cross_gpsimd(pool, ch, "cb", i, 1024)
                cross_gpsimd(pool, ch, "cc", i, 512)


def program(nc, A, out):
    with ExitStack() as ctx:
        ctx.enter_context(nc.allow_non_contiguous_dma(reason="vectors are loaded as columns"))
        e = Env()
        sb = lambda n, s, d=F32: ctx.enter_context(nc.sbuf_tensor(n, s, d))
        e.x = sb("x", [P, TILES, C])
        e.ident, e.ident_bf = sb("ident", [P, P]), sb("ident_bf", [P, P], BF16)
        e.eps = sb("eps", [P, 1])
        e.ones = sb("ones", [P, 64])
        e.tok, e.tokT = sb("tok", [S2, B, C]), sb("tokT", [P, KC, P])
        e.ctxT = sb("ctxT", [96, 2, P])
        attn = ctx.enter_context(ExitStack())
        ab = lambda n, s, d=F32: attn.enter_context(nc.sbuf_tensor(n, s, d))
        e.proj_w, e.proj_brep = ab("proj_w", [P, 4, C]), ab("proj_brep", [P, C])
        e.sel, e.tri, e.tri_bf = ab("sel", [P, P]), ab("tri", [P, P]), ab("tri_bf", [P, P], BF16)
        e.v_all = ab("v_all", [P, B, 4, TB, 64])
        qkv = attn.enter_context(ExitStack())
        qb = lambda n, s, d=F32: qkv.enter_context(nc.sbuf_tensor(n, s, d))
        e.hT = qb("hT", [P, KC, B * T])
        e.qkv_w, e.qkv_b, e.qkv_bs, e.v0_brep = (qb("qkv_w", [P, KC, 3 * C]), qb("qkv_b", [P, 4]),
                                                 qb("qkv_bs", [P, 4]), qb("v0_brep", [P, C]))
        e.mask_dram = nc.dram_tensor("mask_dram", [8, T], F32).ap()
        e.qk_dram = nc.dram_tensor("qk_dram", [2, 8, 2, 64, T], F32).ap()
        e.max_dram = nc.dram_tensor("max_dram", [2, 32, P], F32).ap()

        part_prologue(nc, e, A)
        part_qkv0(nc, e)
        qkv.close()
        e.aT0 = ab("aT0", [P, 8, T])
        part_attention0(nc, e)
        part_project0(nc, e)
        attn.close()
        turned = ctx.enter_context(ExitStack())
        e.hT = turned.enter_context(nc.sbuf_tensor("hT_2", [P, KC, B * T], F32))
        front = ctx.enter_context(ExitStack())
        fb = lambda n, s, d=F32: front.enter_context(nc.sbuf_tensor(n, s, d))
        e.m0, e.bias0, e.vw0 = fb("m0", [P, B, KC, 1024]), fb("bias0", [P, B, 1024]), fb("vw0", [P, B, 8, C])
        later = chain_loads0(nc, e, A, fb)
        part_context0(nc, e, A, later)
        part_chain0(nc, e)
        front.close()
        back = ctx.enter_context(ExitStack())
        bb = lambda n, s, d=F32: back.enter_context(nc.sbuf_tensor(n, s, d))
        e.aT2, e.wo_w, e.wo_brep = bb("aT2", [P, 8, T]), bb("wo_w", [P, 8, C]), bb("wo_brep", [P, C])
        part_load(nc, [(e.wo_w[:], A["L2_xattn_sa_wo"].rearrange("(k p) c -> p k c", p=P)),
                       (e.wo_brep[:], A["L2_xattn_sa_bo"].partition_broadcast(P))])
        for b in range(B):
            part_attention2(nc, e, A, b)
            part_project2(nc, e, b)
        back.close()
        turned.close()
        bb = sb
        e.m2, e.vw2 = bb("m2", [P, B, KC, 1024]), bb("vw2", [P, B, 8, C])
        e.m3, e.vw3, e.bias3 = bb("m3", [P, B, KC, 512]), bb("vw3", [P, B, 4, C]), bb("bias3", [P, B, S2])
        later = chain_loads2(nc, e, A, bb)
        part_context2(nc, e, A, later)
        part_chain2(nc, e, out)


def kernel(**inputs):
    import numpy as _np
    import concourse.bacc as _bacc
    from concourse import mybir as _mybir
    from concourse.bass_utils import run_bass_kernel_spmd as _run

    nc = _bacc.Bacc("TRN2", target_bir_lowering=False, num_devices=1)
    arrays, args = {}, {}
    for name in inputs:
        a = _np.ascontiguousarray(inputs[name])
        arrays[f"in_{name}"] = a
        args[name] = nc.dram_tensor(f"in_{name}", a.shape, _mybir.dt.from_np(a.dtype), kind="ExternalInput").ap()
    out = nc.dram_tensor("out", (B, T, C), F32, kind="ExternalOutput").ap()
    program(nc, args, out)
    r = _run(nc, [arrays], core_ids=[0])
    return r.results[0]["out"]
```

```python
import numpy as np
import concourse.bass as bass
from concourse import mybir
from contextlib import ExitStack

ALU = mybir.AluOpType
ACT = mybir.ActivationFunctionType
AX = mybir.AxisListType
F32 = mybir.dt.float32
F32R = mybir.dt.float32r
BF16 = mybir.dt.bfloat16
ds = bass.ds

P = 128
B, T, C = 2, 1024, 256
S2, CC = 64, 192
KC = C // P
TILES = B * T // P
TB = T // P
EPS = 1e-5
MASKED = -1e30


class Steps:

    def __init__(self, sem, names):
        self.sem, self.names, self.next = sem, names, 0
        assert len(set(names)) == len(names)

    def value(self, name, turn=0):
        return turn * len(self.names) + (self.names.index(name) + 1)

    def one(self, name):
        assert self.names[self.next % len(self.names)] == name, (name, self.names[self.next % len(self.names)])
        self.next += 1
        return 1


def part_load(nc, loads):
    with nc.semaphore("loaded") as loaded, nc.Block() as block:
        @block.sync
        def _(sp):
            for dst, src in loads:
                sp.dma_start(dst, src).then_inc(loaded, 16)
            sp.wait_ge(loaded, 16 * len(loads))


class Env:
    pass


def column(ap, n):
    return ap.rearrange("(c p) -> p c", p=P)


def part_prologue(nc, e, A):
    with ExitStack() as ctx:
        sb = lambda n, s, d=F32: ctx.enter_context(nc.sbuf_tensor(n, s, d))
        sem = lambda n: ctx.enter_context(nc.semaphore(n))
        ln1_g, ln1_b = sb("ln1_g", [P, KC]), sb("ln1_b", [P, KC])
        mask_row = sb("mask_row", [B, T], mybir.dt.uint8)
        mask_f = sb("mask_f", [B, T])
        stats = sb("stats", [P, TILES, 6])
        moments = sb("moments", [P, TILES, 2])
        rstd = sb("rstd", [P, TILES])
        h = sb("h", [P, TILES, C])
        ps = [ctx.enter_context(nc.psum_tensor(f"pre{i}", [P, 512], F32)) for i in range(8)]
        x_in, w_in, p_in, m_out = (sem(n) for n in ("x_in", "w_in", "p_in", "m_out"))
        order = [f"hT{i}" for i in range(8)]
        pe = Steps(sem("pre_pe"), order)
        ev = Steps(sem("pre_evac"), order)
        dv = Steps(sem("pre_dve"), ["maskf", "consts", "stats", "moments"] + [f"h{i}" for i in range(8)])
        ln = Steps(sem("pre_ln"), ["logvar", "rstd"])
        gp = Steps(sem("pre_pool"), ["zeros", "ident", "fills", "selects"])
        N_LOADS = 7
        block = ctx.enter_context(nc.Block())

        @block.sync
        def _(sp):
            sp.dma_start(e.x[:], A["x"].rearrange("b (t p) c -> p (b t) c", p=P)).then_inc(x_in, 16)
            rows = lambda n: A[n].rearrange("(k p) c -> p k c", p=P)
            loads = [
                (ln1_g[:], column(A["L0_xattn_ln1_w"], KC)), (ln1_b[:], column(A["L0_xattn_ln1_b"], KC)),
                (mask_row[:], A["mask_BxS_bf0"]),
                (e.qkv_w[:], rows("L0_xattn_qkv_w")),
                (e.qkv_b[:], column(A["L0_xattn_qkv_b"][0:2 * C], 2 * KC)),
                (e.v0_brep[:], A["L0_xattn_qkv_b"][2 * C:3 * C].partition_broadcast(P)),
                (e.proj_brep[:], A["L0_xattn_proj_b"].partition_broadcast(P)),
            ]
            assert len(loads) == N_LOADS
            for dst, src in loads:
                sp.dma_start(dst, src).then_inc(w_in, 16)
            sp.wait_ge(gp.sem, gp.value("fills"))
            for j in range(4):
                sp.dma_start(e.proj_w[32 * j:32 * j + 16, :, :],
                             A["L0_xattn_proj_w"].rearrange("(g j d) c -> j d g c", j=4, d=16)[j]).then_inc(p_in, 16)
            sp.wait_ge(dv.sem, dv.value("maskf"))
            for g in range(4):
                for b in range(B):
                    sp.dma_start(e.mask_dram[4 * b + g:4 * b + g + 1, :], mask_f[b:b + 1, :]).then_inc(m_out, 16)
            sp.wait_ge(m_out, 16 * 8)
            sp.wait_ge(p_in, 16 * 4)

        @block.gpsimd
        def _(pool):
            nc.gpsimd.memset(e.ident[:], 0.0)
            nc.gpsimd.memset(e.tri[:], 0.0)
            nc.gpsimd.memset(e.sel[:], 0.0).then_inc(gp.sem, gp.one("zeros"))
            pool.wait_ge(gp.sem, gp.value("zeros"))
            nc.gpsimd.affine_select(out=e.ident[:], in_=e.ident[:], compare_op=ALU.not_equal, fill=1.0, base=0,
                                    pattern=[[-1, P]], channel_multiplier=1).then_inc(gp.sem, gp.one("ident"))
            nc.gpsimd.memset(e.eps[:], EPS)
            nc.gpsimd.memset(e.ones[:], 1.0)
            nc.gpsimd.memset(e.proj_w[:], 0.0).then_inc(gp.sem, gp.one("fills"))
            nc.gpsimd.affine_select(out=e.tri[:], in_=e.tri[:], compare_op=ALU.is_ge, fill=MASKED, base=0,
                                    pattern=[[-1, P]], channel_multiplier=1)
            nc.gpsimd.affine_select(out=e.sel[:].rearrange("p (j d) -> p j d", j=4),
                                    in_=e.sel[:].rearrange("p (j d) -> p j d", j=4), compare_op=ALU.not_equal,
                                    fill=1.0, base=-16, pattern=[[-32, 4], [0, 32]],
                                    channel_multiplier=1).then_inc(gp.sem, gp.one("selects"))

        @block.vector
        def _(dve):
            dve.wait_ge(w_in, 16 * N_LOADS)
            dve.tensor_scalar(mask_f[:], mask_row[:], MASKED, None, ALU.mult).then_inc(dv.sem, dv.one("maskf"))
            dve.wait_ge(gp.sem, gp.value("selects"))
            dve.tensor_scalar(e.qkv_bs[:], e.qkv_b[:], 0.25, None, ALU.mult)
            dve.tensor_copy(e.ident_bf[:], e.ident[:])
            dve.tensor_copy(e.tri_bf[:], e.tri[:]).then_inc(dv.sem, dv.one("consts"))
            dve.wait_ge(x_in, 16)
            for t in range(TILES):
                ins = dve.bn_stats(stats[:, t, :], e.x[:, t, :])
            ins.then_inc(dv.sem, dv.one("stats"))
            dve.wait_ge(dv.sem, dv.value("stats"))
            for t in range(TILES):
                ins = dve.bn_aggr(moments[:, t, :], stats[:, t, :])
            ins.then_inc(dv.sem, dv.one("moments"))
            dve.wait_ge(ln.sem, ln.value("rstd"))
            for t in range(TILES):
                ins = dve.tensor_scalar(h[:, t, :], e.x[:, t, :], moments[:, t, 0:1], rstd[:, t:t + 1],
                                        ALU.subtract, ALU.mult)
                if t % 2:
                    ins.then_inc(dv.sem, dv.one(f"h{t // 2}"))

        @block.scalar
        def _(act):
            act.wait_ge(gp.sem, gp.value("fills"))
            act.wait_ge(w_in, 16 * N_LOADS)
            act.wait_ge(dv.sem, dv.value("moments"))
            act.activation(rstd[:], moments[:, :, 1], ACT.Ln, bias=e.eps[:]).then_inc(ln.sem, ln.one("logvar"))
            act.wait_ge(ln.sem, ln.value("logvar"))
            act.activation(rstd[:], rstd[:], ACT.Exp, scale=-0.5).then_inc(ln.sem, ln.one("rstd"))
            for i in range(8):
                act.wait_ge(pe.sem, pe.value(f"hT{i}"))
                for c in range(KC):
                    ins = act.activation(e.hT[:, c, i * 256:(i + 1) * 256], ps[i][:, c * 256:(c + 1) * 256],
                                         ACT.Identity, bias=ln1_b[:, c:c + 1], scale=ln1_g[:, c:c + 1])
                ins.then_inc(ev.sem, ev.one(f"hT{i}"))

        @block.tensor
        def _(te):
            te.wait_ge(gp.sem, gp.value("ident"))
            for i in range(8):
                te.wait_ge(dv.sem, dv.value(f"h{i}"))
                for c in range(KC):
                    for t in range(2):
                        ins = te.transpose(ps[i][:, (2 * c + t) * P:(2 * c + t + 1) * P],
                                           h[:, 2 * i + t, c * P:(c + 1) * P], e.ident[:])
                ins.then_inc(pe.sem, pe.one(f"hT{i}"))


def part_qkv0(nc, e):
    with ExitStack() as ctx:
        sb = lambda n, s, d=F32: ctx.enter_context(nc.sbuf_tensor(n, s, d))
        sem = lambda n: ctx.enter_context(nc.semaphore(n))
        full = [sb(f"qk_full{i}", [P, 512]) for i in range(2)]
        high = [sb(f"qk_high{i}", [P, 512], F32R) for i in range(2)]
        low = [sb(f"qk_low{i}", [P, 512], F32R) for i in range(2)]
        ps = [ctx.enter_context(nc.psum_tensor(f"qkv{i}", [P, 512], F32)) for i in range(8)]
        made, evacuated, split, v_kept = sem("qkv_made"), sem("qk_evacuated"), sem("qk_split"), sem("v_kept")
        stored = [sem("qk_stored0"), sem("qk_stored1")]
        QK = [(w, fc, quarter) for w in range(2) for fc in range(KC) for quarter in range(4)]
        block = ctx.enter_context(nc.Block())

        @block.tensor
        def _(te):
            for u, (w, fc, quarter) in enumerate(QK):
                if u >= 8:
                    te.wait_ge(evacuated, u - 7)
                for k in range(KC):
                    ins = te.matmul(ps[u % 8][:], e.qkv_w[:, k, w * C + fc * P:w * C + (fc + 1) * P],
                                    e.hT[:, k, quarter * 512:(quarter + 1) * 512], start=k == 0, stop=k == KC - 1)
                ins.then_inc(made, 1)
            for u in range(8):
                te.wait_ge(evacuated, 9 + u)
                for t in range(2):
                    for k in range(KC):
                        ins = te.matmul(ps[u][:, t * C:(t + 1) * C],
                                        e.hT[:, k, (2 * u + t) * P:(2 * u + t + 1) * P],
                                        e.qkv_w[:, k, 2 * C:3 * C], start=k == 0, stop=k == KC - 1)
                ins.then_inc(made, 1)

        @block.scalar
        def _(act):
            for u, (w, fc, quarter) in enumerate(QK):
                act.wait_ge(made, u + 1)
                if u >= 2:
                    act.wait_ge(split, 2 * (u - 1))
                act.activation(full[u % 2][:], ps[u % 8][:], ACT.Identity, scale=0.25 if w == 0 else 1.0,
                               bias=(e.qkv_bs if w == 0 else e.qkv_b)[:, 2 * w + fc:2 * w + fc + 1]
                               ).then_inc(evacuated, 1)

        @block.vector
        def _(dve):
            for u in range(len(QK)):
                dve.wait_ge(evacuated, u + 1)
                if u >= 2:
                    dve.wait_ge(stored[u % 2], 64 * (u // 2))
                dve.tensor_copy(high[u % 2][:], full[u % 2][:]).then_inc(split, 1)
                dve.wait_ge(split, 2 * u + 1)
                dve.tensor_tensor(out=low[u % 2][:], in0=full[u % 2][:], in1=high[u % 2][:].bitcast(F32),
                                  op=ALU.subtract).then_inc(split, 1)
            for u in range(8):
                dve.wait_ge(made, 17 + u)
                b, kt = 2 * u // TB, 2 * u % TB
                for t in range(2):
                    dve.tensor_tensor(out=e.v_all[:, b, :, kt + t, :],
                                      in0=ps[u][:, t * C:(t + 1) * C].rearrange("p (g f) -> p g f", g=4),
                                      in1=e.v0_brep[:].rearrange("p (g f) -> p g f", g=4), op=ALU.add)

        @block.sync
        def _(sp):
            for u, (w, fc, quarter) in enumerate(QK):
                b, cols = quarter // 2, slice((quarter % 2) * 512, (quarter % 2 + 1) * 512)
                sp.wait_ge(split, 2 * u + 2)
                for part, tile in ((0, high), (1, low)):
                    for half in range(2):
                        sp.dma_start(e.qk_dram[w, 4 * b + 2 * fc + half, part, :, cols],
                                     tile[u % 2][64 * half:64 * half + 64, :].bitcast(F32)).then_inc(stored[u % 2], 16)
            for i in range(2):
                sp.wait_ge(stored[i], 64 * 8)


def part_attention0(nc, e):
    with ExitStack() as ctx:
        sb = lambda n, s, d=F32: ctx.enter_context(nc.sbuf_tensor(n, s, d))
        sem = lambda n: ctx.enter_context(nc.semaphore(n))
        qs = [sb(f"q_stack{i}", [66, 4, T], F32R) for i in range(2)]
        ks = [sb(f"k_stack{i}", [66, 4, T], F32R) for i in range(2)]
        v4 = [sb(f"v_group{i}", [P, TB, 4, 32]) for i in range(2)]
        probs = [[sb(f"probs{j}{i}", [P, T]) for i in range(2)] for j in range(4)]
        raw, rden = sb("raw", [P, T]), sb("rden", [P, T])
        part_max, row_max = sb("part_max", [P, 2, 4, 4]), sb("row_max", [P, 4, TB])
        max_row = sb("max_row", [32, P], F32R)
        s1 = [ctx.enter_context(nc.psum_tensor(f"s1_{i}", [P, 512], F32)) for i in range(2)]
        s2 = [ctx.enter_context(nc.psum_tensor(f"s2_{i}", [P, T], F32)) for i in range(2)]
        o = ctx.enter_context(nc.psum_tensor("o", [P, T], F32))
        stack_in = [sem("stack_in0"), sem("stack_in1")]
        v_ready, rows_set = sem("v_ready"), sem("rows_set")
        s1_made, s1_max, max_made, max_turned, max_kept = (
            sem(n) for n in ("s1_made", "s1_max", "max_made", "max_turned", "max_kept"))
        max_out, max_in = sem("max_out"), sem("max_in")
        s2_made, exp_made, pv_made, raw_made = sem("s2_made"), sem("exp_made"), sem("pv_made"), sem("raw_made")
        den_made, log_made, rden_made, a_made = sem("den_made"), sem("log_made"), sem("rden_made"), sem("a_made")

        CH = [(j, t, k0, min(k0 + 512, (t + 1) * P)) for j in range(4) for t in range(TB)
              for k0 in range(0, (t + 1) * P, 512)]
        UN = [(kt, j) for kt in range(TB) for j in range(4)]
        N1, N2, G = len(CH), len(UN), 8
        pieces = lambda kt: [(max(kt * P, c0), c0 + 512) for c0 in (0, 512) if c0 + 512 > kt * P]

        def groups(engine, emit):
            emit(None, 0, 1, 1)
            emit(0, 1, 0, 1)
            with engine.Fori(0, 3) as i:
                emit(2 * i + 1, 2 * i + 2, 1, i + 2)
                emit(2 * i + 2, 2 * i + 3, 0, i + 2)
            emit(7, None, 1, None)

        block = ctx.enter_context(nc.Block())

        @block.sync
        def _(sp):
            sp.wait_ge(rows_set, 1)

            def emit(cur, nxt, par, loads):
                if nxt is not None:
                    q, k, done = qs[1 - par], ks[1 - par], stack_in[1 - par]
                    loads = [(stack[16 * i:16 * i + 16].bitcast(F32),
                              src[ds(nxt, 1), part].rearrange("g (j d) t -> d (g j) t", j=4))
                             for stack, src, parts in ((q, e.qk_dram[0], (0, 1, 0, 1)), (k, e.qk_dram[1], (0, 0, 1, 1)))
                             for i, part in enumerate(parts)]
                    if cur is not None and not (isinstance(cur, int) and cur == 0):
                        sp.wait_ge(s2_made, N2 * cur)
                    for dst, rows in loads:
                        sp.dma_start(dst, rows).then_inc(done, 16)
                    mask = e.mask_dram[ds(nxt, 1), :]
                    for j in range(4):
                        sp.dma_start(k[64:65, j, :].bitcast(F32), mask).then_inc(done, 16)
                    sp.wait_ge(max_kept, nxt + 1)
                    sp.dma_start(e.max_dram[1 - par], max_row[:].bitcast(F32)).then_inc(max_out, 16)
                    sp.wait_ge(max_out, 16 * (nxt + 1))
                    sp.dma_start(qs[1 - par][65:66].bitcast(F32), e.max_dram[1 - par].rearrange("(o j t) q -> o j (t q)", o=1, j=4)
                                 ).then_inc(max_in, 16)

            groups(sp, emit)

        @block.gpsimd
        def _(pool):
            pool.wait_ge(rows_set, 1)

            def emit(cur, nxt, par, loads):
                if nxt is not None:
                    if cur is not None and not (isinstance(cur, int) and cur == 0):
                        pool.wait_ge(pv_made, TB * cur)
                    src = e.v_all[:].rearrange("p b g k f -> p (b g) k f")[:, ds(nxt, 1)]
                    pool.tensor_copy(v4[1 - par][:, :, :, 0:16],
                                     src.rearrange("p o k (j d) -> p (o k) j d", j=4)).then_inc(v_ready, 1)

            groups(pool, emit)

        @block.tensor
        def _(te):
            te.wait_ge(rows_set, 1)

            def emit(cur, nxt, par, loads):
                if nxt is not None:
                    q1, k1 = qs[1 - par], ks[1 - par]

                    def chunk(i):
                        j, t, c0, c1 = CH[i]
                        if i >= 2:
                            te.wait_ge(s1_max, N1 * nxt + i - 1)
                        elif cur is not None and not (isinstance(cur, int) and cur == 0):
                            te.wait_ge(log_made, cur)
                        elif cur is not None:
                            te.wait_ge(max_kept, 1)
                        diagonal = c1 == (t + 1) * P
                        ins = te.matmul(s1[i % 2][:, 0:c1 - c0], q1[0:65, j, t * P:(t + 1) * P], k1[0:65, j, c0:c1],
                                        start=True, stop=not diagonal)
                        if diagonal:
                            ins = te.matmul(s1[i % 2][:, t * P - c0:c1 - c0], e.ident_bf[:], e.tri_bf[:],
                                            start=False, stop=True)
                        ins.then_inc(s1_made, 1)
                if cur is not None:
                    q2, k2, v = qs[par], ks[par], v4[par]

                    def unit(u):
                        kt, j = UN[u]
                        if u >= 2:
                            te.wait_ge(exp_made, N2 * cur + u - 1)
                        elif not (isinstance(cur, int) and cur == 0):
                            te.wait_ge(exp_made, N2 * cur)
                        for c0, c1 in pieces(kt):
                            diagonal = c0 == kt * P
                            ins = te.matmul(s2[u % 2][:, c0:c1], k2[0:66, j, kt * P:(kt + 1) * P], q2[0:66, j, c0:c1],
                                            start=True, stop=not diagonal)
                            if diagonal:
                                ins = te.matmul(s2[u % 2][:, c0:c0 + P], e.tri_bf[:], e.ident_bf[:],
                                                start=False, stop=True)
                        ins.then_inc(s2_made, 1)

                    def values(kt):
                        te.wait_ge(exp_made, N2 * cur + 4 * kt + 4)
                        for c0, c1 in pieces(kt):
                            for j in range(4):
                                last = kt == (3 if c1 == 512 else 7)
                                ins = te.matmul(o[32 * j:32 * j + 32, c0:c1], v[:, kt, j, :],
                                                probs[j][kt % 2][:, c0:c1], start=kt == 0, stop=last)
                        ins.then_inc(pv_made, 1)

                    te.wait_ge(max_in, 16 * (cur + 1))
                    te.wait_ge(v_ready, cur + 1)
                if cur is not None:
                    done = 0
                    for u in range(N2):
                        unit(u)
                        if u % 4 == 1 and u >= 5:
                            values(u // 4 - 1)
                        if nxt is not None and u >= 8:
                            if u == 8:
                                te.wait_ge(stack_in[1 - par], 192 * loads)
                            while done < (u - 7) * N1 // (N2 - 8):
                                chunk(done)
                                done += 1
                    values(TB - 1)
                else:
                    te.wait_ge(stack_in[1 - par], 192 * loads)
                    for i in range(N1):
                        chunk(i)
                if nxt is not None:
                    te.wait_ge(max_made, nxt + 1)
                    te.transpose(s1[0][0:32, 0:P], row_max[:].rearrange("p j t -> p (j t)"),
                                 e.ident[:]).then_inc(max_turned, 1)
                if cur is not None:
                    te.wait_ge(raw_made, cur + 1)
                    if nxt is not None:
                        te.wait_ge(max_kept, nxt + 1)
                    else:
                        te.wait_ge(s1_max, N1 * G)
                    for half in range(2):
                        ins = te.matmul(s1[half][:], e.sel[:], raw[:, half * 512:(half + 1) * 512],
                                        start=True, stop=True)
                    ins.then_inc(den_made, 1)

            groups(te, emit)

        @block.vector
        def _(dve):
            for i in range(2):
                dve.memset(qs[i][64:66].bitcast(F32), 1.0)
                dve.memset(v4[i][:], 1.0)
                ins = dve.memset(ks[i][64:66].bitcast(F32), 1.0)
            ins.then_inc(rows_set, 1)

            def emit(cur, nxt, par, loads):
                if nxt is not None:
                    for i, (j, t, c0, c1) in enumerate(CH):
                        dve.wait_ge(s1_made, N1 * nxt + i + 1)
                        dst = row_max[:, j, t:t + 1] if t < 4 else part_max[:, c0 // 512, j, t - 4:t - 3]
                        if i == 0 and cur is not None:
                            dve.wait_ge(max_turned, nxt)
                        dve.tensor_reduce(dst, s1[i % 2][:, 0:c1 - c0], AX.X, ALU.max).then_inc(s1_max, 1)
                    dve.wait_ge(s1_max, N1 * nxt + N1)
                    dve.tensor_tensor(out=row_max[:, :, 4:8], in0=part_max[:, 0], in1=part_max[:, 1],
                                      op=ALU.max).then_inc(max_made, 1)
                if cur is not None:
                    dve.wait_ge(rden_made, cur + 1)
                    dve.tensor_tensor(out=e.aT0[:, ds(cur, 1), :].rearrange("p o t -> p (o t)"), in0=raw[:],
                                      in1=rden[:], op=ALU.mult).then_inc(a_made, 1)

            groups(dve, emit)

        @block.scalar
        def _(act):
            def emit(cur, nxt, par, loads):
                if cur is not None:
                    for u, (kt, j) in enumerate(UN):
                        act.wait_ge(s2_made, N2 * cur + u + 1)
                        if kt >= 2:
                            act.wait_ge(pv_made, TB * cur + kt - 1)
                        elif not (isinstance(cur, int) and cur == 0) and j == 0:
                            act.wait_ge(pv_made, TB * cur)
                        act.activation(probs[j][kt % 2][:, kt * P:T], s2[u % 2][:, kt * P:T],
                                       ACT.Exp).then_inc(exp_made, 1)
                    act.wait_ge(pv_made, TB * (cur + 1))
                    if not (isinstance(cur, int) and cur == 0):
                        act.wait_ge(a_made, cur)
                    act.activation(raw[:], o[:], ACT.Identity).then_inc(raw_made, 1)
                if nxt is not None:
                    act.wait_ge(max_turned, nxt + 1)
                    if cur is not None:
                        act.wait_ge(max_out, 16 * nxt)
                    act.activation(max_row[:], s1[0][0:32, 0:P], ACT.Identity, scale=-1.0).then_inc(max_kept, 1)
                if cur is not None:
                    act.wait_ge(den_made, cur + 1)
                    for half in range(2):
                        ins = act.activation(rden[:, half * 512:(half + 1) * 512], s1[half][:], ACT.Ln)
                    ins.then_inc(log_made, 1)
                    act.wait_ge(log_made, cur + 1)
                    act.activation(rden[:], rden[:], ACT.Exp, scale=-1.0).then_inc(rden_made, 1)

            groups(act, emit)



def part_project0(nc, e):
    with ExitStack() as ctx:
        ps = [ctx.enter_context(nc.psum_tensor(f"prj{i}", [P, 2, C], F32)) for i in range(4)]
        made, added = ctx.enter_context(nc.semaphore("prj_made")), ctx.enter_context(nc.semaphore("prj_added"))
        block = ctx.enter_context(nc.Block())

        @block.tensor
        def _(te):
            for u in range(TILES // 2):
                if u >= 4:
                    te.wait_ge(added, u - 2)
                b = 2 * u // TB
                for i in range(2):
                    t = (2 * u + i) % TB
                    for g in range(4):
                        ins = te.matmul(ps[u % 4][:, i, :], e.aT0[:, 4 * b + g, t * P:(t + 1) * P], e.proj_w[:, g, :],
                                        start=g == 0, stop=g == 3)
                ins.then_inc(made, 1)

        @block.vector
        def _(dve):
            bias = e.proj_brep[:].unsqueeze(1).to_broadcast([P, TILES, C])
            dve.tensor_tensor(out=e.x[:], in0=e.x[:], in1=bias, op=ALU.add).then_inc(added, 1)
            dve.wait_ge(added, 1)
            for u in range(TILES // 2):
                dve.wait_ge(made, u + 1)
                x = e.x[:, 2 * u:2 * u + 2, :]
                dve.tensor_tensor(out=x, in0=ps[u % 4][:], in1=x, op=ALU.add).then_inc(added, 1)


def part_context0(nc, e, A, later):
    with ExitStack() as ctx:
        sb = lambda n, s, d=F32: ctx.enter_context(nc.sbuf_tensor(n, s, d))
        sem = lambda n: ctx.enter_context(nc.semaphore(n))
        ctx_rows = sb("ctx_rows", [P, CC])
        q_w, q_b = sb("q_w", [P, KC, C]), sb("q_b", [P, KC])
        k_w, k_b = sb("k_w", [96, 2, C]), sb("k_b", [P, KC])
        v_w, v_b = sb("v_w", [96, 2, C]), sb("v_b", [P, KC])
        o_w = sb("o_w", [P, KC, C])
        t_w, t_b = sb("t_w", [96, 2, C]), sb("t_b", [P, KC])
        t_brep = sb("t_brep", [S2, C])
        mask8 = sb("mask8", [P, B, S2], mybir.dt.uint8)
        mrep = sb("mrep", [P, B, S2])
        head16 = sb("head16", [P, 8])
        ones_col = sb("ones_col", [P, P])
        q_brep = sb("q_brep", [P, KC, P])
        q_wT = sb("q_wT", [P, KC, C])
        kT, vT = sb("kT", [P, KC, P]), sb("vT", [P, KC, P])
        kbd = sb("kbd", [P, B, KC, 8, S2])
        vbd = sb("vbd", [P, B, KC, 8, S2])
        ps = [ctx.enter_context(nc.psum_tensor(f"cross{i}", [P, 512], F32)) for i in range(8)]
        c_in, w_in, later_in = sem("c_in"), sem("cw_in"), sem("chain_w_in")
        order = (["ctxT", "q_wT", "kT", "vT", "tok", "tokT"]
                 + [f"M{b}{g}{d}" for b in range(B) for g in range(KC) for d in range(KC)]
                 + [f"bias{b}{g}" for b in range(B) for g in range(KC)]
                 + [f"VW{b}{c}" for b in range(B) for c in range(4)])
        pe = Steps(sem("cross_pe"), order)
        ev = Steps(sem("cross_evac"), order)
        dv = Steps(sem("cross_dve"), ["mrep", "brep", "kbd", "vbd"])
        gp = Steps(sem("cross_pool"), ["ones", "first", "second"])
        bank = lambda name: order.index(name) % 8
        N_LOADS = 11
        ALL_W = 16 * N_LOADS
        block = ctx.enter_context(nc.Block())

        @block.sync
        def _(sp):
            sp.dma_start(ctx_rows[:], A["ctx_768"].rearrange("b s c -> (b s) c")).then_inc(c_in, 16)
            rows96 = lambda n: A[n].rearrange("(k p) c -> p k c", p=96)
            rows = lambda n: A[n].rearrange("(k p) c -> p k c", p=P)
            loads = [
                (q_w[:], rows("L0_xattn_q_w")), (q_b[:], column(A["L0_xattn_q_b"], KC)),
                (k_w[:], rows96("L0_xattn_k_w")), (k_b[:], column(A["L0_xattn_k_b"], KC)),
                (v_w[:], rows96("L0_xattn_v_w")), (v_b[:], column(A["L0_xattn_v_b"], KC)),
                (o_w[:], rows("L0_xattn_out_w")),
                (t_w[:], rows96("L1_xattn_W_proj")), (t_b[:], column(A["L1_xattn_b_proj"], KC)),
                (t_brep[:], A["L1_xattn_b_proj"].partition_broadcast(S2)),
                (mask8[:], A["mask_BxS2_bf0"].rearrange("b s -> (b s)").partition_broadcast(P)
                 .rearrange("p (b s) -> p b s", b=B)),
            ]
            for dst, src in loads:
                sp.dma_start(dst, src).then_inc(w_in, 16)
            assert len(loads) == N_LOADS
            for dst, src in later:
                sp.dma_start(dst, src).then_inc(later_in, 16)
            sp.wait_ge(later_in, 16 * len(later))


        @block.gpsimd
        def _(pool):
            pool.memset(head16[:], 1.0)
            pool.memset(ones_col[:], 1.0).then_inc(gp.sem, gp.one("ones"))
            pool.wait_ge(gp.sem, gp.value("ones"))
            pool.affine_select(out=head16[:], in_=head16[:], compare_op=ALU.is_ge, fill=0.0, base=0,
                               pattern=[[-16, 8]], channel_multiplier=1).then_inc(gp.sem, gp.one("first"))
            pool.wait_ge(gp.sem, gp.value("first"))
            pool.affine_select(out=head16[:], in_=head16[:], compare_op=ALU.is_ge, fill=0.0, base=15,
                               pattern=[[16, 8]], channel_multiplier=-1).then_inc(gp.sem, gp.one("second"))

        @block.vector
        def _(dve):
            dve.wait_ge(w_in, ALL_W)
            dve.tensor_scalar(mrep[:], mask8[:], MASKED, None, ALU.mult).then_inc(dv.sem, dv.one("mrep"))
            dve.wait_ge(gp.sem, gp.value("second"))
            for g in range(KC):
                ins = dve.tensor_scalar(q_brep[:, g, :], ones_col[:], q_b[:, g:g + 1], 0.25, ALU.mult,
                                        ALU.mult)
            ins.then_inc(dv.sem, dv.one("brep"))
            head_rep = head16[:].unsqueeze(2).to_broadcast([P, 8, S2])
            dve.wait_ge(ev.sem, ev.value("vT"))
            for name, dst, src in (("kbd", kbd, kT), ("vbd", vbd, vT)):
                for b in range(B):
                    for g in range(KC):
                        rep = src[:, g, b * S2:(b + 1) * S2].unsqueeze(1).to_broadcast([P, 8, S2])
                        ins = dve.tensor_tensor(out=dst[:, b, g], in0=rep, in1=head_rep, op=ALU.mult)
                ins.then_inc(dv.sem, dv.one(name))
            dve.wait_ge(ev.sem, ev.value(f"bias{B - 1}{KC - 1}"))
            for b in range(B):
                view = e.bias0[:, b, :].rearrange("p (h s) -> p h s", s=S2)
                dve.tensor_tensor(out=view, in0=view, in1=mrep[:, b, :].unsqueeze(1).to_broadcast([P, 16, S2]),
                                  op=ALU.add)

        @block.scalar
        def _(act):
            def copy(name, dst, src, **kw):
                act.wait_ge(pe.sem, pe.value(name))
                act.activation(dst, src, ACT.Identity, **kw).then_inc(ev.sem, ev.one(name))

            act.wait_ge(w_in, ALL_W)
            p = lambda name: ps[bank(name)]
            copy("ctxT", e.ctxT[:], p("ctxT")[0:96, 0:256].rearrange("p (k s) -> p k s", k=2))
            copy("q_wT", q_wT[:], p("q_wT")[:].rearrange("p (k c) -> p k c", k=2))
            for name, dst, bias in (("kT", kT, k_b), ("vT", vT, v_b)):
                act.wait_ge(pe.sem, pe.value(name))
                for g in range(KC):
                    ins = act.activation(dst[:, g, :], p(name)[:, g * P:(g + 1) * P], ACT.Identity,
                                         bias=bias[:, g:g + 1])
                ins.then_inc(ev.sem, ev.one(name))
            act.wait_ge(pe.sem, pe.value("tok"))
            act.activation(e.tok[:], p("tok")[0:S2, :].rearrange("p (b c) -> p b c", b=B),
                           ACT.Identity).then_inc(ev.sem, ev.one("tok"))
            act.wait_ge(pe.sem, pe.value("tokT"))
            for g in range(KC):
                ins = act.activation(e.tokT[:, g, :], p("tokT")[:, g * P:(g + 1) * P], ACT.Identity,
                                     bias=t_b[:, g:g + 1])
            ins.then_inc(ev.sem, ev.one("tokT"))
            for b in range(B):
                for g in range(KC):
                    for d in range(KC):
                        copy(f"M{b}{g}{d}", e.m0[:, b, d, g * 512:(g + 1) * 512], p(f"M{b}{g}{d}")[:], scale=0.25)
            for b in range(B):
                for g in range(KC):
                    copy(f"bias{b}{g}", e.bias0[:, b, g * 512:(g + 1) * 512], p(f"bias{b}{g}")[:])
            for b in range(B):
                for c in range(4):
                    copy(f"VW{b}{c}", e.vw0[:, b, 2 * c:2 * c + 2, :],
                         p(f"VW{b}{c}")[:].rearrange("p (c n) -> p c n", c=2))

        @block.tensor
        def _(te):
            free = lambda name: te.wait_ge(ev.sem, order.index(name) - 7) if order.index(name) >= 8 else None
            p = lambda name: ps[bank(name)]
            te.wait_ge(c_in, 16)
            te.wait_ge(w_in, ALL_W)
            for k in range(2):
                ins = te.transpose(p("ctxT")[0:96, k * P:(k + 1) * P], ctx_rows[:, 96 * k:96 * k + 96], e.ident[:])
            ins.then_inc(pe.sem, pe.one("ctxT"))
            for g in range(KC):
                for d in range(KC):
                    ins = te.transpose(p("q_wT")[:, (2 * g + d) * P:(2 * g + d + 1) * P],
                                       q_w[:, d, g * P:(g + 1) * P], e.ident[:])
            ins.then_inc(pe.sem, pe.one("q_wT"))
            te.wait_ge(ev.sem, ev.value("ctxT"))
            for name, w in (("kT", k_w), ("vT", v_w)):
                for g in range(KC):
                    for k in range(2):
                        ins = te.matmul(p(name)[:, g * P:(g + 1) * P], w[:, k, g * P:(g + 1) * P], e.ctxT[:, k, :],
                                        start=k == 0, stop=k == 1)
                ins.then_inc(pe.sem, pe.one(name))
            for b in range(B):
                for k in range(2):
                    te.matmul(p("tok")[0:S2, b * C:(b + 1) * C], e.ctxT[:, k, b * S2:(b + 1) * S2], t_w[:, k, :],
                              start=k == 0, stop=False)
                ins = te.matmul(p("tok")[0:S2, b * C:(b + 1) * C], e.ident[0:S2, 0:S2], t_brep[:],
                                start=False, stop=True)
            ins.then_inc(pe.sem, pe.one("tok"))
            for g in range(KC):
                for k in range(2):
                    ins = te.matmul(p("tokT")[:, g * P:(g + 1) * P], t_w[:, k, g * P:(g + 1) * P], e.ctxT[:, k, :],
                                    start=k == 0, stop=k == 1)
            ins.then_inc(pe.sem, pe.one("tokT"))
            te.wait_ge(dv.sem, dv.value("vbd"))
            for b in range(B):
                for g in range(KC):
                    for d in range(KC):
                        free(f"M{b}{g}{d}")
                        te.matmul(p(f"M{b}{g}{d}")[:], q_wT[:, g, d * P:(d + 1) * P],
                                  kbd[:, b, g].rearrange("p h s -> p (h s)"), start=True,
                                  stop=True).then_inc(pe.sem, pe.one(f"M{b}{g}{d}"))
            for b in range(B):
                for g in range(KC):
                    free(f"bias{b}{g}")
                    te.matmul(p(f"bias{b}{g}")[:], q_brep[:, g, :], kbd[:, b, g].rearrange("p h s -> p (h s)"),
                              start=True, stop=True).then_inc(pe.sem, pe.one(f"bias{b}{g}"))
            for b in range(B):
                for c in range(4):
                    free(f"VW{b}{c}")
                    for i in range(2):
                        g, pair = (2 * c + i) // 4, (2 * c + i) % 4
                        ins = te.matmul(p(f"VW{b}{c}")[:, i * C:(i + 1) * C],
                                        vbd[:, b, g, 2 * pair:2 * pair + 2, :].rearrange("p h s -> p (h s)"),
                                        o_w[:, g, :], start=True, stop=True)
                    ins.then_inc(pe.sem, pe.one(f"VW{b}{c}"))


BLOCKS = TB // 2


def norm_steps(name):
    return [f"{name}.stats", f"{name}.moments", f"{name}.h"]


class Chain:

    def __init__(self, nc, ctx, label, te, dve, act, pool, bias_columns):
        self.nc = nc
        sem = lambda n: ctx.enter_context(nc.semaphore(n))
        self.te, self.dve, self.act, self.pool = (
            [Steps(sem(f"{label}_{name}{s}"), order) for s in range(B)]
            for name, order in (("tensor", te), ("vector", dve), ("scalar", act), ("gpsimd", pool)))
        sb = lambda n, shape, d=F32: [ctx.enter_context(nc.sbuf_tensor(f"{label}_{n}{s}", shape, d)) for s in range(B)]
        self.sb = sb
        self.h, self.hT = sb("h", [P, 2, C]), sb("hT", [P, KC, 256])
        self.stats, self.moments, self.rstd = sb("stats", [P, 2, 6]), sb("moments", [P, 2, 2]), sb("rstd", [P, 2])
        self.scores, self.pT = sb("scores", [P, 2, 1024]), sb("pT", [P, 8, 256])
        self.top, self.total = sb("top", [P, 2, 16]), sb("total", [P, 2, 16])
        self.spare, self.power_set = sb("spare", [1, 1]), sem(f"{label}_power_set")
        one = lambda n, shape, d: ctx.enter_context(nc.sbuf_tensor(f"{label}_{n}", shape, d))
        self.rows, self.ones = one("rows", [96, bias_columns], BF16), one("ones", [96, P], BF16)
        self.power = one("power", [P, 2], F32)
        self.part, self.rows_made = one("part", [96, 1024], BF16), sem(f"{label}_rows_made")
        self.xc, self.xT = sb("xc", [P, 2, C]), sb("xT", [P, KC, 256])
        self.ps = [ctx.enter_context(nc.psum_tensor(f"{label}_ps{s}", [P, 2048], F32)) for s in range(B)]


class Tail:

    def __init__(self, nc, ctx, ch, label, dve, pool):
        sem = lambda n: ctx.enter_context(nc.semaphore(n))
        self.dve, self.pool = ([Steps(sem(f"{label}_{name}{s}"), order) for s in range(B)]
                               for name, order in (("vector", dve), ("gpsimd", pool)))
        self.h, self.stats, self.moments, self.rstd, self.spare = (
            ch.sb(f"t_{n}", shape) for n, shape in (("h", [P, 2, C]), ("stats", [P, 2, 6]), ("moments", [P, 2, 2]),
                                                    ("rstd", [P, 2]), ("spare", [1, 1])))
        self.power = ch.power


def chain_blocks(engine, emit):
    emit(0, True, False)
    with engine.Fori(1, BLOCKS - 1) as i:
        emit(i, False, False)
    emit(BLOCKS - 1, False, True)


def after(engine, steps, name, turn):
    engine.wait_ge(steps.sem, steps.value(name, turn))


def after_spare(dve, ch, s, name, turn, steps=None):
    after(dve, (steps or ch.dve)[s], name, turn)
    dve.memset(ch.spare[s][:], 0.0)


def tokens(e, s, i):
    return e.x[:, TB * s:TB * (s + 1), :].rearrange("p (i t) c -> p i (t c)", t=2)[:, ds(i, 1), :].rearrange(
        "p o (t c) -> p (o t) c", t=2)


def norm_vector(dve, ch, name, i, source, before=None, scaled=False, streams=range(B)):
    for s in streams:
        if before:
            before(s)
        for t in range(2):
            ins = dve.bn_stats(ch.stats[s][:, t, :], source(s)[:, t, :])
        ins.then_inc(ch.dve[s].sem, ch.dve[s].one(f"{name}.stats"))
    for s in streams:
        after_spare(dve, ch, s, f"{name}.stats", i)
        for t in range(2):
            ins = dve.bn_aggr(ch.moments[s][:, t, :], ch.stats[s][:, t, :])
        ins.then_inc(ch.dve[s].sem, ch.dve[s].one(f"{name}.moments"))
    if scaled:
        return
    for s in streams:
        after(dve, ch.pool[s], f"{name}.rstd", i)
        for t in range(2):
            ins = dve.tensor_scalar(ch.h[s][:, t, :], source(s)[:, t, :], ch.moments[s][:, t, 0:1],
                                    ch.rstd[s][:, t:t + 1], ALU.subtract, ALU.mult)
        ins.then_inc(ch.dve[s].sem, ch.dve[s].one(f"{name}.h"))


def norm_gpsimd(pool, ch, e, name, i):
    for s in range(B):
        after(pool, ch.dve[s], f"{name}.moments", i)
        pool.tensor_tensor(out=ch.rstd[s][:], in0=ch.moments[s][:, :, 1], in1=e.eps[:].to_broadcast([P, 2]),
                           op=ALU.add).then_inc(ch.pool[s].sem, ch.pool[s].one(f"{name}.shifted"))
        after(pool, ch.pool[s], f"{name}.shifted", i)
        pool.tensor_tensor(out=ch.rstd[s][:], in0=ch.rstd[s][:], in1=ch.power[:], op=ALU.pow).then_inc(
            ch.pool[s].sem, ch.pool[s].one(f"{name}.rstd"))


def scaled_vector(dve, ch, name, i, source, gain, bias, dst, done):
    for s in range(B):
        after(dve, ch.pool[s], f"{name}.rstd", i)
        for t in range(2):
            ins = dve.scalar_tensor_tensor(out=ch.h[s][:, t, :], in0=source(s)[:, t, :],
                                           scalar=ch.moments[s][:, t, 0:1], in1=gain[:], op0=ALU.subtract,
                                           op1=ALU.mult)
        ins.then_inc(ch.dve[s].sem, ch.dve[s].one(f"{name}.h"))
    for s in range(B):
        after(dve, ch.dve[s], f"{name}.h", i)
        for t in range(2):
            ins = dve.scalar_tensor_tensor(out=dst(s)[:, t, :], in0=ch.h[s][:, t, :], scalar=ch.rstd[s][:, t:t + 1],
                                           in1=bias[:], op0=ALU.mult, op1=ALU.add)
        ins.then_inc(ch.dve[s].sem, ch.dve[s].one(done))


def bias_rows(dve, ch, source, piece):
    made, rest = ch.rows_made, ch.scores[0][0:96, 0, 0:piece]
    count = 1
    dve.memset(ch.rows[:], 0.0)
    dve.memset(ch.ones[:], 1.0).then_inc(made, 1)
    for c0 in range(0, ch.rows.shape[1], piece):
        src = source[0:96, c0:c0 + piece]
        for row in (0, 32, 64):
            dve.wait_ge(made, count)
            dve.tensor_copy(ch.rows[row:row + 1, c0:c0 + piece], src[row:row + 1])
            if row < 64:
                dve.tensor_copy(ch.part[:, 0:piece], src).then_inc(made, 1)
                dve.wait_ge(made, count + 1)
                dve.tensor_tensor(out=rest, in0=src, in1=ch.part[:, 0:piece], op=ALU.subtract).then_inc(made, 1)
                src = rest
                count += 2
    dve.wait_ge(made, count)
    dve.sem_inc(made, 1)
    return count + 1


def add_bias(te, ch, dst, c0, stop=True):
    return te.matmul(dst, ch.ones[:], ch.rows[:, c0:c0 + dst.shape[-1]], start=False, stop=stop)


def turn_tensor(te, ch, e, src, s, bank):
    for c in range(KC):
        for t in range(2):
            ins = te.transpose(ch.ps[s][:, 512 * bank + (2 * c + t) * P:512 * bank + (2 * c + t + 1) * P],
                               src[:, t, c * P:(c + 1) * P], e.ident[:])
    return ins


def turn_step(te, ch, e, i, name, s, bank=0):
    after(te, ch.dve[s], f"{name}.h", i)
    turn_tensor(te, ch, e, ch.h[s], s, bank).then_inc(ch.te[s].sem, ch.te[s].one(f"{name}.T"))


def turned_scalar(act, ch, s, bank, dst, gain=None, bias=None):
    for c in range(KC):
        kw = dict(scale=gain[:, c:c + 1], bias=bias[:, c:c + 1]) if gain is not None else {}
        ins = act.activation(dst[:, c, :], ch.ps[s][:, 512 * bank + 256 * c:512 * bank + 256 * (c + 1)],
                             ACT.Identity, **kw)
    return ins


def scores_tensor(te, ch, e, name, i, lhs, lhs_ready, m, cols, bias, turn):
    for s in range(B):
        if s == 0:
            turn(0)
        after(te, ch.act[s], lhs_ready, i)
        for t in range(2):
            for c0 in range(0, cols, 512):
                dst = ch.ps[s][:, t * cols + c0:t * cols + c0 + 512]
                for k in range(KC):
                    ins = te.matmul(dst, lhs[s][:, k, t * P:(t + 1) * P], m[:, s, k, c0:c0 + 512],
                                    start=k == 0, stop=k == KC - 1 and bias is None)
                if bias is not None:
                    ins = add_bias(te, ch, dst, bias + s * cols + c0)
            ins.then_inc(ch.te[s].sem, ch.te[s].one(f"{name}.scores{t}"))
            if s == 0 and t == 0:
                turn(1)


def cross_tensor(te, ch, e, name, i, vw, cols, out_bias):
    def turn(s):
        for t in range(2):
            after(te, ch.pool[s], f"{name}.probs{t}", i)
            for c in range(cols // P):
                ins = te.transpose(ch.ps[s][:, c * 256 + t * P:c * 256 + (t + 1) * P],
                                   scores_of(ch, s, cols)[:, t, c * P:(c + 1) * P], e.ident[:])
        ins.then_inc(ch.te[s].sem, ch.te[s].one(f"{name}.turned"))

    turn(0)
    for s in range(B):
        after(te, ch.act[s], f"{name}.kept", i)
        after(te, ch.dve[s], f"{name}.kept", i)
        for t in range(2):
            dst = ch.ps[s][:, t * C:(t + 1) * C]
            for c in range(cols // P):
                ins = te.matmul(dst, ch.pT[s][:, c, t * P:(t + 1) * P], vw[:, s, c, :],
                                start=c == 0, stop=c == cols // P - 1 and out_bias is None)
            if out_bias is not None:
                ins = add_bias(te, ch, dst, out_bias)
            if t == 1:
                ins.then_inc(ch.te[s].sem, ch.te[s].one(f"{name}.out"))
            elif s == 0:
                turn(1)


def scores_of(ch, s, cols):
    return ch.scores[s][:].rearrange("p t n -> p (t n)")[:, 0:2 * cols].rearrange("p (t n) -> p t n", t=2)


def cross_vector_steps(name):
    return [f"{name}.{x}" for x in ("top0", "less0", "top1", "less1", "total0", "inverse0", "total1", "inverse1",
                                    "kept")]


def cross_vector(dve, ch, name, i, cols):
    heads = cols // S2
    by_head = lambda ap: ap.rearrange("p (h k) -> p h k", k=S2)
    sc = lambda s, t: by_head(scores_of(ch, s, cols)[:, t])

    def sums(s, t):
        after(dve, ch.act[s], f"{name}.exp{t}", i)
        dve.tensor_reduce(ch.total[s][:, t, 0:heads], sc(s, t), AX.X, ALU.add).then_inc(
            ch.dve[s].sem, ch.dve[s].one(f"{name}.total{t}"))
        after(dve, ch.dve[s], f"{name}.total{t}", i)
        dve.reciprocal(ch.total[s][:, t, 0:heads], ch.total[s][:, t, 0:heads]).then_inc(
            ch.dve[s].sem, ch.dve[s].one(f"{name}.inverse{t}"))

    last = None
    for s in range(B):
        for t in range(2):
            src, top = by_head(ch.ps[s][:, t * cols:(t + 1) * cols]), ch.top[s][:, t, 0:heads]
            after(dve, ch.te[s], f"{name}.scores{t}", i)
            dve.tensor_reduce(top, src, AX.X, ALU.max).then_inc(ch.dve[s].sem, ch.dve[s].one(f"{name}.top{t}"))
            after(dve, ch.dve[s], f"{name}.top{t}", i)
            dve.tensor_tensor(out=sc(s, t), in0=src, in1=top.unsqueeze(2).to_broadcast([P, heads, S2]),
                              op=ALU.subtract).then_inc(ch.dve[s].sem, ch.dve[s].one(f"{name}.less{t}"))
            if last:
                sums(*last)
            last = (s, t)
    sums(*last)
    for s in range(B):
        after(dve, ch.te[s], f"{name}.turned", i)
        dve.tensor_copy(ch.pT[s][:, cols // 256:cols // P, :].rearrange("p c n -> p (c n)"),
                        ch.ps[s][:, cols:2 * cols]).then_inc(ch.dve[s].sem, ch.dve[s].one(f"{name}.kept"))


def cross_scalar_steps(name):
    return [f"{name}.exp0", f"{name}.exp1", f"{name}.kept"]


def cross_scalar(act, ch, name, i, cols):
    for s in range(B):
        for t in range(2):
            after(act, ch.dve[s], f"{name}.less{t}", i)
            sc = scores_of(ch, s, cols)[:, t]
            act.activation(sc, sc, ACT.Exp).then_inc(ch.act[s].sem, ch.act[s].one(f"{name}.exp{t}"))
    for s in range(B):
        after(act, ch.te[s], f"{name}.turned", i)
        act.activation(ch.pT[s][:, 0:cols // 256, :].rearrange("p c n -> p (c n)"), ch.ps[s][:, 0:cols],
                       ACT.Identity).then_inc(ch.act[s].sem, ch.act[s].one(f"{name}.kept"))


def cross_gpsimd(pool, ch, name, i, cols):
    heads = cols // S2
    for s in range(B):
        for t in range(2):
            after(pool, ch.dve[s], f"{name}.inverse{t}", i)
            sc = scores_of(ch, s, cols)[:, t].rearrange("p (h k) -> p h k", k=S2)
            pool.tensor_tensor(out=sc, in0=sc, in1=ch.total[s][:, t, 0:heads].unsqueeze(2).to_broadcast(
                [P, heads, S2]), op=ALU.mult).then_inc(ch.pool[s].sem, ch.pool[s].one(f"{name}.probs{t}"))


def add_vector(dve, ch, e, name, i, producer, s, dst=None):
    after(dve, ch.te[s], producer, i)
    x = tokens(e, s, i)
    dve.tensor_tensor(out=x if dst is None else dst, in0=ch.ps[s][:, 0:512].rearrange("p (t c) -> p t c", t=2),
                      in1=x, op=ALU.add).then_inc(ch.dve[s].sem, ch.dve[s].one(name))


def chain_loads0(nc, e, A, fb):
    rows = lambda n: A[n].rearrange("(k p) c -> p k c", p=P)
    w = e.w0 = Env()
    w.vec = {}
    w.m1, w.m1b, w.m2 = fb("mlp1_w", [P, KC, 1024]), fb("mlp1_b", [P, 8]), fb("mlp2_w", [P, 8, C])
    w.wu, w.wr, w.wn = (fb(n, [P, 4, C]) for n in ("w_u", "w_r", "w_n"))
    later_biases = []
    cols = {"ln2_g": "L0_xattn_ln2_w", "ln2_b": "L0_xattn_ln2_b", "ln3_g": "L0_xattn_ln3_w", "ln3_b": "L0_xattn_ln3_b",
            "st_g": "L1_xattn_g_state", "st_b": "L1_xattn_beta_state", "in_g": "L1_xattn_g_input",
            "in_b": "L1_xattn_beta_input", "r_b": "L1_xattn_b_r", "l2_g": "L2_xattn_ln1_g", "l2_b": "L2_xattn_ln1_b"}
    for n, src in enumerate(("L0_xattn_out_b", "L0_xattn_mlp2_b", "L1_xattn_b_u", "L1_xattn_b_n")):
        later_biases.append((e.biases0[:, n * C:(n + 1) * C], A[src].partition_broadcast(P)))
    reps = {"o_g": "L1_xattn_g_out", "o_b": "L1_xattn_beta_out"}
    loads = [(w.m1[:], rows("L0_xattn_mlp1_w")), (w.m1b[:], column(A["L0_xattn_mlp1_b"], 8)),
             (w.m2[:], rows("L0_xattn_mlp2_w")), (w.wu[:], rows("L1_xattn_W_u")), (w.wr[:], rows("L1_xattn_W_r")),
             (w.wn[:], rows("L1_xattn_W_n"))]
    for n, src in cols.items():
        w.vec[n] = fb(f"c0_{n}", [P, KC])
        loads.append((w.vec[n][:], column(A[src], KC)))
    for n, src in reps.items():
        w.vec[n] = fb(f"r0_{n}", [P, C])
        loads.append((w.vec[n][:], A[src].partition_broadcast(P)))
    return loads + later_biases


def part_chain0(nc, e):
    with ExitStack() as ctx:
        w = e.w0
        te_steps = ["n2.T", "ca.scores0", "ca.scores1", "ca.turned", "ca.out", "n3.T", "mlp.up", "mlp.down", "n4.T", "rt.scores",
                    "rt.turned", "rt.routed", "n5.T", "gates", "cand"]
        dve_steps = (norm_steps("n2") + cross_vector_steps("ca") + ["ca.x"] + norm_steps("n3")
                     + ["xc"] + norm_steps("n4") + ["rt.top", "rt.minus", "rt.inverse", "rt.probs"]
                     + norm_steps("n5") + ["reset"])
        act_steps = ["n2.hT", *cross_scalar_steps("ca"), "n3.hT", "mlp.gelu",
                     "x.T", "n4.hT", "rt.exp", "rt.kept", "n5.hT",
                     "r", "u", "tanh"]
        ch = Chain(nc, ctx, "c0", te_steps, dve_steps, act_steps,
                   ["n2.shifted", "n2.rstd", "ca.probs0", "ca.probs1", "n3.shifted", "n3.rstd", "n4.shifted",
                    "n4.rstd", "n5.shifted", "n5.rstd"], e.biases0.shape[1])
        tail = Tail(nc, ctx, ch, "c0_tail", norm_steps("n6") + ["out.x"],
                    ["cand.less", "cand.gated", "mixed", "n6.shifted", "n6.rstd"])
        PIECE = 1024
        ROWS_MADE = 2 + 4 * (e.biases0.shape[1] // PIECE)
        stT, inT, rT = ch.sb("stT", [P, KC, 256]), ch.sb("inT", [P, KC, 256]), ch.sb("rT", [P, KC, 256])
        u, cand = ch.sb("u", [P, 2, C]), ch.sb("cand", [P, 2, C])
        rp, rpT = ch.sb("rp", [P, 2, P]), ch.sb("rpT", [S2, 256])
        top, total = ch.sb("rtop", [P, 2]), ch.sb("rtotal", [P, 2])
        up = ch.pT
        tiles = lambda s, bank: ch.ps[s][:, 512 * bank:512 * (bank + 1)].rearrange("p (t c) -> p t c", t=2)
        rep = lambda ap: ap[:].unsqueeze(1).to_broadcast([P, 2, C])
        block = ctx.enter_context(nc.Block())

        @block.tensor
        def _(te):
            te.wait_ge(ch.rows_made, ROWS_MADE)

            def head(i):
                scores_tensor(te, ch, e, "ca", i, ch.hT, "n2.hT", e.m0, 1024, 4 * C,
                              lambda s: turn_step(te, ch, e, i, "n2", s))

            def emit(i, first, last):
                def turn4(s):
                    after(te, ch.dve[s], "n4.h", i)
                    turn_tensor(te, ch, e, ch.xc[s], s, 0)
                    turn_tensor(te, ch, e, ch.h[s], s, 1).then_inc(ch.te[s].sem, ch.te[s].one("n4.T"))

                def routing_scores(s):
                    after(te, ch.act[s], "x.T", i)
                    for t in range(2):
                        for k in range(KC):
                            ins = te.matmul(ch.ps[s][:, 1024 + t * S2:1024 + (t + 1) * S2],
                                            ch.xT[s][:, k, t * P:(t + 1) * P], e.tokT[:, k, s * S2:(s + 1) * S2],
                                            start=k == 0, stop=k == KC - 1)
                    ins.then_inc(ch.te[s].sem, ch.te[s].one("rt.scores"))

                def routing_turned(s):
                    after(te, ch.dve[s], "rt.probs", i)
                    for t in range(2):
                        ins = te.transpose(ch.ps[s][:, 1024 + t * P:1024 + (t + 1) * P], rp[s][:, t, :], e.ident[:])
                    ins.then_inc(ch.te[s].sem, ch.te[s].one("rt.turned"))

                def routed(s):
                    after(te, ch.act[s], "rt.kept", i)
                    for t in range(2):
                        ins = te.matmul(ch.ps[s][:, 1536 + t * C:1536 + (t + 1) * C], rpT[s][:, t * P:(t + 1) * P],
                                        e.tok[:, s, :], start=True, stop=True)
                    ins.then_inc(ch.te[s].sem, ch.te[s].one("rt.routed"))

                def gates(s, k0, src):
                    for t in range(2):
                        dst = ch.ps[s][:, 512 + t * C:512 + (t + 1) * C]
                        for k in range(2):
                            te.matmul(dst, src[s][:, k, t * P:(t + 1) * P], w.wu[:, k0 + k, :],
                                      start=k0 + k + t == 0, stop=False)
                        if k0:
                            add_bias(te, ch, dst, 2 * C, t == 1)
                    for f in range(KC):
                        for k in range(2):
                            ins = te.matmul(ch.ps[s][:, f * 256:(f + 1) * 256], w.wr[:, k0 + k, f * P:(f + 1) * P],
                                            src[s][:, k, :], start=k0 + k + f == 0, stop=k0 + k == 3 and f == KC - 1)
                    return ins

                if first:
                    head(0)
                cross_tensor(te, ch, e, "ca", i, e.vw0, 1024, 0)
                turn_step(te, ch, e, i, "n3", 0)
                for s in range(B):
                    after(te, ch.act[s], "n3.hT", i)
                    for f in range(8):
                        if s == 0 and f == 4:
                            turn_step(te, ch, e, i, "n3", 1)
                        for k in range(KC):
                            ins = te.matmul(ch.ps[s][:, 256 * f:256 * (f + 1)], w.m1[:, k, f * P:(f + 1) * P],
                                            ch.hT[s][:, k, :], start=k == 0, stop=k == KC - 1)
                    ins.then_inc(ch.te[s].sem, ch.te[s].one("mlp.up"))
                for s in range(B):
                    after(te, ch.act[s], "mlp.gelu", i)
                    for t in range(2):
                        for f in range(8):
                            te.matmul(ch.ps[s][:, t * C:(t + 1) * C], up[s][:, f, t * P:(t + 1) * P],
                                      w.m2[:, f, :], start=f == 0, stop=False)
                        ins = add_bias(te, ch, ch.ps[s][:, t * C:(t + 1) * C], C)
                        if t == 1:
                            ins.then_inc(ch.te[s].sem, ch.te[s].one("mlp.down"))
                        elif s == 1:
                            turn4(0)
                routing_scores(0)
                after(te, ch.act[0], "n4.hT", i)
                gates(0, 0, stT)
                turn4(1)
                routing_turned(0)
                routing_scores(1)
                routed(0)
                after(te, ch.act[1], "n4.hT", i)
                gates(1, 0, stT)
                routing_turned(1)
                turn_step(te, ch, e, i, "n5", 0, 2)
                routed(1)
                for s in range(B):
                    after(te, ch.act[s], "n5.hT", i)
                    gates(s, 2, inT).then_inc(ch.te[s].sem, ch.te[s].one("gates"))
                    if s == 0:
                        turn_step(te, ch, e, i, "n5", 1, 2)
                for s in range(B):
                    after(te, ch.dve[s], "reset", i)
                    for t in range(2):
                        for k, (src, c) in enumerate([(rT[s], 0), (rT[s], 1), (inT[s], 0), (inT[s], 1)]):
                            te.matmul(ch.ps[s][:, 1536 + t * C:1536 + (t + 1) * C],
                                      src[:, c, t * P:(t + 1) * P], w.wn[:, k, :], start=k == 0, stop=False)
                        ins = add_bias(te, ch, ch.ps[s][:, 1536 + t * C:1536 + (t + 1) * C], 3 * C)
                    ins.then_inc(ch.te[s].sem, ch.te[s].one("cand"))
                if not last:
                    head(i + 1)

            chain_blocks(te, emit)

        @block.vector
        def _(dve):
            for s in range(B):
                dve.memset(rp[s][:, :, S2:P], 0.0)
            assert bias_rows(dve, ch, e.biases0, PIECE) == ROWS_MADE

            def head(i):
                for s in range(B):
                    norm_vector(dve, ch, "n2", i, lambda s: tokens(e, s, i), streams=[s])

            def finish_block(i):
                mixed = lambda s: ch.xc[s][:]
                norm_vector(dve, tail, "n6", i, mixed, lambda s: after_spare(dve, tail, s, "mixed", i, tail.pool),
                            scaled=True)
                scaled_vector(dve, tail, "n6", i, mixed, w.vec["o_g"], w.vec["o_b"], lambda s: tokens(e, s, i), "out.x")

            def emit(i, first, last):
                one = lambda s, name: (ch.dve[s].sem, ch.dve[s].one(name))
                x = lambda s: tokens(e, s, i)
                if first:
                    head(0)
                cross_vector(dve, ch, "ca", i, 1024)
                if not first:
                    finish_block(i - 1)
                for s in range(B):
                    add_vector(dve, ch, e, "ca.x", i, "ca.out", s)
                    norm_vector(dve, ch, "n3", i, x, lambda s: after_spare(dve, ch, s, "ca.x", i), streams=[s])
                for s in range(B):
                    add_vector(dve, ch, e, "xc", i, "mlp.down", s, ch.xc[s][:])
                    norm_vector(dve, ch, "n4", i, lambda s: ch.xc[s][:], lambda s: after(dve, ch.dve[s], "xc", i),
                                streams=[s])
                for s in range(B):
                    after(dve, ch.te[s], "rt.scores", i)
                    dve.tensor_reduce(top[s][:], ch.ps[s][:, 1024:1024 + 2 * S2].rearrange("p (t k) -> p t k", t=2),
                                      AX.X, ALU.max).then_inc(*one(s, "rt.top"))
                    after(dve, ch.dve[s], "rt.top", i)
                    dve.tensor_scalar(top[s][:], top[s][:], -1.0 / 16, None, ALU.mult).then_inc(*one(s, "rt.minus"))
                    after(dve, ch.act[s], "rt.exp", i)
                    dve.reciprocal(total[s][:], total[s][:]).then_inc(*one(s, "rt.inverse"))
                    after(dve, ch.dve[s], "rt.inverse", i)
                    dve.tensor_tensor(out=rp[s][:, :, 0:S2], in0=rp[s][:, :, 0:S2],
                                      in1=total[s][:].unsqueeze(2).to_broadcast([P, 2, S2]),
                                      op=ALU.mult).then_inc(*one(s, "rt.probs"))
                for s in range(B):
                    norm_vector(dve, ch, "n5", i, lambda s: tiles(s, 3), lambda s: after(dve, ch.te[s], "rt.routed", i),
                                streams=[s])
                for s in range(B):
                    after(dve, ch.act[s], "r", i)
                    dve.tensor_tensor(out=rT[s][:], in0=rT[s][:], in1=stT[s][:], op=ALU.mult).then_inc(
                        *one(s, "reset"))
                if not last:
                    head(i + 1)
                else:
                    finish_block(i)

            chain_blocks(dve, emit)

        @block.scalar
        def _(act):
            one = lambda s, name: (ch.act[s].sem, ch.act[s].one(name))

            def head(i):
                for s in range(B):
                    after(act, ch.te[s], "n2.T", i)
                    turned_scalar(act, ch, s, 0, ch.hT[s], w.vec["ln2_g"], w.vec["ln2_b"]).then_inc(*one(s, "n2.hT"))

            def emit(i, first, last):
                if first:
                    head(0)
                cross_scalar(act, ch, "ca", i, 1024)
                for s in range(B):
                    after(act, ch.te[s], "n3.T", i)
                    turned_scalar(act, ch, s, 0, ch.hT[s], w.vec["ln3_g"], w.vec["ln3_b"]).then_inc(*one(s, "n3.hT"))
                for s in range(B):
                    after(act, ch.te[s], "mlp.up", i)
                    for f in range(8):
                        ins = act.activation(up[s][:, f, :], ch.ps[s][:, 256 * f:256 * (f + 1)], ACT.Gelu,
                                             bias=w.m1b[:, f:f + 1])
                    ins.then_inc(*one(s, "mlp.gelu"))

                def turned4(s):
                    after(act, ch.te[s], "n4.T", i)
                    turned_scalar(act, ch, s, 0, ch.xT[s]).then_inc(*one(s, "x.T"))
                    turned_scalar(act, ch, s, 1, stT[s], w.vec["st_g"], w.vec["st_b"]).then_inc(*one(s, "n4.hT"))

                def routing_exp(s):
                    after(act, ch.dve[s], "rt.minus", i)
                    for t in range(2):
                        ins = act.activation(rp[s][:, t, 0:S2], ch.ps[s][:, 1024 + t * S2:1024 + (t + 1) * S2], ACT.Exp,
                                             scale=1.0 / 16, bias=top[s][:, t:t + 1], accum_out=total[s][:, t:t + 1])
                    ins.then_inc(*one(s, "rt.exp"))

                def routing_kept(s):
                    after(act, ch.te[s], "rt.turned", i)
                    act.activation(rpT[s][:], ch.ps[s][0:S2, 1024:1024 + 256], ACT.Identity).then_inc(
                        *one(s, "rt.kept"))

                turned4(0)
                routing_exp(0)
                turned4(1)
                routing_kept(0)
                routing_exp(1)
                routing_kept(1)
                for s in range(B):
                    after(act, ch.te[s], "n5.T", i)
                    turned_scalar(act, ch, s, 2, inT[s], w.vec["in_g"], w.vec["in_b"]).then_inc(*one(s, "n5.hT"))
                for s in range(B):
                    after(act, ch.te[s], "gates", i)
                    for f in range(KC):
                        ins = act.activation(rT[s][:, f, :], ch.ps[s][:, f * 256:(f + 1) * 256],
                                             ACT.Sigmoid, bias=w.vec["r_b"][:, f:f + 1])
                    ins.then_inc(*one(s, "r"))
                    act.activation(u[s][:], tiles(s, 1), ACT.Sigmoid).then_inc(*one(s, "u"))
                for s in range(B):
                    after(act, ch.te[s], "cand", i)
                    act.activation(cand[s][:], tiles(s, 3), ACT.Tanh).then_inc(*one(s, "tanh"))
                if not last:
                    head(i + 1)

            chain_blocks(act, emit)

        @block.gpsimd
        def _(pool):
            pool.memset(ch.power[:], -0.5).then_inc(ch.power_set, 1)
            pool.wait_ge(ch.power_set, 1)

            def emit(i, first, last):
                if first:
                    norm_gpsimd(pool, ch, e, "n2", 0)
                cross_gpsimd(pool, ch, "ca", i, 1024)
                if not first:
                    norm_gpsimd(pool, tail, e, "n6", i - 1)
                for name in ("n3", "n4", "n5"):
                    norm_gpsimd(pool, ch, e, name, i)
                if not last:
                    norm_gpsimd(pool, ch, e, "n2", i + 1)
                for s in range(B):
                    after(pool, ch.act[s], "tanh", i)
                    pool.tensor_tensor(out=cand[s][:], in0=cand[s][:], in1=ch.xc[s][:], op=ALU.subtract).then_inc(
                        tail.pool[s].sem, tail.pool[s].one("cand.less"))
                for s in range(B):
                    after(pool, tail.pool[s], "cand.less", i)
                    pool.tensor_tensor(out=cand[s][:], in0=cand[s][:], in1=u[s][:], op=ALU.mult).then_inc(
                        tail.pool[s].sem, tail.pool[s].one("cand.gated"))
                for s in range(B):
                    after(pool, tail.pool[s], "cand.gated", i)
                    pool.tensor_tensor(out=ch.xc[s][:], in0=ch.xc[s][:], in1=cand[s][:], op=ALU.add).then_inc(
                        tail.pool[s].sem, tail.pool[s].one("mixed"))
                if last:
                    norm_gpsimd(pool, tail, e, "n6", i)

            chain_blocks(pool, emit)


def part_norm2(nc, e):
    with ExitStack() as ctx:
        w = e.w0
        sb = lambda n, s, d=F32: ctx.enter_context(nc.sbuf_tensor(n, s, d))
        sem = lambda n: ctx.enter_context(nc.semaphore(n))
        h = sb("h_all", [P, TILES, C])
        stats, moments, rstd = sb("stats_all", [P, TILES, 6]), sb("moments_all", [P, TILES, 2]), sb("rstd_all", [P, TILES])
        power = sb("power_all", [P, TILES])
        ps = [ctx.enter_context(nc.psum_tensor(f"n7_{i}", [P, 512], F32)) for i in range(8)]
        stats_made, moments_made, rstd_made, h_made, turned, kept = (
            sem(f"n7_{n}") for n in ("stats", "moments", "rstd", "h", "turned", "kept"))
        block = ctx.enter_context(nc.Block())

        @block.vector
        def _(dve):
            for t in range(TILES):
                ins = dve.bn_stats(stats[:, t, :], e.x[:, t, :])
                if t % 4 == 3:
                    ins.then_inc(stats_made, 1)
            for t in range(TILES):
                if t % 4 == 0:
                    dve.wait_ge(stats_made, t // 4 + 1)
                ins = dve.bn_aggr(moments[:, t, :], stats[:, t, :])
            ins.then_inc(moments_made, 1)
            dve.wait_ge(rstd_made, 3)
            for t in range(TILES):
                ins = dve.tensor_scalar(h[:, t, :], e.x[:, t, :], moments[:, t, 0:1], rstd[:, t:t + 1],
                                        ALU.subtract, ALU.mult)
                if t % 2:
                    ins.then_inc(h_made, 1)

        @block.gpsimd
        def _(pool):
            pool.memset(power[:], -0.5).then_inc(rstd_made, 1)
            pool.wait_ge(moments_made, 1)
            pool.tensor_tensor(out=rstd[:], in0=moments[:, :, 1], in1=e.eps[:].to_broadcast([P, TILES]),
                               op=ALU.add).then_inc(rstd_made, 1)
            pool.wait_ge(rstd_made, 2)
            pool.tensor_tensor(out=rstd[:], in0=rstd[:], in1=power[:], op=ALU.pow).then_inc(rstd_made, 1)

        @block.tensor
        def _(te):
            for i in range(8):
                te.wait_ge(h_made, i + 1)
                for c in range(KC):
                    for t in range(2):
                        ins = te.transpose(ps[i][:, (2 * c + t) * P:(2 * c + t + 1) * P],
                                           h[:, 2 * i + t, c * P:(c + 1) * P], e.ident[:])
                ins.then_inc(turned, 1)

        @block.scalar
        def _(act):
            for i in range(8):
                act.wait_ge(turned, i + 1)
                for c in range(KC):
                    act.activation(e.hT[:, c, i * 256:(i + 1) * 256], ps[i][:, c * 256:(c + 1) * 256],
                                   ACT.Identity, bias=w.vec["l2_b"][:, c:c + 1], scale=w.vec["l2_g"][:, c:c + 1])


def part_attention2(nc, e, A, b):
    with ExitStack() as ctx:
        sb = lambda n, s, d=F32: ctx.enter_context(nc.sbuf_tensor(f"{n}_b{b}", s, d))
        sem = lambda n: ctx.enter_context(nc.semaphore(f"{n}_b{b}"))
        two = range(2)
        PAIRS, U, KEPT = 8, 16, 3
        w_c = [[sb(f"w{n}{i}", [P, KC, P]) for n in "qkv"] for i in two]
        qf, kf = sb("q_full", [P, T]), sb("k_full", [P, T])
        q_hl = [[sb(f"q_hl{j}{i}", [P, T], F32R) for j in two] for i in two]
        k_hh = [[sb(f"k_hh{j}{i}", [P, T], F32R) for j in two] for i in two]
        q_m = [[sb(f"q_m{j}{i}", [65, T], F32R) for j in two] for i in two]
        k_l = [[sb(f"k_l{j}{i}", [65, T], F32R) for j in two] for i in two]
        v = [sb(f"v{i}", [P, TB, P]) for i in two]
        probs = [[sb(f"pr{j}{i}", [P, T]) for i in range(KEPT)] for j in two]
        total = [sb(f"sum{j}", [P, T]) for j in two]
        rden = sb("rden2", [P, T])
        part_max, row_max = sb("pmax", [P, 2, 2, TB]), sb("rmax", [P, 2, TB])
        max_row = sb("maxr", [16, P], F32R)
        ring = ctx.enter_context(nc.psum_tensor(f"ring_b{b}", [P, T], F32))
        s2 = [ctx.enter_context(nc.psum_tensor(f"sc{i}_b{b}", [P, T], F32)) for i in two]
        o = ctx.enter_context(nc.psum_tensor(f"o_b{b}", [P, T], F32))
        w_in = [sem("w_in0"), sem("w_in1")]
        dup_in, max_out, max_in = [sem("dup_in0"), sem("dup_in1")], sem("max_out2"), sem("max_in2")
        rows_set = sem("rows_set2")
        proj_made, proj_kept, split = sem("proj_made"), sem("proj_kept"), sem("split")
        s1_made, s1_max, max_made, max_turned, max_kept = (
            sem(n) for n in ("s1m", "s1x", "max_made2", "max_turned2", "max_kept2"))
        s2_made, exp_made, pv_made = sem("s2m"), sem("expm"), sem("pvm")
        sum_a, sum_b = sem("sum_a"), sem("sum_b")
        den_made, log_made, rden_made, a_made = sem("denm"), sem("logm"), sem("rdenm"), sem("am")
        CH = [(j, t, half) for j in two for t in range(TB) for half in two]
        N1 = len(CH)
        hT = e.hT[:, :, b * T:(b + 1) * T]
        halves = [slice(0, 512), slice(512, T)]
        hi, lo = (slice(0, 64), slice(64, P)), (slice(64, P), slice(0, 64))
        running = lambda cur: cur is not None and not (isinstance(cur, int) and cur == 0)

        def pairs(engine, emit):
            emit(None, 0, 1, 1)
            emit(0, 1, 0, 1)
            with engine.Fori(0, 2) as i:
                emit(2 * i + 1, 2 * i + 2, 1, i + 2)
                emit(2 * i + 2, 2 * i + 3, 0, i + 2)
            emit(5, 6, 1, 4)
            emit(6, 7, 0, 4)
            emit(7, None, 1, None)

        block = ctx.enter_context(nc.Block())

        @block.sync
        def _(sp):
            def load(pair, par):
                for tile, n in zip(w_c[par], ("sa_wq", "sa_wk", "sa_wv")):
                    src = A["L2_xattn_" + n].rearrange("(k p) (g f) -> p k g f", p=P, f=P)[:, :, ds(pair, 1), :]
                    sp.dma_start(tile[:], src.rearrange("p k o f -> p k (o f)")).then_inc(w_in[par], 16)

            load(0, 0)

            def emit(cur, nxt, par, loads):
                if nxt is None:
                    return
                new = 1 - par
                if not (isinstance(nxt, int) and nxt == PAIRS - 1):
                    if running(nxt):
                        sp.wait_ge(proj_made, 3 * nxt)
                    load(nxt + 1, par)
                for j in two:
                    if running(cur) and j == 0:
                        sp.wait_ge(s2_made, U * cur)
                    sp.wait_ge(split, 8 * nxt + 1 + j)
                    sp.dma_start(q_m[new][j][0:64].bitcast(F32), q_hl[new][j][hi[j]].bitcast(F32)).then_inc(
                        dup_in[new], 16)
                for j in two:
                    sp.wait_ge(split, 8 * nxt + 3 + j)
                    sp.dma_start(k_hh[new][j][lo[j]].bitcast(F32), k_hh[new][j][hi[j]].bitcast(F32)).then_inc(
                        dup_in[new], 16)
                sp.wait_ge(max_kept, nxt + 1)
                sp.dma_start(e.max_dram[new, 0:16], max_row[:].bitcast(F32)).then_inc(max_out, 16)
                sp.wait_ge(max_out, 16 * (nxt + 1))
                for j in two:
                    sp.dma_start(q_m[new][j][64:65].bitcast(F32),
                                 e.max_dram[new, 8 * j:8 * j + 8].rearrange("(o t) q -> o (t q)", o=1)
                                 ).then_inc(max_in, 16)

            pairs(sp, emit)

        @block.tensor
        def _(te):
            te.wait_ge(rows_set, 1)

            def emit(cur, nxt, par, loads):
                new = 1 - par
                if nxt is not None:
                    te.wait_ge(w_in[new], 48 * loads)
                    if running(cur):
                        te.wait_ge(log_made, cur)
                    elif cur is not None:
                        te.wait_ge(max_kept, 1)
                    for n in range(2):
                        if n == 1:
                            te.wait_ge(proj_kept, 3 * nxt + 1)
                        for half in halves:
                            for k in range(KC):
                                ins = te.matmul(ring[:, half], w_c[new][n][:, k, :], hT[:, k, half], start=k == 0,
                                                stop=k == KC - 1)
                        ins.then_inc(proj_made, 1)
                    te.wait_ge(proj_kept, 3 * nxt + 2)
                    for t in range(TB):
                        for k in range(KC):
                            ins = te.matmul(ring[:, t * P:(t + 1) * P], hT[:, k, t * P:(t + 1) * P],
                                            w_c[new][2][:, k, :], start=k == 0, stop=k == KC - 1)
                    ins.then_inc(proj_made, 1)

                    def chunk(i):
                        j, t, half = CH[i]
                        if i < 2:
                            te.wait_ge(proj_kept, 3 * nxt + 3)
                        else:
                            te.wait_ge(s1_max, N1 * nxt + i - 1)
                        te.matmul(ring[:, halves[i % 2]], q_hl[new][j][:, t * P:(t + 1) * P],
                                  k_hh[new][j][:, halves[half]], start=True, stop=True).then_inc(s1_made, 1)

                def ready():
                    te.wait_ge(split, 8 * nxt + 8)
                    te.wait_ge(dup_in[new], 64 * loads)

                if cur is None:
                    ready()
                    for i in range(N1):
                        chunk(i)
                else:
                    def unit(u):
                        kt, j = divmod(u, 2)
                        keys = slice(kt * P, (kt + 1) * P)
                        if u >= 2 or running(cur):
                            te.wait_ge(exp_made, U * cur + u - 1 if u >= 2 else U * cur)
                        for half in halves:
                            te.matmul(s2[u % 2][:, half], k_hh[par][j][:, keys], q_hl[par][j][:, half],
                                      start=True, stop=False)
                            ins = te.matmul(s2[u % 2][:, half], k_l[par][j][:, keys], q_m[par][j][:, half],
                                            start=False, stop=True)
                        ins.then_inc(s2_made, 1)

                    def values(kt):
                        te.wait_ge(exp_made, U * cur + 2 * kt + 2)
                        if kt == 0 and running(cur):
                            te.wait_ge(a_made, cur)
                        for half in halves:
                            for j in two:
                                ins = te.matmul(o[64 * j:64 * j + 64, half], v[par][:, kt, 64 * j:64 * j + 64],
                                                probs[j][kt % KEPT][:, half], start=kt == 0, stop=kt == TB - 1)
                        ins.then_inc(pv_made, 1)

                    te.wait_ge(max_in, 32 * (cur + 1))
                    for u in range(U):
                        unit(u)
                        if u % 2 and u >= 3:
                            values(u // 2 - 1)
                        if nxt is not None:
                            if u == 0:
                                ready()
                            chunk(2 * u)
                            chunk(2 * u + 1)
                    values(TB - 1)
                if nxt is not None:
                    te.wait_ge(max_made, nxt + 1)
                    te.transpose(ring[0:16, 0:P], row_max[:].rearrange("p j t -> p (j t)"),
                                 e.ident[:]).then_inc(max_turned, 1)
                if cur is not None:
                    te.wait_ge(sum_a, 7 * (cur + 1))
                    te.wait_ge(sum_b, 7 * (cur + 1))
                    te.wait_ge(max_kept, nxt + 1 if nxt is not None else PAIRS)
                    for half in halves:
                        for j in two:
                            ins = te.matmul(ring[64 * j:64 * j + 64, half], e.ones[:], total[j][:, half],
                                            start=True, stop=True)
                    ins.then_inc(den_made, 1)

            pairs(te, emit)

        def sum_step(engine, j, done, cur, kt):
            engine.wait_ge(exp_made, U * cur + 2 * kt + 1 + j)
            if kt == 1:
                if running(cur):
                    engine.wait_ge(den_made, cur)
            else:
                engine.wait_ge(done, 7 * cur + kt - 1)
            other = probs[j][0] if kt == 1 else total[j]
            engine.tensor_tensor(out=total[j][:], in0=other[:], in1=probs[j][kt % KEPT][:],
                                 op=ALU.add).then_inc(done, 1)

        @block.gpsimd
        def _(pool):
            def emit(cur, nxt, par, loads):
                if cur is not None:
                    for kt in range(1, TB):
                        sum_step(pool, 0, sum_a, cur, kt)

            pairs(pool, emit)

        @block.vector
        def _(dve):
            for i in two:
                for j in two:
                    ins = dve.memset(k_l[i][j][64:65].bitcast(F32), 1.0)
            ins.then_inc(rows_set, 1)

            def emit(cur, nxt, par, loads):
                new = 1 - par
                if nxt is not None:
                    for n, (src, dst) in enumerate(((qf, q_hl), (kf, k_hh))):
                        dve.wait_ge(proj_kept, 3 * nxt + 1 + n)
                        for j in two:
                            dve.tensor_copy(dst[new][j][hi[j]], src[hi[j]]).then_inc(split, 1)
                    for n, (src, high, dst) in enumerate(((qf, q_hl, q_hl), (kf, k_hh, k_l))):
                        for j in two:
                            dve.wait_ge(split, 8 * nxt + 2 * n + j + 1)
                            rows = lo[j] if n == 0 else slice(0, 64)
                            dve.tensor_tensor(out=dst[new][j][rows], in0=src[hi[j]],
                                              in1=high[new][j][hi[j]].bitcast(F32), op=ALU.subtract
                                              ).then_inc(split, 1)

                def reduce(i):
                    j, t, half = CH[i]
                    dve.wait_ge(s1_made, N1 * nxt + i + 1)
                    dve.tensor_reduce(part_max[:, half, j, t:t + 1], ring[:, halves[i % 2]], AX.X,
                                      ALU.max).then_inc(s1_max, 1)

                for u in range(U):
                    if nxt is not None:
                        reduce(2 * u)
                        reduce(2 * u + 1)
                    if cur is not None and u % 2 and u >= 5:
                        sum_step(dve, 1, sum_b, cur, u // 2 - 1)
                if nxt is not None:
                    dve.wait_ge(s1_max, N1 * nxt + N1)
                    if cur is not None:
                        dve.wait_ge(max_turned, nxt)
                    dve.tensor_tensor(out=row_max[:], in0=part_max[:, 0], in1=part_max[:, 1],
                                      op=ALU.max).then_inc(max_made, 1)
                if cur is not None:
                    sum_step(dve, 1, sum_b, cur, TB - 1)
                    dve.wait_ge(rden_made, cur + 1)
                    dve.wait_ge(pv_made, TB * (cur + 1))
                    dve.tensor_tensor(out=e.aT2[:, ds(cur, 1), :].rearrange("p o t -> p (o t)"), in0=o[:],
                                      in1=rden[:], op=ALU.mult).then_inc(a_made, 1)

            pairs(dve, emit)

        @block.scalar
        def _(act):
            def emit(cur, nxt, par, loads):
                new = 1 - par
                if nxt is not None:
                    for n, (dst, scale) in enumerate(((qf, 0.125), (kf, 1.0))):
                        act.wait_ge(proj_made, 3 * nxt + 1 + n)
                        if cur is not None:
                            act.wait_ge(split, 8 * nxt - 2 + 2 * n)
                        act.activation(dst[:], ring[:], ACT.Identity, scale=scale).then_inc(proj_kept, 1)
                    act.wait_ge(proj_made, 3 * nxt + 3)
                    if running(cur):
                        act.wait_ge(pv_made, TB * cur)
                    act.activation(v[new][:].rearrange("p t f -> p (t f)"), ring[:],
                                   ACT.Identity).then_inc(proj_kept, 1)
                if cur is not None:
                    for u in range(U):
                        kt, j = divmod(u, 2)
                        act.wait_ge(s2_made, U * cur + u + 1)
                        if kt >= KEPT:
                            act.wait_ge(pv_made, TB * cur + kt - KEPT + 1)
                            act.wait_ge((sum_a, sum_b)[j], 7 * cur + max(kt - KEPT, 1))
                        elif running(cur):
                            act.wait_ge(pv_made, TB * cur)
                            act.wait_ge((sum_a, sum_b)[j], 7 * cur)
                        act.activation(probs[j][kt % KEPT][:], s2[u % 2][:], ACT.Exp).then_inc(exp_made, 1)
                if nxt is not None:
                    act.wait_ge(max_turned, nxt + 1)
                    if cur is not None:
                        act.wait_ge(max_out, 16 * nxt)
                    act.activation(max_row[:], ring[0:16, 0:P], ACT.Identity, scale=-1.0).then_inc(max_kept, 1)
                if cur is not None:
                    act.wait_ge(den_made, cur + 1)
                    if running(cur):
                        act.wait_ge(a_made, cur)
                    act.activation(rden[:], ring[:], ACT.Ln).then_inc(log_made, 1)
                    act.wait_ge(log_made, cur + 1)
                    act.activation(rden[:], rden[:], ACT.Exp, scale=-1.0).then_inc(rden_made, 1)

            pairs(act, emit)


def part_project2(nc, e, b):
    with ExitStack() as ctx:
        ps = [ctx.enter_context(nc.psum_tensor(f"wo{i}_b{b}", [P, 2, C], F32)) for i in range(4)]
        made, added = (ctx.enter_context(nc.semaphore(f"wo_{n}_b{b}")) for n in ("made", "added"))
        block = ctx.enter_context(nc.Block())

        @block.tensor
        def _(te):
            for u in range(TB // 2):
                for i in range(2):
                    t = 2 * u + i
                    for g in range(8):
                        ins = te.matmul(ps[u][:, i, :], e.aT2[:, g, t * P:(t + 1) * P], e.wo_w[:, g, :],
                                        start=g == 0, stop=g == 7)
                ins.then_inc(made, 1)

        @block.vector
        def _(dve):
            x = e.x[:, b * TB:(b + 1) * TB, :]
            dve.tensor_tensor(out=x, in0=x, in1=e.wo_brep[:].unsqueeze(1).to_broadcast([P, TB, C]),
                              op=ALU.add).then_inc(added, 1)
            dve.wait_ge(added, 1)
            for u in range(TB // 2):
                dve.wait_ge(made, u + 1)
                tile = x[:, 2 * u:2 * u + 2, :]
                dve.tensor_tensor(out=tile, in0=ps[u][:], in1=tile, op=ALU.add).then_inc(added, 1)


def part_context2(nc, e, A, later):
    with ExitStack() as ctx:
        sb = lambda n, s, d=F32: ctx.enter_context(nc.sbuf_tensor(n, s, d))
        sem = lambda n: ctx.enter_context(nc.semaphore(n))
        F3 = 16
        mask3 = sb("mask3", [P, B, S2], mybir.dt.int32)
        head64 = sb("head64", [P, 2])
        wq = [sb(f"wq{i}", [P, KC, 1024]) for i in range(2)]
        wk, wv = ([sb(f"w{n}_{i}", [96, 2, 1024]) for i in range(2)] for n in "kv")
        wo = [sb(f"wo{i}", [P, 8, C]) for i in range(2)]
        wqT = sb("wqT", [P, 8, C])
        kT, vT = sb("kT2", [P, 8, P]), sb("vT2", [P, 8, P])
        kbd, vbd = sb("kbd2", [P, B, 8, 2, S2]), sb("vbd2", [P, B, 8, 2, S2])
        ps = [ctx.enter_context(nc.psum_tensor(f"ctx{i}", [P, 512], F32)) for i in range(8)]
        w_in = [sem(f"w2_in{i}") for i in range(3)]
        later_in, mask_in = sem("chain2_w_in"), sem("mask3_in")
        names = []
        for g in range(3):
            names += [f"{g}.wqT{i}" for i in range(4)] + [f"{g}.kT{i}" for i in range(2)] + [f"{g}.vT{i}" for i in range(2)]
            if g == 0:
                names += [f"{g}.m{b}{d}{h}" for b in range(B) for d in range(KC) for h in range(2)]
                names += [f"{g}.vw{b}{i}" for b in range(B) for i in range(4)]
            else:
                names += [f"{g}.m{d}" for d in range(KC)] + [f"{g}.vw{b}" for b in range(B)]
        pe, ev = Steps(sem("ctx2_tensor"), names), Steps(sem("ctx2_scalar"), names)
        dv = Steps(sem("ctx2_vector"), ["mask", "kbd", "vbd"])
        gp = Steps(sem("ctx2_gpsimd"), ["ones", "first", "second"])
        bank = lambda n: ps[names.index(n) % 8]
        block = ctx.enter_context(nc.Block())

        @block.sync
        def _(sp):
            sp.dma_start(mask3[:], A["mask_BxS2_if1"].rearrange("b s -> (b s)").partition_broadcast(P)
                         .rearrange("p (b s) -> p b s", b=B)).then_inc(mask_in, 16)
            for g in range(3):
                if g == 2:
                    sp.wait_ge(ev.sem, ev.value("0.vw13"))
                names4 = (("L2_xattn_ca_wq", "L2_xattn_ca_wk", "L2_xattn_ca_wv", "L2_xattn_ca_wo") if g == 0 else
                          ("L3_xattn_Wq", "L3_xattn_Wk", "L3_xattn_Wv", "L3_xattn_Wo"))
                c0 = 1024 * max(g - 1, 0)
                for tile, n, p in ((wq, names4[0], P), (wk, names4[1], 96), (wv, names4[2], 96)):
                    sp.dma_start(tile[g % 2][:], A[n].rearrange("(k p) c -> p k c", p=p)[:, :, c0:c0 + 1024]
                                 ).then_inc(w_in[g], 16)
                sp.dma_start(wo[g % 2][:], A[names4[3]][c0:c0 + 1024, :].rearrange("(k p) c -> p k c", p=P)
                             ).then_inc(w_in[g], 16)
            for dst, src in later:
                sp.dma_start(dst, src).then_inc(later_in, 16)
            sp.wait_ge(later_in, 16 * len(later))

        @block.gpsimd
        def _(pool):
            pool.memset(head64[:], 1.0).then_inc(gp.sem, gp.one("ones"))
            pool.wait_ge(gp.sem, gp.value("ones"))
            pool.affine_select(out=head64[:], in_=head64[:], compare_op=ALU.is_ge, fill=0.0, base=0,
                               pattern=[[-64, 2]], channel_multiplier=1).then_inc(gp.sem, gp.one("first"))
            pool.wait_ge(gp.sem, gp.value("first"))
            pool.affine_select(out=head64[:], in_=head64[:], compare_op=ALU.is_ge, fill=0.0, base=63,
                               pattern=[[64, 2]], channel_multiplier=-1).then_inc(gp.sem, gp.one("second"))

        @block.vector
        def _(dve):
            dve.wait_ge(mask_in, 16)
            for b in range(B):
                ins = dve.tensor_scalar(e.bias3[:, b], mask3[:, b].unsqueeze(1).to_broadcast([P, 8, S2]), 0.0, MASKED,
                                        ALU.is_equal, ALU.mult)
            ins.then_inc(dv.sem, dv.one("mask"))
            dve.wait_ge(gp.sem, gp.value("second"))
            head_rep = head64[:].unsqueeze(2).to_broadcast([P, 2, S2])
            for name, dst, src in (("kbd", kbd, kT), ("vbd", vbd, vT)):
                dve.wait_ge(ev.sem, ev.value("0." + name[0] + "T1"))
                for b in range(B):
                    for c in range(8):
                        rep = src[:, c, b * S2:(b + 1) * S2].unsqueeze(1).to_broadcast([P, 2, S2])
                        ins = dve.tensor_tensor(out=dst[:, b, c], in0=rep, in1=head_rep, op=ALU.mult)
                ins.then_inc(dv.sem, dv.one(name))

        @block.scalar
        def _(act):
            def copy(name, dst, src, scale=1.0):
                act.wait_ge(pe.sem, pe.value(name))
                act.activation(dst, src, ACT.Identity, scale=scale).then_inc(ev.sem, ev.one(name))

            for g in range(3):
                if g == 1:
                    act.wait_ge(dv.sem, dv.value("vbd"))
                for i in range(4):
                    copy(f"{g}.wqT{i}", wqT[:, 2 * i:2 * i + 2, :], bank(f"{g}.wqT{i}")[:].rearrange(
                        "p (k c) -> p k c", k=2))
                for n, dst in (("k", kT), ("v", vT)):
                    for i in range(2):
                        copy(f"{g}.{n}T{i}", dst[:, 4 * i:4 * i + 4, :].rearrange("p k c -> p (k c)"),
                             bank(f"{g}.{n}T{i}")[:])
                if g == 0:
                    for b in range(B):
                        for d in range(KC):
                            for h in range(2):
                                copy(f"0.m{b}{d}{h}", e.m2[:, b, d, h * 512:(h + 1) * 512], bank(f"0.m{b}{d}{h}")[:],
                                     0.125)
                    for b in range(B):
                        for i in range(4):
                            copy(f"0.vw{b}{i}", e.vw2[:, b, 2 * i:2 * i + 2, :],
                                 bank(f"0.vw{b}{i}")[:].rearrange("p (k c) -> p k c", k=2))
                else:
                    heads = slice((g - 1) * 256, g * 256)
                    for d in range(KC):
                        n = f"{g}.m{d}"
                        act.wait_ge(pe.sem, pe.value(n))
                        for b in range(B):
                            src = bank(n)[:].rearrange("p (h b s) -> p b h s", b=B, s=S2)[:, b]
                            ins = act.activation(e.m3[:, b, d, heads].rearrange("p (h s) -> p h s", s=S2), src,
                                                 ACT.Identity, scale=0.0625)
                        ins.then_inc(ev.sem, ev.one(n))
                    for b in range(B):
                        copy(f"{g}.vw{b}", e.vw3[:, b, 2 * (g - 1):2 * g, :],
                             bank(f"{g}.vw{b}")[:].rearrange("p (k c) -> p k c", k=2))

        @block.tensor
        def _(te):
            def made(name, ins):
                ins.then_inc(pe.sem, pe.one(name))

            def free(name):
                if names.index(name) >= 8:
                    te.wait_ge(ev.sem, names.index(name) - 7)

            for g in range(3):
                te.wait_ge(w_in[g], 64)
                for i in range(4):
                    n = f"{g}.wqT{i}"
                    free(n)
                    for c in range(2):
                        for d in range(KC):
                            ins = te.transpose(bank(n)[:, (2 * c + d) * P:(2 * c + d + 1) * P],
                                               wq[g % 2][:, d, (2 * i + c) * P:(2 * i + c + 1) * P], e.ident[:])
                    ins.then_inc(pe.sem, pe.one(n))
                for letter, w in (("k", wk), ("v", wv)):
                    for i in range(2):
                        n = f"{g}.{letter}T{i}"
                        free(n)
                        for c in range(4):
                            for k in range(2):
                                ins = te.matmul(bank(n)[:, c * P:(c + 1) * P],
                                                w[g % 2][:, k, (4 * i + c) * P:(4 * i + c + 1) * P], e.ctxT[:, k, :],
                                                start=k == 0, stop=k == 1)
                        ins.then_inc(pe.sem, pe.one(n))
                if g == 0:
                    te.wait_ge(dv.sem, dv.value("vbd"))
                    for b in range(B):
                        for d in range(KC):
                            for h in range(2):
                                n = f"0.m{b}{d}{h}"
                                free(n)
                                for c in range(4):
                                    ins = te.matmul(bank(n)[:, c * P:(c + 1) * P], wqT[:, 4 * h + c, d * P:(d + 1) * P],
                                                    kbd[:, b, 4 * h + c].rearrange("p h s -> p (h s)"),
                                                    start=True, stop=True)
                                ins.then_inc(pe.sem, pe.one(n))
                    for b in range(B):
                        for i in range(4):
                            n = f"0.vw{b}{i}"
                            free(n)
                            for c in range(2):
                                ins = te.matmul(bank(n)[:, c * C:(c + 1) * C],
                                                vbd[:, b, 2 * i + c].rearrange("p h s -> p (h s)"),
                                                wo[0][:, 2 * i + c, :], start=True, stop=True)
                            ins.then_inc(pe.sem, pe.one(n))
                else:
                    te.wait_ge(ev.sem, ev.value(f"{g}.vT1"))
                    for d in range(KC):
                        n = f"{g}.m{d}"
                        free(n)
                        for h in range(4):
                            for c in range(2):
                                ins = te.matmul(bank(n)[:, h * P:(h + 1) * P], wqT[:, 2 * h + c, d * P:(d + 1) * P],
                                                kT[:, 2 * h + c, :], start=c == 0, stop=c == 1)
                        ins.then_inc(pe.sem, pe.one(n))
                    for b in range(B):
                        n = f"{g}.vw{b}"
                        free(n)
                        for h in range(4):
                            for c in range(2):
                                ins = te.matmul(bank(n)[64 * (h % 2):64 * (h % 2) + 64, (h // 2) * C:(h // 2 + 1) * C],
                                                vT[:, 2 * h + c, b * S2:(b + 1) * S2], wo[g % 2][:, 2 * h + c, :],
                                                start=c == 0, stop=c == 1)
                        ins.then_inc(pe.sem, pe.one(n))


def chain_loads2(nc, e, A, bb):
    rows = lambda n: A[n].rearrange("(k p) c -> p k c", p=P)
    w = e.w2 = Env()
    w.vec = {}
    w.f1, w.f1b, w.f2 = bb("ff1_w", [P, KC, 2048]), bb("ff1_b", [P, 16]), bb("ff2_w", [P, 8, C])
    loads = [(w.f1[:], rows("L2_xattn_ff_w1")), (w.f1b[:], column(A["L2_xattn_ff_b1"], 16)),
             (w.f2[:], rows("L2_xattn_ff_w2"))]
    for n, src in {"ln2_g": "L2_xattn_ln2_g", "ln2_b": "L2_xattn_ln2_b", "ln3_g": "L2_xattn_ln3_g",
                   "ln3_b": "L2_xattn_ln3_b"}.items():
        w.vec[n] = bb(f"c2_{n}", [P, KC])
        loads.append((w.vec[n][:], column(A[src], KC)))
    later_biases = [(e.biases2[:, n * C:(n + 1) * C], A[src].partition_broadcast(P))
                    for n, src in enumerate(("L2_xattn_ca_bo", "L2_xattn_ff_b2"))]
    for n, src in {"gamma": "L3_xattn_gamma",
                   "beta": "L3_xattn_beta"}.items():
        w.vec[n] = bb(f"r2_{n}", [P, C])
        loads.append((w.vec[n][:], A[src].partition_broadcast(P)))
    return loads + later_biases


def part_chain2(nc, e, out):
    with ExitStack() as ctx:
        w = e.w2
        te_steps = ["n8.T", "cb.scores0", "cb.scores1", "cb.turned", "cb.out", "n9.T", "ff.up0", "ff.up1", "ff.down", "x.T",
                    "cc.scores0", "cc.scores1", "cc.turned", "cc.out"]
        dve_steps = (norm_steps("n8") + cross_vector_steps("cb") + ["cb.x"] + norm_steps("n9")
                     + ["ff.gated0", "ff.gated1", "xc"] + cross_vector_steps("cc"))
        act_steps = ["n8.hT", *cross_scalar_steps("cb"), "n9.hT", "ff.gelu0",
                     "ff.gelu1", "x.T", *cross_scalar_steps("cc")]
        ch = Chain(nc, ctx, "c2", te_steps, dve_steps, act_steps,
                   ["n8.shifted", "n8.rstd", "cb.probs0", "cb.probs1", "n9.shifted", "n9.rstd", "cc.probs0", "cc.probs1"], e.biases2.shape[1])
        tail = Tail(nc, ctx, ch, "c2_tail", ["x.last"] + norm_steps("n10") + ["out"], ["n10.shifted", "n10.rstd"])
        PIECE = 512
        ROWS_MADE = 2 + 4 * (e.biases2.shape[1] // PIECE)
        gate, inner = ch.sb("gate", [P, 4, 256]), ch.pT
        result = ch.sb("result", [P, 2, C])
        stored = [ctx.enter_context(nc.semaphore(f"out_stored{s}")) for s in range(B)]
        tiles = lambda s, bank: ch.ps[s][:, 512 * bank:512 * (bank + 1)].rearrange("p (t c) -> p t c", t=2)
        rep = lambda ap: ap[:].unsqueeze(1).to_broadcast([P, 2, C])
        block = ctx.enter_context(nc.Block())

        @block.sync
        def _(sp):
            with sp.Fori(0, BLOCKS) as i:
                for s in range(B):
                    after(sp, tail.dve[s], "out", i)
                    dst = out[s].rearrange("(i t p) c -> p i t c", p=P, t=2)[:, ds(i, 1)]
                    sp.dma_start(dst.rearrange("p o t c -> p (o t) c"), result[s][:]).then_inc(stored[s], 16)
            for s in range(B):
                sp.wait_ge(stored[s], 16 * BLOCKS)

        @block.tensor
        def _(te):
            te.wait_ge(ch.rows_made, ROWS_MADE)

            def head(i):
                scores_tensor(te, ch, e, "cb", i, ch.hT, "n8.hT", e.m2, 1024, None, lambda s: None)

            def emit(i, first, last):
                def turn_x(s):
                    after(te, ch.dve[s], "xc", i)
                    turn_tensor(te, ch, e, ch.xc[s], s, 0).then_inc(ch.te[s].sem, ch.te[s].one("x.T"))

                if first:
                    for s in range(B):
                        turn_step(te, ch, e, 0, "n8", s, 3)
                    head(0)
                cross_tensor(te, ch, e, "cb", i, e.vw2, 1024, 0)
                turn_step(te, ch, e, i, "n9", 0)
                for half in range(2):
                    for s in range(B):
                        if half == 0:
                            after(te, ch.act[s], "n9.hT", i)
                        else:
                            after(te, ch.dve[s], "ff.gated0", i)
                        for part in range(2):
                            if half == 0 and s == 0 and part == 1:
                                turn_step(te, ch, e, i, "n9", 1)
                            for f in range(4):
                                chunk = 8 * part + 4 * half + f
                                for k in range(KC):
                                    ins = te.matmul(ch.ps[s][:, 1024 * part + 256 * f:1024 * part + 256 * (f + 1)],
                                                    w.f1[:, k, chunk * P:(chunk + 1) * P], ch.hT[s][:, k, :],
                                                    start=k == 0, stop=k == KC - 1)
                        ins.then_inc(ch.te[s].sem, ch.te[s].one(f"ff.up{half}"))
                for s in range(B):
                    after(te, ch.dve[s], "ff.gated1", i)
                    for t in range(2):
                        for f in range(8):
                            te.matmul(ch.ps[s][:, t * C:(t + 1) * C], inner[s][:, f, t * P:(t + 1) * P],
                                      w.f2[:, f, :], start=f == 0, stop=False)
                        ins = add_bias(te, ch, ch.ps[s][:, t * C:(t + 1) * C], C)
                    ins.then_inc(ch.te[s].sem, ch.te[s].one("ff.down"))
                scores_tensor(te, ch, e, "cc", i, ch.xT, "x.T", e.m3, 512, 2 * C, turn_x)
                cross_tensor(te, ch, e, "cc", i, e.vw3, 512, None)
                if not last:
                    for s in range(B):
                        turn_step(te, ch, e, i + 1, "n8", s, 3)
                    for s in range(B):
                        after(te, tail.dve[s], "x.last", i)
                    head(i + 1)

            chain_blocks(te, emit)

        @block.vector
        def _(dve):
            assert bias_rows(dve, ch, e.biases2, PIECE) == ROWS_MADE

            def head(i):
                for s in range(B):
                    norm_vector(dve, ch, "n8", i, lambda s: tokens(e, s, i), streams=[s])

            def finish_block(i, waits):
                last = lambda s: ch.xc[s][:]
                norm_vector(dve, tail, "n10", i, last, lambda s: after_spare(dve, tail, s, "x.last", i), scaled=True)
                if waits:
                    for s in range(B):
                        dve.wait_ge(stored[s], 16 * i)
                scaled_vector(dve, tail, "n10", i, last, w.vec["gamma"], w.vec["beta"], lambda s: result[s][:], "out")

            def emit(i, first, last):
                one = lambda s, name: (ch.dve[s].sem, ch.dve[s].one(name))
                x = lambda s: tokens(e, s, i)
                if first:
                    head(0)
                cross_vector(dve, ch, "cb", i, 1024)
                if not first:
                    finish_block(i - 1, not isinstance(i, int) or i > 1)
                for s in range(B):
                    add_vector(dve, ch, e, "cb.x", i, "cb.out", s)
                    norm_vector(dve, ch, "n9", i, x, lambda s: after_spare(dve, ch, s, "cb.x", i), streams=[s])
                for half in range(2):
                    for s in range(B):
                        after(dve, ch.act[s], f"ff.gelu{half}", i)
                        for f in range(4):
                            chunk = 4 * half + f
                            ins = dve.scalar_tensor_tensor(
                                out=inner[s][:, chunk, :], in0=ch.ps[s][:, 256 * f:256 * (f + 1)],
                                scalar=w.f1b[:, chunk:chunk + 1], in1=gate[s][:, f, :], op0=ALU.add, op1=ALU.mult)
                        ins.then_inc(*one(s, f"ff.gated{half}"))
                for s in range(B):
                    add_vector(dve, ch, e, "xc", i, "ff.down", s, ch.xc[s][:])
                cross_vector(dve, ch, "cc", i, 512)
                if not last:
                    head(i + 1)
                for s in range(B):
                    after(dve, ch.te[s], "cc.out", i)
                    dve.tensor_tensor(out=ch.xc[s][:], in0=tiles(s, 0), in1=ch.xc[s][:], op=ALU.add).then_inc(
                        tail.dve[s].sem, tail.dve[s].one("x.last"))
                if last:
                    finish_block(i, True)

            chain_blocks(dve, emit)

        @block.scalar
        def _(act):
            one = lambda s, name: (ch.act[s].sem, ch.act[s].one(name))

            def head(i):
                for s in range(B):
                    after(act, ch.te[s], "n8.T", i)
                    turned_scalar(act, ch, s, 3, ch.hT[s], w.vec["ln2_g"], w.vec["ln2_b"]).then_inc(*one(s, "n8.hT"))

            def emit(i, first, last):
                if first:
                    head(0)
                cross_scalar(act, ch, "cb", i, 1024)
                for s in range(B):
                    after(act, ch.te[s], "n9.T", i)
                    turned_scalar(act, ch, s, 0, ch.hT[s], w.vec["ln3_g"], w.vec["ln3_b"]).then_inc(*one(s, "n9.hT"))
                for half in range(2):
                    for s in range(B):
                        after(act, ch.te[s], f"ff.up{half}", i)
                        for f in range(4):
                            ins = act.activation(gate[s][:, f, :], ch.ps[s][:, 1024 + 256 * f:1024 + 256 * (f + 1)],
                                                 ACT.Gelu, bias=w.f1b[:, 8 + 4 * half + f:9 + 4 * half + f])
                        ins.then_inc(*one(s, f"ff.gelu{half}"))
                for s in range(B):
                    after(act, ch.te[s], "x.T", i)
                    turned_scalar(act, ch, s, 0, ch.xT[s]).then_inc(*one(s, "x.T"))
                cross_scalar(act, ch, "cc", i, 512)
                if not last:
                    head(i + 1)

            chain_blocks(act, emit)

        @block.gpsimd
        def _(pool):
            pool.memset(ch.power[:], -0.5).then_inc(ch.power_set, 1)
            pool.wait_ge(ch.power_set, 1)

            def emit(i, first, last):
                if first:
                    norm_gpsimd(pool, ch, e, "n8", 0)
                cross_gpsimd(pool, ch, "cb", i, 1024)
                if not first:
                    norm_gpsimd(pool, tail, e, "n10", i - 1)
                norm_gpsimd(pool, ch, e, "n9", i)
                cross_gpsimd(pool, ch, "cc", i, 512)
                if not last:
                    norm_gpsimd(pool, ch, e, "n8", i + 1)
                else:
                    norm_gpsimd(pool, tail, e, "n10", i)

            chain_blocks(pool, emit)


def program(nc, A, out):
    with ExitStack() as ctx:
        ctx.enter_context(nc.allow_non_contiguous_dma(reason="vectors are loaded as columns"))
        e = Env()
        sb = lambda n, s, d=F32: ctx.enter_context(nc.sbuf_tensor(n, s, d))
        e.x = sb("x", [P, TILES, C])
        e.ident, e.ident_bf = sb("ident", [P, P]), sb("ident_bf", [P, P], BF16)
        e.eps = sb("eps", [P, 1])
        e.ones = sb("ones", [P, 64])
        e.tok, e.tokT = sb("tok", [S2, B, C]), sb("tokT", [P, KC, P])
        e.ctxT = sb("ctxT", [96, 2, P])
        attn = ctx.enter_context(ExitStack())
        ab = lambda n, s, d=F32: attn.enter_context(nc.sbuf_tensor(n, s, d))
        e.proj_w, e.proj_brep = ab("proj_w", [P, 4, C]), ab("proj_brep", [P, C])
        e.sel, e.tri, e.tri_bf = ab("sel", [P, P]), ab("tri", [P, P]), ab("tri_bf", [P, P], BF16)
        e.v_all = ab("v_all", [P, B, 4, TB, 64])
        qkv = attn.enter_context(ExitStack())
        qb = lambda n, s, d=F32: qkv.enter_context(nc.sbuf_tensor(n, s, d))
        e.hT = qb("hT", [P, KC, B * T])
        e.qkv_w, e.qkv_b, e.qkv_bs, e.v0_brep = (qb("qkv_w", [P, KC, 3 * C]), qb("qkv_b", [P, 4]),
                                                 qb("qkv_bs", [P, 4]), qb("v0_brep", [P, C]))
        e.mask_dram = nc.dram_tensor("mask_dram", [8, T], F32).ap()
        e.qk_dram = nc.dram_tensor("qk_dram", [2, 8, 2, 64, T], F32).ap()
        e.max_dram = nc.dram_tensor("max_dram", [2, 32, P], F32).ap()

        part_prologue(nc, e, A)
        part_qkv0(nc, e)
        qkv.close()
        e.aT0 = ab("aT0", [P, 8, T])
        part_attention0(nc, e)
        part_project0(nc, e)
        attn.close()
        turned = ctx.enter_context(ExitStack())
        e.hT = turned.enter_context(nc.sbuf_tensor("hT_2", [P, KC, B * T], F32))
        front = ctx.enter_context(ExitStack())
        fb = lambda n, s, d=F32: front.enter_context(nc.sbuf_tensor(n, s, d))
        e.m0, e.vw0 = fb("m0", [P, B, KC, 1024]), fb("vw0", [P, B, 8, C])
        e.biases0 = fb("biases0", [P, 4 * C + B * 1024])
        e.bias0 = e.biases0[:, 4 * C:].rearrange("p (b n) -> p b n", b=B)
        later = chain_loads0(nc, e, A, fb)
        part_context0(nc, e, A, later)
        part_chain0(nc, e)
        part_norm2(nc, e)
        front.close()
        back = ctx.enter_context(ExitStack())
        bb = lambda n, s, d=F32: back.enter_context(nc.sbuf_tensor(n, s, d))
        e.aT2, e.wo_w, e.wo_brep = bb("aT2", [P, 8, T]), bb("wo_w", [P, 8, C]), bb("wo_brep", [P, C])
        part_load(nc, [(e.wo_w[:], A["L2_xattn_sa_wo"].rearrange("(k p) c -> p k c", p=P)),
                       (e.wo_brep[:], A["L2_xattn_sa_bo"].partition_broadcast(P))])
        for b in range(B):
            part_attention2(nc, e, A, b)
            part_project2(nc, e, b)
        back.close()
        turned.close()
        bb = sb
        e.m2, e.vw2 = bb("m2", [P, B, KC, 1024]), bb("vw2", [P, B, 8, C])
        e.m3, e.vw3 = bb("m3", [P, B, KC, 512]), bb("vw3", [P, B, 4, C])
        e.biases2 = bb("biases2", [P, 2 * C + B * 512])
        e.bias3 = e.biases2[:, 2 * C:].rearrange("p (b h k) -> p b h k", b=B, k=S2)
        later = chain_loads2(nc, e, A, bb)
        part_context2(nc, e, A, later)
        part_chain2(nc, e, out)


def kernel(**inputs):
    import numpy as _np
    import concourse.bacc as _bacc
    from concourse import mybir as _mybir
    from concourse.bass_utils import run_bass_kernel_spmd as _run

    nc = _bacc.Bacc("TRN2", target_bir_lowering=False, num_devices=1)
    arrays, args = {}, {}
    for name in inputs:
        a = _np.ascontiguousarray(inputs[name])
        arrays[f"in_{name}"] = a
        args[name] = nc.dram_tensor(f"in_{name}", a.shape, _mybir.dt.from_np(a.dtype), kind="ExternalInput").ap()
    out = nc.dram_tensor("out", (B, T, C), F32, kind="ExternalOutput").ap()
    program(nc, args, out)
    r = _run(nc, [arrays], core_ids=[0])
    return r.results[0]["out"]
```
